# Optimizing a Trainium2 kernel written in Bass

```python
import numpy as np
import jax
import jax.numpy as jnp

def _softmax(x, axis=-1):
    return jax.nn.softmax(x, axis=axis)

def _gelu(x):
    return jax.nn.gelu(x, approximate=True)

def _silu(x):
    return jax.nn.silu(x)

def _sigmoid(x):
    return jax.nn.sigmoid(x)

def _layernorm(x, axis=-1, eps=1e-05):
    m = jnp.mean(x, axis=axis, keepdims=True)
    v = jnp.var(x, axis=axis, keepdims=True)
    return (x - m) / jnp.sqrt(v + eps)

def _scatter_add(tgt, idx, src, axis=0):
    return tgt.at[idx].add(src)

def _segment_sum(src, seg, n):
    return jax.ops.segment_sum(src, seg, n)
kernel_name = 'mk_decoder_postln_d1_seqx_r4_7d43ac'

def setup_inputs(seed: int=0):
    np.random.seed(seed)
    _w = jnp.asarray

    def _rec_inputs():
        import jax
        import jax.numpy as jnp
        _rk = jax.random.key(seed)
        x = -0.0002928 + 1 * jax.random.normal(jax.random.fold_in(_rk, 1), (32, 256, 256), jnp.float32)
        _lenS = 256 - jax.random.randint(jax.random.fold_in(_rk, 7), (32,), 0, max(1, 256 // 4) + 1, jnp.int32)
        _lenS2 = 256 - jax.random.randint(jax.random.fold_in(_rk, 8), (32,), 0, max(1, 256 // 4) + 1, jnp.int32)
        _ctx_1024P = jax.random.normal(jax.random.fold_in(_rk, 11), (32, 16, 256), jnp.float32)
        _ctx_1024c = jax.random.dirichlet(jax.random.fold_in(_rk, 511), 0.3 * jnp.ones((16,), jnp.float32), (32, 256))
        _ctx_1024t = jnp.einsum('bsk,bkd->bsd', _ctx_1024c, _ctx_1024P)
        _ctx_1024t = _ctx_1024t * jax.lax.rsqrt(jnp.mean(jnp.square(_ctx_1024t)) + 1e-12) * 0.953939
        ctx_1024 = -1.39393e-06 + 0.999914 * (_ctx_1024t + 0.3 * jax.random.normal(jax.random.fold_in(_rk, 611), (32, 256, 256), jnp.float32))
        _validS = jnp.arange(256)[None, :] < _lenS[:, None]
        _validS2 = jnp.arange(256)[None, :] < _lenS2[:, None]
        _causal = jnp.tril(jnp.ones((256, 256), dtype=bool))
        mask_BxSxS2_bf0 = jnp.logical_not(jnp.ones((32, 256, 256), dtype=bool))
        return (x, ctx_1024, mask_BxSxS2_bf0)
    x, ctx_1024, mask_BxSxS2_bf0 = _rec_inputs()

    def _L0_attn_setup():
        import jax, jax.numpy as jnp
        import numpy as np
        L, B, D = (1024, 4, 256)
        key = jax.random.key(seed)
        k1, k2, k3, k4 = jax.random.split(key, 4)
        return {'x': jax.random.normal(k1, (L, B, D), dtype=jnp.float32), 'lmlg': jax.random.normal(k2, (D,), dtype=jnp.float32), 'theta': jax.random.normal(k3, (D,), dtype=jnp.float32), 'last_conv_init': jax.random.normal(k4, (D,), dtype=jnp.float32)}
    _L0_attn_all = _L0_attn_setup()
    _L0_attn_in = {k: v for k, v in _L0_attn_all.items() if k in ('lmlg', 'theta', 'last_conv_init')}
    del _L0_attn_all

    def _L0_xattn_setup():
        import jax, jax.numpy as jnp
        import numpy as np
        H = 16
        C = 256
        EPS = 1e-05
        key = jax.random.key(seed)
        ks = jax.random.split(key, 10)
        B, T = (2, 512)
        s = 0.02
        return {'Q': jax.random.normal(ks[0], (B, T, C), jnp.float32), 'K': jax.random.normal(ks[1], (B, T, C), jnp.float32), 'V': jax.random.normal(ks[2], (B, T, C), jnp.float32), 'key_pad_masks': jnp.zeros((B, T, T), jnp.bool_), 'query_pad_masks': jnp.zeros((B, T, T), jnp.bool_), 'Wq': jax.random.normal(ks[3], (C, C), jnp.float32) * s, 'bq': jnp.zeros((C,), jnp.float32), 'Wk': jax.random.normal(ks[4], (C, C), jnp.float32) * s, 'bk': jnp.zeros((C,), jnp.float32), 'Wv': jax.random.normal(ks[5], (C, C), jnp.float32) * s, 'bv': jnp.zeros((C,), jnp.float32), 'ln_g': jnp.ones((C,), jnp.float32), 'ln_b': jnp.zeros((C,), jnp.float32)}
    _L0_xattn_all = _L0_xattn_setup()
    _L0_xattn_in = {k: v for k, v in _L0_xattn_all.items() if k in ('Wq', 'bq', 'Wk', 'bk', 'Wv', 'bv', 'ln_g', 'ln_b')}
    del _L0_xattn_all

    def _L0_ffn_setup():
        import jax, jax.numpy as jnp
        import numpy as np
        EPS = 1e-06
        N_EXPERTS = 8

        def _rms_norm(x, scale, eps=EPS):
            mean_sq = jnp.mean(x.astype(jnp.float32) ** 2, axis=-1, keepdims=True)
            s = scale.astype(jnp.float32) * jax.lax.rsqrt(mean_sq + eps)
            return x * s.astype(x.dtype)

        def _dist2(x, y):
            nx = jnp.sum(x ** 2, axis=-1)[..., :, None]
            ny = jnp.sum(y ** 2, axis=-1)[..., None, :]
            return nx + ny - 2.0 * (x @ y.T)
        key = jax.random.key(seed)
        ks = jax.random.split(key, 5)
        dim, hidden, E = (256, 512, N_EXPERTS)
        x = jax.random.normal(ks[0], (4, 512, dim), dtype=jnp.float32)
        scale = jnp.ones((dim,), dtype=jnp.float32)
        centroids = jax.random.normal(ks[1], (E, dim), dtype=jnp.float32)
        up_w = jax.random.normal(ks[2], (E, dim, hidden * 2), dtype=jnp.float32) * dim ** (-0.5)
        down_w = jax.random.normal(ks[3], (E, hidden, dim), dtype=jnp.float32) * hidden ** (-0.5)
        return {'x': x, 'scale': scale, 'centroids': centroids, 'up_w': up_w, 'down_w': down_w}
    _L0_ffn_all = _L0_ffn_setup()
    _L0_ffn_in = {k: v for k, v in _L0_ffn_all.items() if k in ('scale', 'centroids', 'up_w', 'down_w')}
    del _L0_ffn_all
    return {'x': x, 'ctx_1024': ctx_1024, 'mask_BxSxS2_bf0': mask_BxSxS2_bf0, 'L0_attn_lmlg': _L0_attn_in['lmlg'], 'L0_attn_theta': _L0_attn_in['theta'], 'L0_attn_last_conv_init': _L0_attn_in['last_conv_init'], 'L0_xattn_Wq': _L0_xattn_in['Wq'], 'L0_xattn_bq': _L0_xattn_in['bq'], 'L0_xattn_Wk': _L0_xattn_in['Wk'], 'L0_xattn_bk': _L0_xattn_in['bk'], 'L0_xattn_Wv': _L0_xattn_in['Wv'], 'L0_xattn_bv': _L0_xattn_in['bv'], 'L0_xattn_ln_g': _L0_xattn_in['ln_g'], 'L0_xattn_ln_b': _L0_xattn_in['ln_b'], 'L0_ffn_scale': _L0_ffn_in['scale'], 'L0_ffn_centroids': _L0_ffn_in['centroids'], 'L0_ffn_up_w': _L0_ffn_in['up_w'], 'L0_ffn_down_w': _L0_ffn_in['down_w']}

def reference(x, ctx_1024, mask_BxSxS2_bf0, L0_attn_lmlg, L0_attn_theta, L0_attn_last_conv_init, L0_xattn_Wq, L0_xattn_bq, L0_xattn_Wk, L0_xattn_bk, L0_xattn_Wv, L0_xattn_bv, L0_xattn_ln_g, L0_xattn_ln_b, L0_ffn_scale, L0_ffn_centroids, L0_ffn_up_w, L0_ffn_down_w):
    import jax
    import jax.numpy as jnp

    def _L0_attn_ref(x, lmlg, theta, last_conv_init):
        import jax, jax.numpy as jnp
        import numpy as np
        L, B, D = (1024, 4, 256)
        seq_len, batch, dim = x.shape
        gamma = jnp.exp(-jnp.exp(lmlg))
        c = gamma * jnp.exp(1j * theta)
        n = jnp.arange(seq_len)[:, None]
        filt = c[None, :] ** n
        filt_fft = jnp.fft.fft(filt, n=2 * seq_len, axis=0)
        x_fft = jnp.fft.fft(x, n=2 * seq_len, axis=0)
        conv_filter_x = jnp.fft.ifft(filt_fft[:, None, :] * x_fft, axis=0)[:seq_len]
        last_conv = jax.lax.stop_gradient(jnp.broadcast_to(last_conv_init.astype(conv_filter_x.dtype), (batch, dim)))
        conv_with_past = conv_filter_x + last_conv[None, :, :] * filt[:, None, :] * c[None, None, :]
        return conv_with_past.real * x

    def _L0_xattn_ref(Q, K, V, key_pad_masks, query_pad_masks, Wq, bq, Wk, bk, Wv, bv, ln_g, ln_b):
        import jax, jax.numpy as jnp
        import numpy as np
        H = 16
        C = 256
        EPS = 1e-05
        Qp = jax.nn.relu(Q @ Wq + bq)
        Kp = jax.nn.relu(K @ Wk + bk)
        Vp = jax.nn.relu(V @ Wv + bv)
        B, T, _ = Qp.shape
        dh = C // H
        q = Qp.reshape(B, T, H, dh)
        k = Kp.reshape(B, T, H, dh)
        v = Vp.reshape(B, T, H, dh)
        scores = jnp.einsum('bqhd,bkhd->bhqk', q, k) / dh ** 0.5
        probs = jax.nn.softmax(scores, axis=-1)
        out = jnp.einsum('bhqk,bkhd->bqhd', probs, v).reshape(B, T, C)
        out = out + Qp
        mean = jnp.mean(out, axis=-1, keepdims=True)
        var = jnp.var(out, axis=-1, keepdims=True)
        return ln_g * (out - mean) / jnp.sqrt(var + EPS) + ln_b

    def _L0_ffn_ref(x, scale, centroids, up_w, down_w):
        import jax, jax.numpy as jnp
        import numpy as np
        EPS = 1e-06
        N_EXPERTS = 8

        def _rms_norm(x, scale, eps=EPS):
            mean_sq = jnp.mean(x.astype(jnp.float32) ** 2, axis=-1, keepdims=True)
            s = scale.astype(jnp.float32) * jax.lax.rsqrt(mean_sq + eps)
            return x * s.astype(x.dtype)

        def _dist2(x, y):
            nx = jnp.sum(x ** 2, axis=-1)[..., :, None]
            ny = jnp.sum(y ** 2, axis=-1)[..., None, :]
            return nx + ny - 2.0 * (x @ y.T)
        skip = x
        xn = _rms_norm(x, scale)
        ids = jnp.argmin(_dist2(xn, centroids), axis=-1)
        out = jnp.zeros_like(x)
        for e in range(N_EXPERTS):
            h = jnp.einsum('bsd,dh->bsh', xn, up_w[e])
            a, g = jnp.split(h, 2, axis=-1)
            y = jnp.einsum('bsh,hd->bsd', a * jax.nn.silu(g), down_w[e])
            out = jnp.where((ids == e)[..., None], y, out)
        return out + skip
    x = _layernorm(x + _L0_attn_ref(x, L0_attn_lmlg, L0_attn_theta, L0_attn_last_conv_init), axis=-1)
    x = _layernorm(x + _L0_xattn_ref(x, ctx_1024, ctx_1024, mask_BxSxS2_bf0, mask_BxSxS2_bf0, L0_xattn_Wq, L0_xattn_bq, L0_xattn_Wk, L0_xattn_bk, L0_xattn_Wv, L0_xattn_bv, L0_xattn_ln_g, L0_xattn_ln_b), axis=-1)
    x = _layernorm(x + _L0_ffn_ref(x, L0_ffn_scale, L0_ffn_centroids, L0_ffn_up_w, L0_ffn_down_w), axis=-1)
    return x

_drawn_inputs = setup_inputs


def setup_inputs(seed=0):
    import zlib

    import numpy as np

    out = dict(_drawn_inputs(seed))
    spreads = {'L0_xattn_bq': (0.0, 0.1),
     'L0_xattn_bk': (0.0, 0.1),
     'L0_xattn_bv': (0.0, 0.1),
     'L0_xattn_ln_g': (1.0, 0.2),
     'L0_xattn_ln_b': (0.0, 0.1),
     'L0_ffn_scale': (1.0, 0.2)}
    factors = {}
    for name, (base, spread) in spreads.items():
        noise = np.random.default_rng([zlib.crc32(name.encode()), seed]).standard_normal(out[name].shape)
        drawn = base * np.exp(spread * noise) if base else spread * noise
        out[name] = jnp.asarray(drawn.astype(out[name].dtype))
    for name, factor in factors.items():
        out[name] = (out[name] * factor).astype(out[name].dtype)
    return out
```

```python
import numpy as np
import concourse.bass as bass
from concourse import mybir
from contextlib import ExitStack

F32 = mybir.dt.float32
F32R = mybir.dt.float32r
BF16 = mybir.dt.bfloat16
U32 = mybir.dt.uint32
I32 = mybir.dt.int32
ALU = mybir.AluOpType
ACT = mybir.ActivationFunctionType
AX = mybir.AxisListType

P = 128
SEQ, TOK, C = 32, 256, 256
NCH = C // P
NTC = TOK // P
H = 16
DH = C // H
HPC = H // NCH
E, HID = 8, 512
HCH = HID // P
LN_EPS, RMS_EPS = 1e-5, 1e-6
ROWW = C + 2
CAP = SEQ * TOK + P
PAD = E * CAP
NTILES = SEQ * TOK // P + E - 1
SETUP_DVE = 13
NOID = 1 << 20
STACK = 3 * DH
AUG = STACK + 2
TWO_PI_A = 6.28125
TWO_PI_B = float(np.float32(2 * np.pi - TWO_PI_A))
TWO_PI_C = float(np.float32(2 * np.pi - TWO_PI_A - TWO_PI_B))
ROUND = 1.5 * 2 ** 23


class Item:

    def __init__(self, i, k):
        self.i, self.k = i, k
        self.runtime = not isinstance(i, int)

    def __add__(self, d):
        return Item(self.i, self.k + d)

    def __sub__(self, d):
        return Item(self.i, self.k - d)

    def mod(self, m):
        return self.k % m

    def times(self, c, j=0):
        return self.i * (4 * c) + (self.k * c + j) if self.runtime else (4 * self.i + self.k) * c + j

    def uses(self, m):
        return self.i * (4 // m) + (self.k // m + 1) if self.runtime else (4 * self.i + self.k) // m + 1

    def within(self, lo, hi):
        return self.runtime or lo <= 4 * self.i + self.k < hi


def build(nc, x, ctx_in, lmlg, theta, last_conv, Wq, bq, Wk, bk, Wv, bv, ln_g, ln_b, ffn_scale, centroids, up_w, down_w, out):
    stack = ExitStack()
    with stack:
        def sb(name, shape, dt=F32):
            return stack.enter_context(nc.sbuf_tensor(name, shape, dt))

        def bank(name, scope=stack):
            return scope.enter_context(nc.psum_tensor(name, [P, 512], F32))

        def sem(name):
            return stack.enter_context(nc.semaphore(name))

        q_dram = nc.dram_tensor("q_pieces", (2, NCH, 2, P, TOK), F32)
        k_dram = nc.dram_tensor("k_pieces", (2, NCH, 2, P, TOK), F32)
        m_dram = nc.dram_tensor("neg_max", (2, 2, 2, HPC, TOK), F32)
        buckets = nc.dram_tensor("buckets", (PAD + P, ROWW), F32)

        up_sb = sb("up_sb", [P, E * NCH * 2 * HID])
        ident = sb("ident", [P, P])
        scale_bc = sb("scale_bc", [P, C])
        neg_half = sb("neg_half", [P, 1])
        filled = sb("filled", [P, E])
        pad_row = sb("pad_row", [P, ROWW])
        tile_row = sb("tile_row", [1, NTILES], I32)
        tile_up = sb("tile_up", [1, NTILES], I32)
        tile_dn = sb("tile_dn", [1, NTILES], I32)
        tail_row = sb("tail_row", [1, E], I32)

        phase1 = ExitStack()

        def sb1(name, shape, dt=F32):
            return phase1.enter_context(nc.sbuf_tensor(name, shape, dt))

        with phase1:
            wq_sb = sb1("wq_sb", [P, NCH, C])
            wk_sb = sb1("wk_sb", [P, NCH, C])
            wv_sb = sb1("wv_sb", [P, NCH, C])
            bq_sb = sb1("bq_sb", [P, NCH])
            bk_sb = sb1("bk_sb", [P, NCH])
            bv_bc = sb1("bv_bc", [P, C])
            g_bc = sb1("g_bc", [P, C])
            b_bc = sb1("b_bc", [P, C])
            decay_re = sb1("decay_re", [P, C])
            decay_im = sb1("decay_im", [P, C])
            cent = sb1("cent", [E, C])
            centT = sb1("centT", [P, NCH, E])
            cent_sq = sb1("cent_sq", [P, NCH, E])
            cent_norm = sb1("cent_norm", [P, E])
            ones_f = sb1("ones_f", [P, P])
            ones_bf = sb1("ones_bf", [P, P], BF16)
            before = sb1("before", [P, P], BF16)
            expert_no = sb1("expert_no", [P, NTC, E])
            state = sb1("state", [P, 2, NTC, C])
            by_im = sb1("by_im", [P, 2, NTC, C])
            xt = sb1("xt", [P, 2, NTC, C])
            ct = sb1("ct", [P, 2, NTC, C])
            u = sb1("u", [P, NTC, C])
            st1 = sb1("st1", [P, NTC, 6])
            mv1 = sb1("mv1", [P, NTC, 2])
            rs1 = sb1("rs1", [P, 2, NTC])
            x1 = sb1("x1", [P, 4, NTC, C])
            x1T = sb1("x1T", [P, NCH, TOK])
            ctT = sb1("ctT", [P, NCH, TOK])
            q32 = sb1("q32", [P, 4, NCH, TOK])
            k32 = sb1("k32", [P, NCH, TOK])
            q_hi = sb1("q_hi", [P, NCH, TOK], F32R)
            q_lo = sb1("q_lo", [P, NCH, TOK], F32R)
            k_hi = sb1("k_hi", [P, NCH, TOK], F32R)
            k_lo = sb1("k_lo", [P, NCH, TOK], F32R)
            v_sum = sb1("v_sum", [P, NTC, C])
            VW = DH + 1
            v_aug = sb1("v_aug", [P, 4, NTC, H * VW + 32 - VW])
            q_st = sb1("q_st", [P, H, TOK], F32R)
            k_st = sb1("k_st", [P, H, TOK], F32R)
            neg_max = sb1("neg_max_sb", [P, 2, NTC, H])
            nm_pieces = sb1("nm_pieces", [HPC, 2, TOK], F32R)
            probs = sb1("probs", [P, 8, NTC, TOK])
            lm_t, th_t, turns, angle, angle2 = (probs[:, k, 0, :] for k in range(5))
            trig = probs[:, 5]
            oT = sb1("oT", [P, H // 4, TOK])
            rden = sb1("rden", [P, NTC, H])
            o = sb1("o", [P, NTC, C])
            oq = sb1("oq", [P, NTC, C])
            stx = sb1("stx", [P, NTC, 6])
            mvx = sb1("mvx", [P, NTC, 2])
            rsx = sb1("rsx", [P, 2, NTC])
            y1, y2 = o, oq
            st2 = sb1("st2", [P, NTC, 6])
            mv2 = sb1("mv2", [P, NTC, 2])
            rs2 = sb1("rs2", [P, 2, NTC])
            row = sb1("row", [P, 2, NTC, ROWW])
            junk = sb1("junk", [P, C], BF16)
            ms = sb1("ms", [P, 2, NTC])
            xn = sb1("xn", [P, NTC, C])
            nx = sb1("nx", [P, NTC])
            xnT = x1T
            dist = sb1("dist", [P, 2, NTC, E])
            least = sb1("least", [P, NTC])
            cand = sb1("cand", [P, 2, NTC, E])
            choice = sb1("choice", [P, NTC])
            onehot = sb1("onehot", [P, NTC, E])
            onehot_bf = sb1("onehot_bf", [P, NTC, E], BF16)
            place = sb1("place", [P, 2, NTC, E])
            slot_f = sb1("slot_f", [P, NTC])
            slot = sb1("slot", [P, 2, NTC], U32)
            ids = sb1("ids", [P, NTC], I32)

            S_ps = [bank("S0", phase1), bank("S1", phase1)]
            T_ps = [bank("T0", phase1), bank("T1", phase1)]
            O_ps = bank("O", phase1)
            M_ps = [bank(n, phase1) for n in ("M0", "M1", "M2")]
            names = """params setup_pool setup_dve setup_act setup_pe pads ups ident_ok
                x_in0 x_in1 ctx_in0 ctx_in1 conv u_ok ln1 rstd1 x1_ok x1T_pe x1T_ok ctT_pe ctT_ok
                q_pe q_ok k_pe k_ok q_cut k_cut v_pe v_added v_ok q_out0 q_out1 stack0 stack1 s_pe max_ok
                negT neg_ok neg_out neg_in0 neg_in1 t_pe exp_ok pv o_ev x_pe o_ok qn_pe oq_ok lnx rstdx
                x1b_ok y_ok ln2 rstd2 x2_ok ms_ok rms xn_ok nx_ok xnT_pe xnT_ok dist_pe pick rank_pe slot_ok
                id_ok scat0 scat1 pool_waits sp_waits dve_waits"""
            s = {n: sem(n) for n in names.split()}
            x_in, ctx_in_s, q_out, stack_in = ([s[a + "0"], s[a + "1"]] for a in ("x_in", "ctx_in", "q_out", "stack"))
            neg_in, scat = [s["neg_in0"], s["neg_in1"]], [s["scat0"], s["scat1"]]

            def wait(eng, name, item, per=1, j=None):
                if not item.runtime and item.k >= SEQ:
                    item, j = Item(0, SEQ - 1), per
                wait_value(eng, name, item.times(per, per if j is None else j))

            def wait_value(eng, name, v):
                sm = s[name] if isinstance(name, str) else name
                if isinstance(v, int):
                    if v > 0:
                        eng.wait_ge(sm, v)
                else:
                    eng.wait_ge(sm, v)
                    after_register_wait(eng)

            def wait_ring(eng, sm, item, ring, per):
                if not item.runtime:
                    while item.k >= SEQ:
                        item = item - ring
                wait_value(eng, sm, item.uses(ring) * per)

            def after_register_wait(eng):
                if eng.engine in (mybir.EngineType.Pool, mybir.EngineType.SP):
                    eng.sem_inc(s["pool_waits" if eng.engine == mybir.EngineType.Pool else "sp_waits"], 1)

            def steps(eng, body):
                lead = 5
                for n in range(-1, lead):
                    body(Item(0, n))
                loops = (SEQ - 3 - lead) // 4
                with eng.Fori(0, loops) as i:
                    for k in range(4):
                        body(Item(i, lead + k))
                for n in range(lead + 4 * loops, SEQ + 3):
                    body(Item(0, n))

            def active(item):
                return item.within(0, SEQ)

            block = phase1.enter_context(nc.Block())

            x_v = x.rearrange("n (c p) d -> p (n c) d", p=P)
            c_v = ctx_in.rearrange("n (c p) d -> p (n c) d", p=P)

            def bcast(v):
                return v.rearrange("(a n) -> a n", a=1).to_broadcast([P, C])

            @block.sync
            def _(sp):
                def load(item):
                    if not active(item):
                        return
                    p = item.mod(2)
                    wait(sp, "u_ok", item - 2)
                    sp.dma_start(xt[:, p], x_v[:, bass.ds(item.times(NTC), NTC), :]).then_inc(x_in[p], 16)
                    wait(sp, "ctT_pe", item - 2)
                    sp.dma_start(ct[:, p], c_v[:, bass.ds(item.times(NTC), NTC), :]).then_inc(ctx_in_s[p], 16)

                def neg_round_trip(item, half):
                    if not active(item):
                        return
                    p = item.mod(2)
                    wait(sp, "neg_ok", item, 4, 2 * half + 2)
                    wait(sp, neg_in[half], item - 2, 16)
                    sp.dma_start(m_dram[p, half].rearrange("w h t -> h w t"), nm_pieces[:, :, :].bitcast(F32)).then_inc(s["neg_out"], 16)
                    wait(sp, "neg_out", item, 32, 16 * half + 16)
                    sp.dma_start(q_st[64 * p + STACK:64 * p + AUG, half * HPC:(half + 1) * HPC, :].bitcast(F32),
                                 m_dram[p, half]).then_inc(neg_in[half], 16)

                def write_pieces(item, dram, hi, lo, name):
                    p = item.mod(2)
                    wait(sp, name, item, 2)
                    for half in range(2):
                        wait(sp, stack_in[half], item - 2, 64)
                    for w, piece in enumerate((hi, lo)):
                        sp.dma_start(dram[p, :, w].rearrange("o p t -> p o t"), piece[:, :, :].bitcast(F32)).then_inc(q_out[p], 16)

                def read_stacks(item, half):
                    if not active(item):
                        return
                    p = item.mod(2)
                    b = 64 * p
                    wait(sp, "t_pe", item - 2, H, HPC * (half + 1))
                    hs = slice(half * HPC, (half + 1) * HPC)
                    view = "w (c h) t -> (w c) h t"
                    qd = q_dram[p, half].rearrange(view, h=HPC)
                    kd = k_dram[p, half].rearrange(view, h=HPC)
                    sp.dma_start(q_st[b:b + DH, hs, :].bitcast(F32), qd[0:DH]).then_inc(stack_in[half], 16)
                    sp.dma_start(q_st[b + DH:b + 3 * DH, hs, :].bitcast(F32), qd).then_inc(stack_in[half], 16)
                    sp.dma_start(k_st[b:b + 2 * DH, hs, :].bitcast(F32), kd).then_inc(stack_in[half], 16)
                    sp.dma_start(k_st[b + 2 * DH:b + 3 * DH, hs, :].bitcast(F32), kd[0:DH]).then_inc(stack_in[half], 16)

                for dst, src in ((wq_sb, Wq), (wk_sb, Wk), (wv_sb, Wv)):
                    sp.dma_start(dst[:, :, :], src.rearrange("(o p) c -> p o c", p=P)).then_inc(s["params"], 16)
                for dst, src in ((bq_sb, bq), (bk_sb, bk)):
                    sp.dma_start(dst[:, :], src.rearrange("(o p) -> p o", p=P), allow_slow_non_contiguous=True).then_inc(s["params"], 16)
                for dst, src in ((bv_bc[:, :], bv), (g_bc[:, :], ln_g), (b_bc[:, :], ln_b), (lm_t, lmlg), (th_t, theta), (scale_bc[:, :], ffn_scale)):
                    sp.dma_start(dst, bcast(src)).then_inc(s["params"], 16)
                for c in range(NTC):
                    sp.dma_start(state[:, 0, c, :], bcast(last_conv)).then_inc(s["params"], 16)
                sp.dma_start(cent[:, :], centroids).then_inc(s["params"], 16)
                sp.wait_ge(s["ident_ok"], 2)
                sp.wait_ge(s["setup_pool"], 13)
                load(Item(0, 0))
                load(Item(0, 1))

                def ups(n):
                    for e in range(2 * n, 2 * n + 2):
                        dst = up_sb[:, e * NCH * 2 * HID:(e + 1) * NCH * 2 * HID].rearrange("p (o n) -> p o n", o=NCH)
                        sp.dma_start(dst, up_w[e].rearrange("(o p) n -> p o n", p=P)).then_inc(s["ups"], 16)

                def step(t):
                    neg_round_trip(t - 1, 1)
                    load(t + 3)
                    nxt = t + 1
                    if active(nxt):
                        write_pieces(nxt, q_dram, q_hi, q_lo, "q_cut")
                        write_pieces(nxt, k_dram, k_hi, k_lo, "k_cut")
                        wait_ring(sp, q_out[nxt.mod(2)], nxt, 2, 64)
                    read_stacks(nxt, 0)
                    neg_round_trip(t, 0)
                    read_stacks(nxt, 1)
                    if not t.runtime and t.k < 3:
                        ups(t.k + 1)

                steps(sp, step)
                sp.wait_ge(s["pads"], 16)
                sp.wait_ge(s["ups"], 16 * E)
                for p in range(2):
                    sp.wait_ge(scat[p], 16 * NTC * SEQ // 2)

            @block.gpsimd
            def _(pool):
                g = nc.gpsimd
                g.memset(ident[:, :], 0.0).then_inc(s["ident_ok"], 1)
                pool.wait_ge(s["ident_ok"], 1)
                g.affine_select(out=ident[:, :], in_=ident[:, :], compare_op=ALU.not_equal, fill=1.0, base=0,
                                pattern=[[-1, P]], channel_multiplier=1).then_inc(s["ident_ok"], 1)
                g.memset(neg_half[:, :], -0.5).then_inc(s["setup_pool"], 1)
                g.memset(ones_f[:, :], 1.0).then_inc(s["setup_pool"], 1)
                g.memset(ones_bf[:, :], 1.0).then_inc(s["setup_pool"], 1)
                g.memset(before[:, :], 1.0).then_inc(s["setup_pool"], 1)
                g.memset(k_st[:, :, :].bitcast(F32), 1.0).then_inc(s["setup_pool"], 1)
                g.memset(v_aug[:, :, :, :], 1.0).then_inc(s["setup_pool"], 1)
                g.memset(state[:, 1], 0.0).then_inc(s["setup_pool"], 1)
                g.memset(pad_row[:, :], 0.0).then_inc(s["setup_pool"], 1)
                g.iota(ids[:, :], pattern=[[P, NTC]], base=0, channel_multiplier=1).then_inc(s["setup_pool"], 1)
                g.iota(expert_no[:, :, :], pattern=[[0, NTC], [1, E]], base=0, channel_multiplier=0,
                       allow_small_or_imprecise_dtypes=True).then_inc(s["setup_pool"], 1)
                g.iota(filled[:, :], pattern=[[CAP, E]], base=0, channel_multiplier=0,
                       allow_small_or_imprecise_dtypes=True).then_inc(s["setup_pool"], 1)
                pool.wait_ge(s["setup_pool"], 11)
                g.affine_select(out=before[:, :], in_=before[:, :], compare_op=ALU.is_gt, fill=0.0, base=0,
                                pattern=[[1, P]], channel_multiplier=-1).then_inc(s["setup_pool"], 1)
                g.memset(pad_row[:, C + 1:C + 2].bitcast(U32), NOID).then_inc(s["setup_pool"], 1)
                pool.wait_ge(s["setup_pool"], 13)
                g.dma_start(buckets[PAD:PAD + P, :], pad_row[:, :]).then_inc(s["pads"], 16)
                pool.wait_ge(s["params"], 14 * 16)
                pool.wait_ge(s["setup_dve"], SETUP_DVE)

                re_b = decay_re[:, :].unsqueeze(1).to_broadcast([P, 2 * NTC, C])
                im_b = decay_im[:, :].unsqueeze(1).to_broadcast([P, 2 * NTC, C])
                z_all = state[:, :, :, :].rearrange("p r c d -> p (r c) d")

                def conv_products(item, j):
                    if not active(item):
                        return
                    if j == 0:
                        wait(pool, "conv", item - 1, 5)
                        g.tensor_tensor(by_im[:, :, :, :].rearrange("p r c d -> p (r c) d"), z_all, im_b, ALU.mult).then_inc(s["conv"], 1)
                    else:
                        wait(pool, "u_ok", item - 1)
                        g.tensor_tensor(z_all, z_all, re_b, ALU.mult).then_inc(s["conv"], 1)

                def conv_sums(item):
                    if not active(item):
                        return
                    wait(pool, "conv", item, 5, 2)
                    g.tensor_tensor(state[:, 1], state[:, 1], by_im[:, 0], ALU.add).then_inc(s["conv"], 1)
                    g.tensor_tensor(state[:, 0], state[:, 0], by_im[:, 1], ALU.subtract).then_inc(s["conv"], 1)
                    wait_ring(pool, x_in[item.mod(2)], item, 2, 16)
                    wait(pool, "conv", item, 5, 4)
                    g.tensor_tensor(state[:, 0], state[:, 0], xt[:, item.mod(2)], ALU.add).then_inc(s["conv"], 1)

                def rstd(item, ready, per, mv, rs, done):
                    if not active(item):
                        return
                    wait(pool, ready, item, per)
                    g.tensor_scalar(rs[:, 0], mv[:, :, 1], LN_EPS, None, ALU.add).then_inc(s[done], 1)
                    wait(pool, done, item, 2, 1)
                    g.tensor_tensor(rs[:, 1], rs[:, 0], neg_half[:, :].to_broadcast([P, NTC]), ALU.pow).then_inc(s[done], 1)

                def rms(item):
                    if not active(item):
                        return
                    p = item.mod(2)
                    wait(pool, "ms_ok", item, 2)
                    g.tensor_scalar(ms[:, 1], ms[:, 0], 1.0 / C, RMS_EPS, ALU.mult, ALU.add).then_inc(s["rms"], 1)
                    wait(pool, "rms", item, 2, 1)
                    g.tensor_tensor(row[:, p, :, C], ms[:, 1], neg_half[:, :].to_broadcast([P, NTC]), ALU.pow).then_inc(s["rms"], 1)

                def cut(item, src, hi, lo, ready, done):
                    if not active(item):
                        return
                    wait(pool, ready, item, 2)
                    wait_ring(pool, q_out[(item - 1).mod(2)], item - 1, 2, 64)
                    g.tensor_copy(hi[:, :, :], src).then_inc(s[done], 1)
                    wait(pool, done, item, 2, 1)
                    g.tensor_tensor(lo[:, :, :], src, hi[:, :, :].bitcast(F32), ALU.subtract).then_inc(s[done], 1)

                def step(t):
                    rms(t - 3)
                    rstd(t + 1, "ln1", 4, mv1, rs1, "rstd1")
                    conv_products(t + 2, 0)
                    a = t - 2
                    if active(a):
                        wait(pool, "x1_ok", a, 2)
                        wait(pool, "x1T_pe", a)
                        g.tensor_tensor(x1[:, a.mod(4)], x1[:, a.mod(4)], b_bc[:, :].unsqueeze(1).to_broadcast([P, NTC, C]),
                                        ALU.add).then_inc(s["x1b_ok"], 1)
                    conv_products(t + 2, 1)
                    b = t - 3
                    if active(b):
                        p = b.mod(2)
                        wait(pool, "slot_ok", b, 7)
                        wait(pool, "id_ok", b, 2)
                        for c in range(NTC):
                            g.indirect_dma_start(out=buckets[:, :], out_offset=bass.IndirectOffsetOnAxis(ap=slot[:, p, c:c + 1], axis=0),
                                                 in_=row[:, p, c, :], in_offset=None, bounds_check=PAD - 1,
                                                 oob_is_err=False).then_inc(scat[p], 16)
                    n = t + 1
                    cut(n, q32[:, n.mod(4)], q_hi, q_lo, "q_ok", "q_cut")
                    cut(n, k32[:, :, :], k_hi, k_lo, "k_ok", "k_cut")
                    rstd(t - 2, "lnx", 4, mvx, rsx, "rstdx")
                    conv_sums(t + 2)
                    if active(n):
                        wait(pool, "v_added", n)
                        wait(pool, "pv", n - 4, 4)
                        dst = v_aug[:, n.mod(4), :, 0:H * VW].rearrange("p k (h w) -> p k h w", w=VW)[:, :, :, 0:DH]
                        for kc in range(NTC):
                            g.tensor_scalar(dst[:, kc], v_sum[:, kc].rearrange("p (h w) -> p h w", w=DH), 0.0, None,
                                            ALU.max).then_inc(s["v_ok"], 1)
                    rstd(t - 2, "ln2", 4, mv2, rs2, "rstd2")

                conv_products(Item(0, 0), 0)
                conv_products(Item(0, 0), 1)
                conv_sums(Item(0, 0))
                steps(pool, step)

            @block.scalar
            def _(act):
                a_ = nc.scalar
                act.wait_ge(s["params"], 14 * 16)
                a_.activation(lm_t, lm_t, ACT.Exp).then_inc(s["setup_act"], 1)
                act.wait_ge(s["setup_act"], 1)
                a_.activation(decay_re[:, :], lm_t, ACT.Exp, scale=-1.0).then_inc(s["setup_act"], 1)
                act.wait_ge(s["setup_dve"], 8)
                a_.activation(trig[:, 0], angle, ACT.Sin).then_inc(s["setup_act"], 1)
                a_.activation(trig[:, 1], angle2, ACT.Sin).then_inc(s["setup_act"], 1)

                def step(t):
                    e_item = t - 1
                    for h in range(H):
                        if active(e_item):
                            wait(act, "t_pe", e_item, H, h + 1)
                            if h % 4 == 0:
                                prev = e_item.times(4, h // 4 - 1) if h >= 8 else (e_item - 1).times(4, h // 4 + 3)
                                wait_value(act, "pv", prev)
                            a_.activation(probs[:, h % 8].rearrange("p k t -> p (k t)"), T_ps[h % 2][:, :], ACT.Exp,
                                          scale=DH ** -0.5).then_inc(s["exp_ok"], 1)
                        b = t - 3
                        if h == 1 and active(b):
                            wait(act, "xn_ok", b, 2)
                            wait(act, "pick", b - 1, 7, 2)
                            for c in range(NTC):
                                if c:
                                    wait(act, "nx_ok", b, 2, 1)
                                a_.activation(junk[:, :], xn[:, c], ACT.Square, accum_out=nx[:, c:c + 1]).then_inc(s["nx_ok"], 1)
                        if h == 2 and active(b):
                            wait(act, "xnT_pe", b)
                            wait(act, "q_pe", t)
                            a_.activation(xnT[:, :, :].rearrange("p o t -> p (o t)"), M_ps[0][:, :], ACT.Copy).then_inc(s["xnT_ok"], 1)
                        n = t + 1
                        if h == 5 and active(n):
                            wait(act, "x1T_pe", n)
                            wait(act, "dist_pe", b)
                            a_.activation(x1T[:, :, :].rearrange("p o t -> p (o t)"), M_ps[0][:, :], ACT.Copy).then_inc(s["x1T_ok"], 1)
                        if h == 6 and active(n):
                            wait(act, "ctT_pe", n)
                            wait(act, "v_pe", n - 1)
                            a_.activation(ctT[:, :, :].rearrange("p o t -> p (o t)"), M_ps[1][:, :], ACT.Copy).then_inc(s["ctT_ok"], 1)
                        if h == 7 and active(n):
                            wait(act, "q_pe", n)
                            wait(act, "qn_pe", n - 4)
                            for c in range(NCH):
                                a_.activation(q32[:, n.mod(4), c], M_ps[0][:, c * TOK:(c + 1) * TOK], ACT.Relu,
                                              bias=bq_sb[:, c:c + 1]).then_inc(s["q_ok"], 1)
                        if h == 8 and active(n):
                            wait(act, "k_pe", n)
                            wait(act, "k_cut", n - 1, 2)
                            for c in range(NCH):
                                a_.activation(k32[:, c], M_ps[1][:, c * TOK:(c + 1) * TOK], ACT.Relu,
                                              bias=bk_sb[:, c:c + 1]).then_inc(s["k_ok"], 1)
                        m = t - 2
                        if h == 15 and active(m):
                            wait(act, "x2_ok", m, 2)
                            wait(act, "rms", m - 1, 2, 1)
                            wait(act, "nx_ok", m - 1, 2)
                            for c in range(NTC):
                                if c:
                                    wait(act, "ms_ok", m, 2, 1)
                                a_.activation(junk[:, :], row[:, m.mod(2), c, 0:C], ACT.Square,
                                              accum_out=ms[:, 0, c:c + 1]).then_inc(s["ms_ok"], 1)

                steps(act, step)

            @block.tensor
            def _(pe):
                t_ = nc.tensor
                pe.wait_ge(s["ident_ok"], 2)
                pe.wait_ge(s["params"], 14 * 16)
                pe.wait_ge(s["setup_pool"], 13)
                for c in range(NCH):
                    last = t_.transpose(M_ps[0][:, c * E:(c + 1) * E], cent[:, c * P:(c + 1) * P], ident[0:E, 0:E])
                last.then_inc(s["setup_pe"], 1)
                pe.wait_ge(s["setup_dve"], SETUP_DVE - 1)
                for c in range(NCH):
                    last = t_.matmul(M_ps[1][:, 0:E], ones_f[:, :], cent_sq[:, c, :], start=(c == 0), stop=(c == NCH - 1))
                last.then_inc(s["setup_pe"], 1)
                pe.wait_ge(s["setup_dve"], SETUP_DVE)

                def flip(dst, src):
                    for oc in range(NCH):
                        for tc in range(NTC):
                            last = t_.transpose(dst[:, oc * TOK + tc * P:oc * TOK + (tc + 1) * P], src[:, tc, oc * P:(oc + 1) * P], ident[:, :])
                    return last

                def neg_flip(item, half, b):
                    wait(pe, "max_ok", item, H, HPC * (half + 1))
                    for c in range(NTC):
                        last = t_.transpose(M_ps[b][0:HPC, c * P:(c + 1) * P], neg_max[:, item.mod(2), c, half * HPC:(half + 1) * HPC], ident[:, :])
                    last.then_inc(s["negT"], 1)

                def weighted_sum(item, grp):
                    wait(pe, "exp_ok", item, H, 4 * grp + 4)
                    if grp == 0:
                        wait(pe, "v_ok", item, 2)
                    prev = item.times(2, grp // 2)
                    wait_value(pe, "o_ev", prev)
                    for kc in range(NTC):
                        for j in range(4):
                            h = 4 * grp + j
                            last = t_.matmul(O_ps[32 * j:32 * j + 32, (grp % 2) * TOK:(grp % 2 + 1) * TOK],
                                             v_aug[:, item.mod(4), kc, h * VW:h * VW + 32], probs[:, h % 8, kc, :],
                                             start=(kc == 0), stop=(kc == NTC - 1))
                    last.then_inc(s["pv"], 1)

                def project(dst, w, xT):
                    for oc in range(NCH):
                        for ic in range(NCH):
                            last = t_.matmul(dst[:, oc * TOK:(oc + 1) * TOK], w[:, ic, oc * P:(oc + 1) * P], xT[:, ic, :],
                                             start=(ic == 0), stop=(ic == NCH - 1))
                    return last

                def step(t):
                    cur, prv, n, a, b = t, t - 1, t + 1, t - 2, t - 3
                    for h in range(H):
                        if active(cur):
                            if h % HPC == 0:
                                wait(pe, stack_in[h // HPC], cur, 64)
                            prev = cur.times(H, h - 1)
                            wait_value(pe, "max_ok", prev)
                            base = 64 * cur.mod(2)
                            for c in range(NTC):
                                last = t_.matmul(S_ps[h % 2][:, c * TOK:(c + 1) * TOK], q_st[base:base + STACK, h, c * P:(c + 1) * P],
                                                 k_st[base:base + STACK, h, :], start=True, stop=True)
                            last.then_inc(s["s_pe"], 1)
                        if active(prv):
                            if h % HPC == 0:
                                wait(pe, neg_in[h // HPC], prv, 16)
                            prev = prv.times(H, h - 1)
                            wait_value(pe, "exp_ok", prev)
                            base = 64 * prv.mod(2)
                            for c in range(NTC):
                                last = t_.matmul(T_ps[h % 2][:, c * TOK:(c + 1) * TOK], k_st[base:base + AUG, h, c * P:(c + 1) * P],
                                                 q_st[base:base + AUG, h, :], start=True, stop=True)
                            last.then_inc(s["t_pe"], 1)
                        if h == 1:
                            wait(pe, "k_ok", t, 2)
                            if not active(t):
                                wait(pe, "o_ok", b, 4)
                            if active(prv):
                                neg_flip(prv, 1, 1)
                            if active(a):
                                weighted_sum(a, 3)
                        if h == 2:
                            wait(pe, "v_added", t)
                            if not active(t):
                                wait(pe, "neg_ok", prv, 4, 2)
                                wait(pe, "o_ok", b, 4, 2)
                        if h == 2 and active(b):
                            wait(pe, "xn_ok", b, 2)
                            flip(M_ps[0], xn).then_inc(s["xnT_pe"], 1)
                        if h == 3 and active(a):
                            wait(pe, "o_ev", a, 2)
                            wait(pe, "xnT_ok", b)
                            for g4 in range(H // 4):
                                last = t_.transpose(M_ps[0][:, g4 * P:(g4 + 1) * P], oT[:, g4, 0:P], ident[:, :])
                            last.then_inc(s["x_pe"], 1)
                        if h == 4:
                            if active(a):
                                wait(pe, "neg_ok", prv, 4)
                                for g4 in range(H // 4):
                                    last = t_.transpose(M_ps[1][:, g4 * P:(g4 + 1) * P], oT[:, g4, P:2 * P], ident[:, :])
                                last.then_inc(s["x_pe"], 1)
                            if active(b):
                                wait(pe, "xnT_ok", b)
                                wait(pe, "oq_ok", b, 2)
                                for c in range(NTC):
                                    for oc in range(NCH):
                                        last = t_.matmul(M_ps[2][:, c * E:(c + 1) * E], xnT[:, oc, c * P:(c + 1) * P], centT[:, oc, :],
                                                         start=(oc == 0), stop=(oc == NCH - 1))
                                last.then_inc(s["dist_pe"], 1)
                        if h == 5:
                            if active(n):
                                wait(pe, "x1_ok", n, 2)
                                wait(pe, "o_ok", a, 4, 2)
                                flip(M_ps[0], x1[:, n.mod(4)]).then_inc(s["x1T_pe"], 1)
                            if active(prv):
                                weighted_sum(prv, 0)
                        if h == 6:
                            if active(n):
                                wait_ring(pe, ctx_in_s[n.mod(2)], n, 2, 16)
                                wait(pe, "o_ok", a, 4)
                                wait(pe, "neg_ok", prv, 4)
                                flip(M_ps[1], ct[:, n.mod(2)]).then_inc(s["ctT_pe"], 1)
                            if active(b):
                                wait(pe, "pick", b, 7)
                                r0, r1, tot = 64, 64 + E, 64 + 2 * E
                                t_.matmul(M_ps[2][:, r0:r0 + E], before[:, :], onehot_bf[:, 0, :], start=True, stop=True)
                                t_.matmul(M_ps[2][:, r1:r1 + E], before[:, :], onehot_bf[:, 1, :], start=True, stop=False)
                                t_.matmul(M_ps[2][:, r1:r1 + E], ones_bf[:, :], onehot_bf[:, 0, :], start=False, stop=True)
                                t_.matmul(M_ps[2][:, tot:tot + E], ones_bf[:, :], onehot_bf[:, 0, :], start=True, stop=False)
                                t_.matmul(M_ps[2][:, tot:tot + E], ones_bf[:, :], onehot_bf[:, 1, :], start=False, stop=True)\
                                    .then_inc(s["rank_pe"], 1)
                        if h == 7 and active(n):
                            wait(pe, "x1T_ok", n)
                            project(M_ps[0], wq_sb, x1T).then_inc(s["q_pe"], 1)
                        if h == 8:
                            if active(n):
                                wait(pe, "ctT_ok", n)
                                project(M_ps[1], wk_sb, ctT).then_inc(s["k_pe"], 1)
                            if active(a):
                                wait(pe, "slot_ok", b, 7)
                                for c in range(NTC):
                                    for oc in range(NCH):
                                        last = t_.transpose(M_ps[2][:, c * C + oc * P:c * C + (oc + 1) * P],
                                                            q32[:, a.mod(4), oc, c * P:(c + 1) * P], ident[:, :])
                                last.then_inc(s["qn_pe"], 1)
                        if h == 9:
                            if active(cur):
                                wait(pe, "q_ok", n, 2)
                                wait(pe, "o_ok", a, 4, 2)
                                neg_flip(cur, 0, 0)
                            if active(prv):
                                weighted_sum(prv, 1)
                        if h == 11 and active(n):
                            wait(pe, "neg_ok", cur, 4, 2)
                            wait(pe, "q_ok", n, 2)
                            for c in range(NTC):
                                for ic in range(NCH):
                                    last = t_.matmul(M_ps[0][:, c * C:(c + 1) * C], ctT[:, ic, c * P:(c + 1) * P], wv_sb[:, ic, :],
                                                     start=(ic == 0), stop=(ic == NCH - 1))
                            last.then_inc(s["v_pe"], 1)
                        if h == 13 and active(prv):
                            weighted_sum(prv, 2)

                steps(pe, step)

            @block.vector
            def _(dve):
                v = nc.vector
                done = [0]

                def setup(ins):
                    done[0] += 1
                    ins.then_inc(s["setup_dve"], 1)
                    dve.wait_ge(s["setup_dve"], done[0])

                dve.wait_ge(s["params"], 14 * 16)
                dve.wait_ge(s["setup_pool"], 13)
                setup(v.tensor_scalar(turns, th_t, 1 / (2 * np.pi), None, ALU.mult))
                setup(v.tensor_scalar(turns, turns, ROUND, -ROUND, ALU.add, ALU.add))
                setup(v.scalar_tensor_tensor(angle, turns, -TWO_PI_A, th_t, ALU.mult, ALU.add))
                setup(v.scalar_tensor_tensor(angle, turns, -TWO_PI_B, angle, ALU.mult, ALU.add))
                setup(v.scalar_tensor_tensor(angle, turns, -TWO_PI_C, angle, ALU.mult, ALU.add))
                setup(v.tensor_scalar(angle, angle, 3.1415925, -3.1415925, ALU.min, ALU.max))
                setup(v.scalar_tensor_tensor(angle2, angle, -1.0, angle, ALU.mult, ALU.max))
                setup(v.tensor_scalar(angle2, angle2, -1.0, np.pi / 2, ALU.mult, ALU.add))
                dve.wait_ge(s["setup_act"], 4)
                setup(v.tensor_tensor(decay_im[:, :], decay_re[:, :], trig[:, 0], ALU.mult))
                setup(v.tensor_tensor(decay_re[:, :], decay_re[:, :], trig[:, 1], ALU.mult))
                dve.wait_ge(s["setup_pe"], 1)
                ctv = centT[:, :, :].rearrange("p o e -> p (o e)")
                setup(v.tensor_scalar(ctv, M_ps[0][:, 0:NCH * E], -2.0, None, ALU.mult))
                setup(v.scalar_tensor_tensor(cent_sq[:, :, :].rearrange("p o e -> p (o e)"), ctv, 0.25, ctv, ALU.mult, ALU.mult))
                dve.wait_ge(s["setup_pe"], 2)
                setup(v.tensor_copy(cent_norm[:, :], M_ps[1][:, 0:E]))
                assert done[0] == SETUP_DVE

                def stats(item, src, st, mv, name):
                    for c in range(NTC):
                        v.bn_stats(st[:, c], src[:, c]).then_inc(s[name], 1)
                    wait(dve, name, item, 4, 2)
                    dve.sem_inc(s["dve_waits"], 1)
                    for c in range(NTC):
                        v.bn_aggr(mv[:, c], st[:, c]).then_inc(s[name], 1)

                def step(t):
                    cur, prv, n, a, b = t, t - 1, t + 1, t - 2, t - 3
                    for h in range(H):
                        if active(cur):
                            wait(dve, "s_pe", cur, H, h + 1)
                            if h == 0:
                                wait(dve, "negT", cur - 2, 2)
                            v.tensor_reduce(neg_max[:, cur.mod(2), :, h], S_ps[h % 2][:, :].rearrange("p (c t) -> p c t", c=NTC),
                                            AX.X, ALU.max, negate=True).then_inc(s["max_ok"], 1)
                        if h == 0 and active(n):
                            wait(dve, "conv", n, 5)
                            wait_ring(dve, x_in[n.mod(2)], n, 2, 16)
                            v.scalar_tensor_tensor(u[:, :, :], state[:, 0], 1.0, xt[:, n.mod(2)], ALU.add, ALU.mult).then_inc(s["u_ok"], 1)
                        if h == 1:
                            if active(n):
                                wait(dve, "u_ok", n)
                                wait(dve, "rstd1", n - 1, 2)
                                stats(n, u, st1, mv1, "ln1")
                            if active(b):
                                wait(dve, "rms", b, 2)
                                wait(dve, "nx_ok", b - 1, 2)
                                wait(dve, "xnT_pe", b - 1)
                                for c in range(NTC):
                                    v.scalar_tensor_tensor(xn[:, c], row[:, b.mod(2), c, 0:C], row[:, b.mod(2), c, C:C + 1], scale_bc[:, :],
                                                           ALU.mult, ALU.mult).then_inc(s["xn_ok"], 1)
                        if h == 2:
                            if active(prv):
                                neg_cut(prv, 1, 1)
                            if active(a):
                                copy_sums(a, 1)
                        if h == 3 and active(n):
                            wait(dve, "rstd1", n, 2)
                            wait(dve, "y_ok", n - 4, 4)
                            for c in range(NTC):
                                v.tensor_scalar(x1[:, n.mod(4), c], u[:, c], mv1[:, c, 0:1], rs1[:, 1, c:c + 1],
                                                ALU.subtract, ALU.mult).then_inc(s["x1_ok"], 1)
                        if h in (4, 5) and active(a):
                            c = h - 4
                            src = M_ps[c][:, :].rearrange("p (h w) -> p h w", w=32)
                            wait(dve, "x_pe", a, 2, c + 1)
                            v.reciprocal(rden[:, c], src[:, :, DH]).then_inc(s["o_ok"], 1)
                            wait(dve, "o_ok", a, 4, 2 * c + 1)
                            v.tensor_tensor(o[:, c].rearrange("p (h w) -> p h w", w=DH), src[:, :, 0:DH],
                                            rden[:, c].unsqueeze(2).to_broadcast([P, H, DH]), ALU.mult).then_inc(s["o_ok"], 1)
                        if h == 5 and active(b):
                            pick(b)
                        if h == 7 and active(b):
                            slots(b)
                        if h == 9 and active(a):
                            wait(dve, "qn_pe", a)
                            wait(dve, "o_ok", a, 4)
                            for c in range(NTC):
                                v.tensor_tensor(oq[:, c].rearrange("p (o h w) -> p o h w", o=NCH, h=HPC),
                                                o[:, c].rearrange("p (o h w) -> p o h w", o=NCH, h=HPC),
                                                M_ps[2][:, c * C:(c + 1) * C].rearrange("p (o w h) -> p o h w", o=NCH, h=HPC),
                                                ALU.add).then_inc(s["oq_ok"], 1)
                            wait(dve, "oq_ok", a, 2)
                            stats(a, oq, stx, mvx, "lnx")
                        if h == 10 and active(cur):
                            neg_cut(cur, 0, 0)
                        if h == 11 and active(prv):
                            copy_sums(prv, 0)
                        if h == 12:
                            if active(a):
                                wait(dve, "rstdx", a, 2)
                                wait(dve, "x1b_ok", a)
                                for c in range(NTC):
                                    v.scalar_tensor_tensor(y1[:, c], oq[:, c], mvx[:, c, 0:1], g_bc[:, :],
                                                           ALU.subtract, ALU.mult).then_inc(s["y_ok"], 1)
                                for c in range(NTC):
                                    wait(dve, "y_ok", a, 4, c + 1)
                                    v.scalar_tensor_tensor(y2[:, c], y1[:, c], rsx[:, 1, c:c + 1], x1[:, a.mod(4), c],
                                                           ALU.mult, ALU.add).then_inc(s["y_ok"], 1)
                            if active(n):
                                wait(dve, "v_pe", n)
                                wait(dve, "v_ok", n - 1, 2)
                                v.tensor_tensor(v_sum[:, :, :], M_ps[0][:, :].rearrange("p (k c) -> p k c", k=NTC),
                                                bv_bc[:, :].unsqueeze(1).to_broadcast([P, NTC, C]), ALU.add).then_inc(s["v_added"], 1)
                        if h == 13 and active(a):
                            wait(dve, "y_ok", a, 4)
                            stats(a, y2, st2, mv2, "ln2")
                        if h == 15 and active(a):
                            wait(dve, "rstd2", a, 2)
                            wait_ring(dve, scat[a.mod(2)], a - 2, 2, 16 * NTC)
                            for c in range(NTC):
                                v.tensor_scalar(row[:, a.mod(2), c, 0:C], y2[:, c], mv2[:, c, 0:1], rs2[:, 1, c:c + 1],
                                                ALU.subtract, ALU.mult).then_inc(s["x2_ok"], 1)
                            wait(dve, "id_ok", a - 1, 2)
                            v.tensor_copy(row[:, a.mod(2), :, C + 1].bitcast(I32), ids[:, :]).then_inc(s["id_ok"], 1)
                            v.tensor_scalar(ids[:, :], ids[:, :], float(TOK), None, ALU.add).then_inc(s["id_ok"], 1)

                def neg_cut(item, half, b):
                    wait(dve, "negT", item, 2, half + 1)
                    wait_value(dve, "neg_out", item.times(32, 16 * half))
                    src = M_ps[b][0:HPC, 0:TOK]
                    v.tensor_copy(nm_pieces[:, 0], src).then_inc(s["neg_ok"], 1)
                    wait(dve, "neg_ok", item, 4, 2 * half + 1)
                    v.tensor_tensor(nm_pieces[:, 1], src, nm_pieces[:, 0].bitcast(F32), ALU.subtract).then_inc(s["neg_ok"], 1)

                def copy_sums(item, pair):
                    wait(dve, "pv", item, 4, 2 * pair + 2)
                    if pair == 0:
                        wait(dve, "x_pe", item - 1, 2)
                    v.tensor_copy(oT[:, 2 * pair:2 * pair + 2, :].rearrange("p g t -> p (g t)"), O_ps[:, :]).then_inc(s["o_ev"], 1)

                def pick(b):
                    wait(dve, "nx_ok", b, 2)
                    wait(dve, "dist_pe", b)
                    for c in range(NTC):
                        v.tensor_scalar(dist[:, 0, c], cent_norm[:, :], nx[:, c:c + 1], None, ALU.add).then_inc(s["pick"], 1)
                    wait(dve, "pick", b, 7, 2)
                    v.tensor_tensor(dist[:, 1], dist[:, 0], M_ps[2][:, 0:NTC * E].rearrange("p (c e) -> p c e", c=NTC), ALU.add).then_inc(s["pick"], 1)
                    wait(dve, "pick", b, 7, 3)
                    v.tensor_reduce(least[:, :], dist[:, 1], AX.X, ALU.min).then_inc(s["pick"], 1)
                    wait(dve, "pick", b, 7, 4)
                    v.tensor_tensor(cand[:, 0], dist[:, 1], least[:, :].unsqueeze(2).to_broadcast([P, NTC, E]), ALU.is_gt).then_inc(s["pick"], 1)
                    wait(dve, "pick", b, 7, 5)
                    v.scalar_tensor_tensor(cand[:, 1], cand[:, 0], float(E), expert_no[:, :, :], ALU.mult, ALU.add).then_inc(s["pick"], 1)
                    wait(dve, "pick", b, 7, 6)
                    v.tensor_reduce(choice[:, :], cand[:, 1], AX.X, ALU.min).then_inc(s["slot_ok"], 1)
                    wait(dve, "slot_ok", b, 7, 1)
                    ch = choice[:, :].unsqueeze(2).to_broadcast([P, NTC, E])
                    v.tensor_tensor(onehot[:, :, :], expert_no[:, :, :], ch, ALU.is_equal).then_inc(s["slot_ok"], 1)
                    v.tensor_tensor(onehot_bf[:, :, :], expert_no[:, :, :], ch, ALU.is_equal).then_inc(s["pick"], 1)

                def slots(b):
                    wait(dve, "rank_pe", b)
                    wait(dve, "slot_ok", b, 7, 2)
                    wait(dve, "slot_ok", b - 1, 7)
                    v.tensor_tensor(place[:, 0], M_ps[2][:, 64:64 + NTC * E].rearrange("p (c e) -> p c e", c=NTC),
                                    filled[:, :].unsqueeze(1).to_broadcast([P, NTC, E]), ALU.add).then_inc(s["slot_ok"], 1)
                    wait(dve, "slot_ok", b, 7, 3)
                    v.tensor_tensor(place[:, 1], place[:, 0], onehot[:, :, :], ALU.mult).then_inc(s["slot_ok"], 1)
                    v.tensor_tensor(filled[:, :], filled[:, :], M_ps[2][:, 64 + NTC * E:64 + (NTC + 1) * E], ALU.add).then_inc(s["slot_ok"], 1)
                    wait(dve, "slot_ok", b, 7, 4)
                    v.tensor_reduce(slot_f[:, :], place[:, 1], AX.X, ALU.add).then_inc(s["slot_ok"], 1)
                    wait(dve, "slot_ok", b, 7, 6)
                    wait_ring(dve, scat[b.mod(2)], b - 2, 2, 16 * NTC)
                    v.tensor_copy(slot[:, b.mod(2)], slot_f[:, :]).then_inc(s["slot_ok"], 1)

                steps(dve, step)

        def sb2(name, shape, dt=F32):
            return stack.enter_context(nc.sbuf_tensor(name, shape, dt))

        dn_sb = sb2("dn_sb", [P, E * HCH * C])
        base = sb2("base", [1, E])
        count = sb2("count", [1, E])
        tiles = sb2("tiles", [1, E])
        ends = sb2("ends", [1, E])
        starts = sb2("starts", [1, E])
        first = sb2("first", [1, E])
        eno = sb2("eno", [1, E])
        tno = sb2("tno", [1, NTILES])
        tno128 = sb2("tno128", [1, NTILES])
        own = sb2("own", [1, 3, NTILES, E])
        picked = sb2("picked", [1, 2, NTILES, E])
        owned = sb2("owned", [1, NTILES])
        row_f = sb2("row_f", [1, 2, NTILES])
        eno_f = sb2("eno_f", [1, NTILES])
        RING = 4
        xr = sb2("xr", [P, RING, ROWW])
        xs = sb2("xs", [P, 2, C])
        xsT = sb2("xsT", [P, 2, NCH, P])
        gate = sb2("gate", [P, 2, HID])
        gated = sb2("gated", [P, 2, HID])
        gT = sb2("gT", [P, 2, HCH, P])
        y = sb2("y", [P, 2, C])
        st3 = sb2("st3", [P, 6])
        mv3 = sb2("mv3", [P, 2])
        rs3 = sb2("rs3", [P, 2])
        res = sb2("res", [P, 2, C])
        token = sb2("token", [P, 2], U32)
        XT_ps, A_ps, G_ps, GT_ps, Y_ps = (bank(n) for n in ("XT", "A", "G", "GT", "Y"))
        names2 = """down_in table_pool table tails tile0 tile1 tile2 tile3 xs_ok xsT_pe xsT_ok g_pe a_pe gate_ok gated_ok gT_pe gT_act
            y_pe y2_ok ln3 rstd3 res_ok token_ok sent0 sent1 pool_waits sp_waits dve_waits"""
        z = {n: sem("z_" + n) for n in names2.split()}
        tile_in = [z[f"tile{r}"] for r in range(RING)]
        sent = [z["sent0"], z["sent1"]]
        out_rows = out.rearrange("n t d -> (n t) d")

        def const_wait(eng):
            if eng.engine in (mybir.EngineType.Pool, mybir.EngineType.SP):
                eng.sem_inc(z["pool_waits" if eng.engine == mybir.EngineType.Pool else "sp_waits"], 1)

        def wait_value(eng, name, v):
            sm = z[name] if isinstance(name, str) else name
            if isinstance(v, int):
                if v > 0:
                    eng.wait_ge(sm, v)
            else:
                eng.wait_ge(sm, v)
                const_wait(eng)

        def wait(eng, name, item, per=1, j=None):
            wait_value(eng, name, item.times(per, per if j is None else j))

        def wait_ring(eng, sm, item, ring, per):
            wait_value(eng, sm, item.uses(ring) * per)

        def steps(eng, body):
            loops = (NTILES - 2 - 3) // 4
            for n in range(-1, 3):
                body(Item(0, n))
            with eng.Fori(0, loops) as i:
                for k in range(4):
                    body(Item(i, 3 + k))
            for n in range(3 + 4 * loops, NTILES + 1):
                body(Item(0, n))

        def active(item):
            return item.within(0, NTILES)

        with nc.Block() as block:
            @block.sync
            def _(sp):
                for e in range(E):
                    dst = dn_sb[:, e * HCH * C:(e + 1) * HCH * C].rearrange("p (o n) -> p o n", o=HCH)
                    sp.dma_start(dst, down_w[e].rearrange("(o p) n -> p o n", p=P)).then_inc(z["down_in"], 16)
                sp.wait_ge(z["table_pool"], 4)
                sp.wait_ge(z["table"], TABLE)
                for e in range(E):
                    r = sp.value_load(tail_row[0:1, e:e + 1], min_val=0, max_val=PAD - P)
                    sp.dma_start(buckets[bass.ds(r, P), :], pad_row[:, :]).then_inc(z["tails"], 16)
                sp.wait_ge(z["tails"], 16 * E)

                def step(t):
                    n = t + 2
                    if active(n):
                        if n.runtime or n.k >= RING:
                            wait(sp, "token_ok", n - RING)
                        r = sp.value_load(tile_row[0:1, bass.ds(n.times(1), 1)], min_val=0, max_val=PAD)
                        sp.dma_start(xr[:, n.mod(RING), :], buckets[bass.ds(r, P), :]).then_inc(tile_in[n.mod(RING)], 16)

                step(Item(0, -2))
                steps(sp, step)
                for p in range(2):
                    sp.wait_ge(sent[p], 16 * ((NTILES + 1 - p) // 2))

            @block.gpsimd
            def _(pool):
                g = nc.gpsimd
                kw = dict(allow_small_or_imprecise_dtypes=True, channel_multiplier=0, base=0)
                g.iota(base[:, :], pattern=[[CAP, E]], **kw).then_inc(z["table_pool"], 1)
                g.iota(eno[:, :], pattern=[[1, E]], **kw).then_inc(z["table_pool"], 1)
                g.iota(tno[:, :], pattern=[[1, NTILES]], **kw).then_inc(z["table_pool"], 1)
                g.iota(tno128[:, :], pattern=[[P, NTILES]], **kw).then_inc(z["table_pool"], 1)
                pool.wait_ge(z["table_pool"], 4)

                def step(t):
                    n = t - 1
                    if active(n):
                        wait(pool, "ln3", n, 2)
                        g.tensor_scalar(rs3[:, 0:1], mv3[:, 1:2], LN_EPS, None, ALU.add).then_inc(z["rstd3"], 1)
                        wait(pool, "rstd3", n, 2, 1)
                        g.tensor_tensor(rs3[:, 1:2], rs3[:, 0:1], neg_half[:, :], ALU.pow).then_inc(z["rstd3"], 1)
                        wait(pool, "res_ok", n)
                        wait(pool, "token_ok", n)
                        g.indirect_dma_start(out=out_rows, out_offset=bass.IndirectOffsetOnAxis(ap=token[:, n.mod(2):n.mod(2) + 1], axis=0),
                                             in_=res[:, n.mod(2), :], in_offset=None, bounds_check=SEQ * TOK - 1,
                                             oob_is_err=False).then_inc(sent[n.mod(2)], 16)

                steps(pool, step)

            @block.scalar
            def _(act):
                a_ = nc.scalar

                def step(t):
                    m = t - 1
                    if active(m):
                        wait(act, "gT_pe", m)
                        a_.activation(gT[:, m.mod(2)].rearrange("p o t -> p (o t)"), GT_ps[:, :], ACT.Copy).then_inc(z["gT_act"], 1)
                    n = t + 1
                    if active(n):
                        wait(act, "xsT_pe", n)
                        wait(act, "a_pe", n - 2)
                        a_.activation(xsT[:, n.mod(2)].rearrange("p o t -> p (o t)"), XT_ps[:, 0:NCH * P], ACT.Copy).then_inc(z["xsT_ok"], 1)
                    if active(t):
                        wait(act, "g_pe", t)
                        wait(act, "gated_ok", t - 2)
                        a_.activation(gate[:, t.mod(2)], G_ps[:, :], ACT.Silu).then_inc(z["gate_ok"], 1)

                steps(act, step)

            @block.tensor
            def _(pe):
                t_ = nc.tensor
                pe.wait_ge(z["table"], TABLE)
                pe.wait_ge(z["down_in"], 16 * E)

                def step(t):
                    m, n = t - 1, t + 1
                    if active(m):
                        wait(pe, "gated_ok", m)
                        wait(pe, "gT_act", m - 1)
                        for c in range(HCH):
                            last = t_.transpose(GT_ps[:, c * P:(c + 1) * P], gated[:, m.mod(2), c * P:(c + 1) * P], ident[:, :])
                        last.then_inc(z["gT_pe"], 1)
                    if active(n):
                        wait(pe, "xs_ok", n)
                        wait(pe, "xsT_ok", n - 1)
                        for c in range(NCH):
                            last = t_.transpose(XT_ps[:, c * P:(c + 1) * P], xs[:, n.mod(2), c * P:(c + 1) * P], ident[:, :])
                        last.then_inc(z["xsT_pe"], 1)
                    if active(t):
                        off = pe.value_load(tile_up[0:1, bass.ds(t.times(1), 1)], min_val=0, max_val=(E - 1) * NCH * 2 * HID)
                        wait(pe, "xsT_ok", t)
                        wait(pe, "gated_ok", t - 1)
                        for half, ps, name in ((1, G_ps, "g_pe"), (0, A_ps, "a_pe")):
                            for ic in range(NCH):
                                last = t_.matmul(ps[:, :], xsT[:, t.mod(2), ic, :],
                                                 up_sb[:, bass.ds(off + (ic * 2 * HID + half * HID), HID)],
                                                 start=(ic == 0), stop=(ic == NCH - 1))
                            last.then_inc(z[name], 1)
                    if active(m):
                        off = pe.value_load(tile_dn[0:1, bass.ds(m.times(1), 1)], min_val=0, max_val=(E - 1) * HCH * C)
                        wait(pe, "gT_act", m)
                        wait(pe, "y2_ok", m - 1)
                        for c in range(HCH):
                            last = t_.matmul(Y_ps[:, 0:C], gT[:, m.mod(2), c, :], dn_sb[:, bass.ds(off + c * C, C)],
                                             start=(c == 0), stop=(c == HCH - 1))
                        last.then_inc(z["y_pe"], 1)

                steps(pe, step)

            @block.vector
            def _(dve):
                v = nc.vector
                done = [0]

                def setup(ins):
                    done[0] += 1
                    ins.then_inc(z["table"], 1)
                    dve.wait_ge(z["table"], done[0])

                dve.wait_ge(z["table_pool"], 4)
                setup(v.tensor_tensor(count[:, :], filled[0:1, :], base[:, :], ALU.subtract))
                setup(v.tensor_copy(tail_row[:, :], filled[0:1, :]))
                setup(v.tensor_scalar(tiles[:, :], count[:, :], float(P - 1), 1.0 / P, ALU.add, ALU.mult))
                setup(v.tensor_scalar(tiles[:, :], tiles[:, :], 0.5 / P - 0.5, None, ALU.add))
                setup(v.tensor_scalar(tiles[:, :], tiles[:, :], ROUND, -ROUND, ALU.add, ALU.add))
                setup(v.tensor_copy(ends[:, 0:1], tiles[:, 0:1]))
                for e in range(1, E):
                    setup(v.tensor_tensor(ends[:, e:e + 1], ends[:, e - 1:e], tiles[:, e:e + 1], ALU.add))
                setup(v.tensor_tensor(starts[:, :], ends[:, :], tiles[:, :], ALU.subtract))
                setup(v.scalar_tensor_tensor(first[:, :], starts[:, :], -float(P), base[:, :], ALU.mult, ALU.add))
                every = [1, NTILES, E]
                tb = tno[:, :].unsqueeze(2).to_broadcast(every)
                setup(v.tensor_tensor(own[:, 0], tb, starts[:, :].unsqueeze(1).to_broadcast(every), ALU.is_ge))
                setup(v.tensor_tensor(own[:, 1], tb, ends[:, :].unsqueeze(1).to_broadcast(every), ALU.is_lt))
                setup(v.tensor_tensor(own[:, 2], own[:, 0], own[:, 1], ALU.mult))
                setup(v.tensor_tensor(picked[:, 0], own[:, 2], first[:, :].unsqueeze(1).to_broadcast(every), ALU.mult))
                setup(v.tensor_tensor(picked[:, 1], own[:, 2], eno[:, :].unsqueeze(1).to_broadcast(every), ALU.mult))
                setup(v.tensor_reduce(owned[:, :], own[:, 2], AX.X, ALU.add))
                setup(v.tensor_reduce(row_f[:, 0], picked[:, 0], AX.X, ALU.add))
                setup(v.tensor_reduce(eno_f[:, :], picked[:, 1], AX.X, ALU.add))
                setup(v.scalar_tensor_tensor(row_f[:, 1], tno128[:, :], -float(PAD), row_f[:, 0], ALU.add, ALU.add))
                setup(v.tensor_tensor(row_f[:, 0], row_f[:, 1], owned[:, :], ALU.mult))
                setup(v.tensor_scalar(tile_row[:, :], row_f[:, 0], float(PAD), None, ALU.add))
                setup(v.tensor_scalar(tile_up[:, :], eno_f[:, :], float(NCH * 2 * HID), None, ALU.mult))
                setup(v.tensor_scalar(tile_dn[:, :], eno_f[:, :], float(HCH * C), None, ALU.mult))
                assert done[0] == TABLE

                def step(t):
                    m, n = t - 1, t + 1
                    if active(n):
                        wait_ring(dve, tile_in[n.mod(RING)], n, RING, 16)
                        wait(dve, "xsT_pe", n - 2)
                        v.scalar_tensor_tensor(xs[:, n.mod(2)], xr[:, n.mod(RING), 0:C], xr[:, n.mod(RING), C:C + 1], scale_bc[:, :],
                                               ALU.mult, ALU.mult).then_inc(z["xs_ok"], 1)
                    if active(t):
                        wait(dve, "gate_ok", t)
                        wait(dve, "a_pe", t)
                        wait(dve, "gT_pe", t - 2)
                        v.tensor_tensor(gated[:, t.mod(2)], A_ps[:, :], gate[:, t.mod(2)], ALU.mult).then_inc(z["gated_ok"], 1)
                    if active(m):
                        wait(dve, "y_pe", m)
                        v.scalar_tensor_tensor(y[:, m.mod(2)], xr[:, m.mod(RING), 0:C], 2.0, Y_ps[:, 0:C],
                                               ALU.mult, ALU.add).then_inc(z["y2_ok"], 1)
                        wait(dve, "y2_ok", m)
                        v.bn_stats(st3[:, :], y[:, m.mod(2)]).then_inc(z["ln3"], 1)
                        wait_ring(dve, sent[m.mod(2)], m - 2, 2, 16)
                        v.tensor_copy(token[:, m.mod(2):m.mod(2) + 1], xr[:, m.mod(RING), C + 1:C + 2].bitcast(U32)).then_inc(z["token_ok"], 1)
                        wait(dve, "ln3", m, 2, 1)
                        dve.sem_inc(z["dve_waits"], 1)
                        v.bn_aggr(mv3[:, :], st3[:, :]).then_inc(z["ln3"], 1)
                        wait(dve, "rstd3", m, 2)
                        v.tensor_scalar(res[:, m.mod(2)], y[:, m.mod(2)], mv3[:, 0:1], rs3[:, 1:2],
                                        ALU.subtract, ALU.mult).then_inc(z["res_ok"], 1)

                steps(dve, step)


TABLE = 28


_INS = ["x", "ctx_1024", "L0_attn_lmlg", "L0_attn_theta", "L0_attn_last_conv_init", "L0_xattn_Wq", "L0_xattn_bq",
        "L0_xattn_Wk", "L0_xattn_bk", "L0_xattn_Wv", "L0_xattn_bv", "L0_xattn_ln_g", "L0_xattn_ln_b",
        "L0_ffn_scale", "L0_ffn_centroids", "L0_ffn_up_w", "L0_ffn_down_w"]
_BY_CHANNEL = {"L0_xattn_Wq", "L0_xattn_bq", "L0_xattn_Wk", "L0_xattn_bk"}


def kernel(**inputs):
    import concourse.bacc as _bacc
    from concourse.bass_utils import run_bass_kernel_spmd as _run

    nc = _bacc.Bacc("TRN2", target_bir_lowering=False, num_devices=1)
    arrays, args = {}, []
    for name in _INS:
        a = np.asarray(inputs[name])
        if name in _BY_CHANNEL:
            lead = a.shape[:-1]
            a = a.reshape(*lead, NCH, HPC, DH).swapaxes(-1, -2).reshape(*lead, C)
        a = np.ascontiguousarray(a)
        arrays[f"in_{name}"] = a
        args.append(nc.dram_tensor(f"in_{name}", a.shape, mybir.dt.from_np(a.dtype), kind="ExternalInput").ap())
    args.append(nc.dram_tensor("out_0", (SEQ, TOK, C), F32, kind="ExternalOutput").ap())
    build(nc, *args)
    r = _run(nc, [arrays], core_ids=[0])
    return r.results[0]["out_0"]
```

```python
import numpy as np
import concourse.bass as bass
from concourse import mybir
from contextlib import ExitStack

F32 = mybir.dt.float32
F32R = mybir.dt.float32r
BF16 = mybir.dt.bfloat16
U32 = mybir.dt.uint32
I32 = mybir.dt.int32
ALU = mybir.AluOpType
ACT = mybir.ActivationFunctionType
AX = mybir.AxisListType

P = 128
SEQ, TOK, C = 32, 256, 256
NCH = C // P
NTC = TOK // P
H = 16
DH = C // H
HPC = H // NCH
E, HID = 8, 512
HCH = HID // P
LN_EPS, RMS_EPS = 1e-5, 1e-6
ROWW = C + 2
CAP = SEQ * TOK + P
PAD = E * CAP
NTILES = SEQ * TOK // P + E - 1
SETUP_DVE = 15
NOID = 1 << 20
STACK = 3 * DH
AUG = STACK + 2
TWO_PI_A = 6.28125
TWO_PI_B = float(np.float32(2 * np.pi - TWO_PI_A))
TWO_PI_C = float(np.float32(2 * np.pi - TWO_PI_A - TWO_PI_B))
ROUND = 1.5 * 2 ** 23


class Item:

    def __init__(self, i, k):
        self.i, self.k = i, k
        self.runtime = not isinstance(i, int)

    def __add__(self, d):
        return Item(self.i, self.k + d)

    def __sub__(self, d):
        return Item(self.i, self.k - d)

    def mod(self, m):
        return self.k % m

    def times(self, c, j=0):
        return self.i * (4 * c) + (self.k * c + j) if self.runtime else (4 * self.i + self.k) * c + j

    def uses(self, m):
        return self.i * (4 // m) + (self.k // m + 1) if self.runtime else (4 * self.i + self.k) // m + 1

    def within(self, lo, hi):
        return self.runtime or lo <= 4 * self.i + self.k < hi


def build(nc, x, ctx_in, lmlg, theta, last_conv, Wq, bq, Wk, bk, Wv, bv, ln_g, ln_b, ffn_scale, centroids, up_w, down_w, out):
    stack = ExitStack()
    with stack:
        def sb(name, shape, dt=F32):
            return stack.enter_context(nc.sbuf_tensor(name, shape, dt))

        def bank(name, scope=stack):
            return scope.enter_context(nc.psum_tensor(name, [P, 512], F32))

        def sem(name):
            return stack.enter_context(nc.semaphore(name))

        q_dram = nc.dram_tensor("q_pieces", (2, NCH, 2, P, TOK), F32)
        k_dram = nc.dram_tensor("k_pieces", (2, NCH, 2, P, TOK), F32)
        m_dram = nc.dram_tensor("neg_max", (2, 2, 2, HPC, TOK), F32)
        buckets = nc.dram_tensor("buckets", (PAD + P, ROWW), F32)

        up_sb = sb("up_sb", [P, E * NCH * 2 * HID])
        ident = sb("ident", [P, P])
        scale_bc = sb("scale_bc", [P, C])
        neg_half = sb("neg_half", [P, 1])
        filled = sb("filled", [P, E])
        pad_row = sb("pad_row", [P, ROWW])
        tile_row = sb("tile_row", [1, NTILES], I32)
        tile_up = sb("tile_up", [1, NTILES], I32)
        tile_dn = sb("tile_dn", [1, NTILES], I32)
        tail_row = sb("tail_row", [1, E], I32)

        phase1 = ExitStack()

        def sb1(name, shape, dt=F32):
            return phase1.enter_context(nc.sbuf_tensor(name, shape, dt))

        with phase1:
            wq_sb = sb1("wq_sb", [P, NCH, C])
            wk_sb = sb1("wk_sb", [P, NCH, C])
            wv_sb = sb1("wv_sb", [P, NCH, C])
            bq_sb = sb1("bq_sb", [P, NCH])
            bk_sb = sb1("bk_sb", [P, NCH])
            bv_cut = sb1("bv_cut", [1, 2, C], F32R)
            g_bc = sb1("g_bc", [P, C])
            b_bc = sb1("b_bc", [P, C])
            decay_re = sb1("decay_re", [P, C])
            decay_im = sb1("decay_im", [P, C])
            centT = sb1("centT", [P, NCH, E])
            cent_sq = sb1("cent_sq", [P, NCH, E])
            cent_norm = sb1("cent_norm", [P, E])
            ones_r = sb1("ones_r", [P, P], F32R)
            ones_bf = sb1("ones_bf", [P, P], BF16)
            before = sb1("before", [P, P], BF16)
            expert_no = sb1("expert_no", [P, NTC, E])
            state = sb1("state", [P, 2, NTC, C])
            by_im = sb1("by_im", [P, 2, NTC, C])
            xt = sb1("xt", [P, 2, NTC, C])
            ct = sb1("ct", [P, 2, NTC, C])
            u = sb1("u", [P, NTC, C])
            st1 = sb1("st1", [P, NTC, 6])
            mv1 = sb1("mv1", [P, NTC, 2])
            rs1 = sb1("rs1", [P, 2, NTC])
            x1 = sb1("x1", [P, 4, NTC, C])
            x1T = sb1("x1T", [P, NCH, TOK])
            ctT = sb1("ctT", [P, NCH, TOK])
            q32 = sb1("q32", [P, NCH, TOK])
            qn = sb1("qn", [P, 4, NTC, C])
            k32 = sb1("k32", [P, NCH, TOK])
            q_hi = sb1("q_hi", [P, NCH, TOK], F32R)
            q_lo = sb1("q_lo", [P, NCH, TOK], F32R)
            k_hi = sb1("k_hi", [P, NCH, TOK], F32R)
            k_lo = sb1("k_lo", [P, NCH, TOK], F32R)
            VW = DH + 1
            v_aug = sb1("v_aug", [P, 4, NTC, H * VW + 32 - VW])
            q_st = sb1("q_st", [P, H, TOK], F32R)
            k_st = sb1("k_st", [P, H, TOK], F32R)
            neg_max = sb1("neg_max_sb", [P, 2, NTC, H])
            nm_pieces = sb1("nm_pieces", [HPC, 2, TOK], F32R)
            probs = sb1("probs", [P, 8, NTC, TOK])
            lm_t, th_t, turns, angle, angle2 = (probs[:, k, 0, :] for k in range(5))
            trig = probs[:, 5]
            cent, bv_row = probs[0:E, 6, 0, :], probs[0:1, 7, 0, :]
            oT = sb1("oT", [P, H // 4, TOK])
            rden = sb1("rden", [P, NTC, H])
            o = sb1("o", [P, NTC, C])
            oq = sb1("oq", [P, NTC, C])
            stx = sb1("stx", [P, NTC, 6])
            mvx = sb1("mvx", [P, NTC, 2])
            rsx = sb1("rsx", [P, 2, NTC])
            y1, y2 = o, oq
            st2 = sb1("st2", [P, NTC, 6])
            mv2 = sb1("mv2", [P, NTC, 2])
            rs2 = sb1("rs2", [P, 2, NTC])
            row = sb1("row", [P, 2, NTC, ROWW])
            junk = sb1("junk", [P, C], BF16)
            ms = sb1("ms", [P, 2, NTC])
            xn = sb1("xn", [P, NTC, C])
            nx = sb1("nx", [P, NTC])
            xnT = sb1("xnT", [P, NCH, TOK])
            dist = sb1("dist", [P, 2, NTC, E])
            least = sb1("least", [P, NTC])
            cand = sb1("cand", [P, 2, NTC, E])
            choice = sb1("choice", [P, NTC])
            onehot = sb1("onehot", [P, NTC, E])
            onehot_bf = sb1("onehot_bf", [P, NTC, E], BF16)
            place = sb1("place", [P, 2, NTC, E])
            slot_f = sb1("slot_f", [P, NTC])
            slot = sb1("slot", [P, 2, NTC], U32)
            ids = sb1("ids", [P, NTC], I32)

            S_ps = [bank("S0", phase1), bank("S1", phase1)]
            T_ps = [bank("T0", phase1), bank("T1", phase1)]
            O_ps = bank("O", phase1)
            M_ps = [bank(n, phase1) for n in ("M0", "M1", "M2")]
            names = """params setup_pool setup_dve setup_act setup_pe pads ups ident_ok
                x_in0 x_in1 ctx_in0 ctx_in1 conv u_ok ln1 rstd1 x1_ok x1T_pe x1T_ok ctT_pe ctT_ok
                q_pe q_ok k_pe k_ok q_cut k_cut v_pe v_ok q_out0 q_out1 stack0 stack1 s_pe max_ok
                negT neg_ok neg_out neg_in0 neg_in1 t_pe exp_ok pv o_ev x_pe o_ok qn_pe qn_ok oq_ok lnx rstdx
                x1b_ok y_ok ln2 rstd2 x2_ok ms_ok rms xn_ok nx_ok xnT_pe xnT_ok dist_pe pick rank_pe slot_ok
                id_ok scat0 scat1 pool_waits sp_waits dve_waits"""
            s = {n: sem(n) for n in names.split()}
            x_in, ctx_in_s, q_out, stack_in = ([s[a + "0"], s[a + "1"]] for a in ("x_in", "ctx_in", "q_out", "stack"))
            neg_in, scat = [s["neg_in0"], s["neg_in1"]], [s["scat0"], s["scat1"]]

            def wait(eng, name, item, per=1, j=None):
                if not item.runtime and item.k >= SEQ:
                    item, j = Item(0, SEQ - 1), per
                wait_value(eng, name, item.times(per, per if j is None else j))

            def wait_value(eng, name, v):
                sm = s[name] if isinstance(name, str) else name
                if isinstance(v, int):
                    if v > 0:
                        eng.wait_ge(sm, v)
                else:
                    eng.wait_ge(sm, v)
                    after_register_wait(eng)

            def wait_ring(eng, sm, item, ring, per):
                if not item.runtime:
                    while item.k >= SEQ:
                        item = item - ring
                wait_value(eng, sm, item.uses(ring) * per)

            def after_register_wait(eng):
                if eng.engine in (mybir.EngineType.Pool, mybir.EngineType.SP):
                    eng.sem_inc(s["pool_waits" if eng.engine == mybir.EngineType.Pool else "sp_waits"], 1)

            def steps(eng, body):
                lead = 5
                for n in range(-2, lead):
                    body(Item(0, n))
                loops = (SEQ - 3 - lead) // 4
                with eng.Fori(0, loops) as i:
                    for k in range(4):
                        body(Item(i, lead + k))
                for n in range(lead + 4 * loops, SEQ + 3):
                    body(Item(0, n))

            def active(item):
                return item.within(0, SEQ)

            block = phase1.enter_context(nc.Block())

            x_v = x.rearrange("n (c p) d -> p (n c) d", p=P)
            c_v = ctx_in.rearrange("n (c p) d -> p (n c) d", p=P)

            def bcast(v):
                return v.rearrange("(a n) -> a n", a=1).to_broadcast([P, C])

            @block.sync
            def _(sp):
                def load_x(item):
                    if not active(item):
                        return
                    p = item.mod(2)
                    wait(sp, "u_ok", item - 2)
                    sp.dma_start(xt[:, p], x_v[:, bass.ds(item.times(NTC), NTC), :]).then_inc(x_in[p], 16)

                def load_context(item):
                    if not active(item):
                        return
                    p = item.mod(2)
                    wait(sp, "ctT_pe", item - 2)
                    sp.dma_start(ct[:, p], c_v[:, bass.ds(item.times(NTC), NTC), :]).then_inc(ctx_in_s[p], 16)

                def write_neg(item, half):
                    if not active(item):
                        return
                    p = item.mod(2)
                    wait(sp, "neg_ok", item, 4, 2 * half + 2)
                    wait(sp, neg_in[half], item - 2, 16)
                    sp.dma_start(m_dram[p, half].rearrange("w h t -> h w t"), nm_pieces[:, :, :].bitcast(F32)).then_inc(s["neg_out"], 16)

                def read_neg(item, half):
                    if not active(item):
                        return
                    p = item.mod(2)
                    wait(sp, "neg_out", item, 32, 16 * half + 16)
                    sp.dma_start(q_st[64 * p + STACK:64 * p + AUG, half * HPC:(half + 1) * HPC, :].bitcast(F32),
                                 m_dram[p, half]).then_inc(neg_in[half], 16)

                def write_pieces(item, dram, hi, lo, name):
                    p = item.mod(2)
                    wait(sp, name, item)
                    for w, piece in enumerate((hi, lo)):
                        sp.dma_start(dram[p, :, w].rearrange("o p t -> p o t"), piece[:, :, :].bitcast(F32)).then_inc(q_out[p], 16)

                def read_stacks(item, half):
                    if not active(item):
                        return
                    p = item.mod(2)
                    b = 64 * p
                    wait(sp, "t_pe", item - 2, H, HPC * (half + 1))
                    hs = slice(half * HPC, (half + 1) * HPC)
                    view = "w (c h) t -> (w c) h t"
                    qd = q_dram[p, half].rearrange(view, h=HPC)
                    kd = k_dram[p, half].rearrange(view, h=HPC)
                    sp.dma_start(q_st[b:b + DH, hs, :].bitcast(F32), qd[0:DH]).then_inc(stack_in[half], 16)
                    sp.dma_start(q_st[b + DH:b + 3 * DH, hs, :].bitcast(F32), qd).then_inc(stack_in[half], 16)
                    sp.dma_start(k_st[b:b + 2 * DH, hs, :].bitcast(F32), kd).then_inc(stack_in[half], 16)
                    sp.dma_start(k_st[b + 2 * DH:b + 3 * DH, hs, :].bitcast(F32), kd[0:DH]).then_inc(stack_in[half], 16)

                for dst, src in ((wq_sb, Wq), (wk_sb, Wk), (wv_sb, Wv)):
                    sp.dma_start(dst[:, :, :], src.rearrange("(o p) c -> p o c", p=P)).then_inc(s["params"], 16)
                for dst, src in ((bq_sb, bq), (bk_sb, bk)):
                    sp.dma_start(dst[:, :], src.rearrange("(o p) -> p o", p=P), allow_slow_non_contiguous=True).then_inc(s["params"], 16)
                for dst, src in ((g_bc[:, :], ln_g), (b_bc[:, :], ln_b), (lm_t, lmlg), (th_t, theta), (scale_bc[:, :], ffn_scale)):
                    sp.dma_start(dst, bcast(src)).then_inc(s["params"], 16)
                sp.dma_start(bv_row, bv.rearrange("(a n) -> a n", a=1)).then_inc(s["params"], 16)
                for c in range(NTC):
                    sp.dma_start(state[:, 0, c, :], bcast(last_conv)).then_inc(s["params"], 16)
                sp.dma_start(cent, centroids).then_inc(s["params"], 16)
                sp.wait_ge(s["ident_ok"], 2)
                sp.wait_ge(s["setup_pool"], 13)
                load_x(Item(0, 0))
                load_context(Item(0, 0))

                def ups(n):
                    for e in range(2 * n, 2 * n + 2):
                        dst = up_sb[:, e * NCH * 2 * HID:(e + 1) * NCH * 2 * HID].rearrange("p (o n) -> p o n", o=NCH)
                        sp.dma_start(dst, up_w[e].rearrange("(o p) n -> p o n", p=P)).then_inc(s["ups"], 16)

                def step(t):
                    nxt = t + 1
                    load_x(t + 3)
                    load_context(t + 3)
                    write_neg(t - 1, 1)
                    read_neg(t - 1, 1)
                    if active(nxt):
                        for half in range(2):
                            wait(sp, stack_in[half], nxt - 2, 64)
                        write_pieces(nxt, q_dram, q_hi, q_lo, "q_cut")
                        write_pieces(nxt, k_dram, k_hi, k_lo, "k_cut")
                    write_neg(t, 0)
                    if active(nxt):
                        wait_ring(sp, q_out[nxt.mod(2)], nxt, 2, 64)
                    read_stacks(nxt, 0)
                    read_neg(t, 0)
                    read_stacks(nxt, 1)
                    if not t.runtime and 0 <= t.k + 1 < 4:
                        ups(t.k + 1)

                steps(sp, step)
                sp.wait_ge(s["pads"], 16)
                sp.wait_ge(s["ups"], 16 * E)
                for p in range(2):
                    sp.wait_ge(scat[p], 16 * NTC * SEQ // 2)

            @block.gpsimd
            def _(pool):
                g = nc.gpsimd
                g.memset(ident[:, :], 0.0).then_inc(s["ident_ok"], 1)
                pool.wait_ge(s["ident_ok"], 1)
                g.affine_select(out=ident[:, :], in_=ident[:, :], compare_op=ALU.not_equal, fill=1.0, base=0,
                                pattern=[[-1, P]], channel_multiplier=1).then_inc(s["ident_ok"], 1)
                g.memset(neg_half[:, :], -0.5).then_inc(s["setup_pool"], 1)
                g.memset(ones_r[:, :].bitcast(F32), 1.0).then_inc(s["setup_pool"], 1)
                g.memset(ones_bf[:, :], 1.0).then_inc(s["setup_pool"], 1)
                g.memset(before[:, :], 1.0).then_inc(s["setup_pool"], 1)
                g.memset(k_st[:, :, :].bitcast(F32), 1.0).then_inc(s["setup_pool"], 1)
                g.memset(v_aug[:, :, :, :], 1.0).then_inc(s["setup_pool"], 1)
                g.memset(state[:, 1], 0.0).then_inc(s["setup_pool"], 1)
                g.memset(pad_row[:, :], 0.0).then_inc(s["setup_pool"], 1)
                g.iota(ids[:, :], pattern=[[P, NTC]], base=0, channel_multiplier=1).then_inc(s["setup_pool"], 1)
                g.iota(expert_no[:, :, :], pattern=[[0, NTC], [1, E]], base=0, channel_multiplier=0,
                       allow_small_or_imprecise_dtypes=True).then_inc(s["setup_pool"], 1)
                g.iota(filled[:, :], pattern=[[CAP, E]], base=0, channel_multiplier=0,
                       allow_small_or_imprecise_dtypes=True).then_inc(s["setup_pool"], 1)
                pool.wait_ge(s["setup_pool"], 11)
                g.affine_select(out=before[:, :], in_=before[:, :], compare_op=ALU.is_gt, fill=0.0, base=0,
                                pattern=[[1, P]], channel_multiplier=-1).then_inc(s["setup_pool"], 1)
                g.memset(pad_row[:, C + 1:C + 2].bitcast(U32), NOID).then_inc(s["setup_pool"], 1)
                pool.wait_ge(s["setup_pool"], 13)
                g.dma_start(buckets[PAD:PAD + P, :], pad_row[:, :]).then_inc(s["pads"], 16)
                pool.wait_ge(s["params"], 14 * 16)
                pool.wait_ge(s["setup_dve"], SETUP_DVE)

                re_b = decay_re[:, :].unsqueeze(1).to_broadcast([P, 2 * NTC, C])
                im_b = decay_im[:, :].unsqueeze(1).to_broadcast([P, 2 * NTC, C])
                z_all = state[:, :, :, :].rearrange("p r c d -> p (r c) d")

                def conv_products(item, j):
                    if not active(item):
                        return
                    if j == 0:
                        wait(pool, "conv", item - 1, 5)
                        g.tensor_tensor(by_im[:, :, :, :].rearrange("p r c d -> p (r c) d"), z_all, im_b, ALU.mult).then_inc(s["conv"], 1)
                    else:
                        wait(pool, "u_ok", item - 1)
                        g.tensor_tensor(z_all, z_all, re_b, ALU.mult).then_inc(s["conv"], 1)

                def conv_sum(item, j):
                    if not active(item):
                        return
                    if j == 0:
                        wait(pool, "conv", item, 5, 2)
                        g.tensor_tensor(state[:, 1], state[:, 1], by_im[:, 0], ALU.add).then_inc(s["conv"], 1)
                    else:
                        g.tensor_tensor(state[:, 0], state[:, 0], by_im[:, 1], ALU.subtract).then_inc(s["conv"], 1)

                def conv_input(item):
                    if not active(item):
                        return
                    wait_ring(pool, x_in[item.mod(2)], item, 2, 16)
                    wait(pool, "conv", item, 5, 4)
                    g.tensor_tensor(state[:, 0], state[:, 0], xt[:, item.mod(2)], ALU.add).then_inc(s["conv"], 1)

                def rstd(item, ready, per, mv, rs, done):
                    if not active(item):
                        return
                    wait(pool, ready, item, per)
                    g.tensor_scalar(rs[:, 0], mv[:, :, 1], LN_EPS, None, ALU.add).then_inc(s[done], 1)
                    wait(pool, done, item, 2, 1)
                    g.tensor_tensor(rs[:, 1], rs[:, 0], neg_half[:, :].to_broadcast([P, NTC]), ALU.pow).then_inc(s[done], 1)

                def rms(item):
                    if not active(item):
                        return
                    p = item.mod(2)
                    wait(pool, "ms_ok", item, 2)
                    g.tensor_scalar(ms[:, 1], ms[:, 0], 1.0 / C, RMS_EPS, ALU.mult, ALU.add).then_inc(s["rms"], 1)
                    wait(pool, "rms", item, 2, 1)
                    g.tensor_tensor(row[:, p, :, C], ms[:, 1], neg_half[:, :].to_broadcast([P, NTC]), ALU.pow).then_inc(s["rms"], 1)

                def cut(item, src, hi, lo, ready, done):
                    if not active(item):
                        return
                    wait(pool, ready, item, 4)
                    wait_ring(pool, q_out[(item - 1).mod(2)], item - 1, 2, 64)
                    g.tensor_tensor(lo[:, :, :], src, hi[:, :, :].bitcast(F32), ALU.subtract).then_inc(s[done], 1)

                def step(t):
                    n, a, b = t + 1, t - 2, t - 3
                    rms(b)
                    conv_products(t + 3, 0)
                    if active(a):
                        wait(pool, "x1_ok", a, 2)
                        wait(pool, "x1T_pe", a)
                        g.tensor_tensor(x1[:, a.mod(4)], x1[:, a.mod(4)], b_bc[:, :].unsqueeze(1).to_broadcast([P, NTC, C]),
                                        ALU.add).then_inc(s["x1b_ok"], 1)
                    cut(n, q32[:, :, :], q_hi, q_lo, "q_ok", "q_cut")
                    conv_products(t + 3, 1)
                    rstd(t + 2, "ln1", 4, mv1, rs1, "rstd1")
                    conv_sum(t + 3, 0)
                    cut(n, k32[:, :, :], k_hi, k_lo, "k_ok", "k_cut")
                    conv_sum(t + 3, 1)
                    rstd(a, "lnx", 4, mvx, rsx, "rstdx")
                    if active(b):
                        p = b.mod(2)
                        wait(pool, "slot_ok", b, 7)
                        wait(pool, "id_ok", b, 2)
                        for c in range(NTC):
                            g.indirect_dma_start(out=buckets[:, :], out_offset=bass.IndirectOffsetOnAxis(ap=slot[:, p, c:c + 1], axis=0),
                                                 in_=row[:, p, c, :], in_offset=None, bounds_check=PAD - 1,
                                                 oob_is_err=False).then_inc(scat[p], 16)
                    conv_input(t + 3)
                    rstd(a, "ln2", 4, mv2, rs2, "rstd2")

                conv_products(Item(0, 0), 0)
                conv_products(Item(0, 0), 1)
                conv_sum(Item(0, 0), 0)
                conv_sum(Item(0, 0), 1)
                conv_input(Item(0, 0))
                steps(pool, step)

            @block.scalar
            def _(act):
                a_ = nc.scalar
                act.wait_ge(s["params"], 14 * 16)
                a_.activation(lm_t, lm_t, ACT.Exp).then_inc(s["setup_act"], 1)
                act.wait_ge(s["setup_act"], 1)
                a_.activation(decay_re[:, :], lm_t, ACT.Exp, scale=-1.0).then_inc(s["setup_act"], 1)
                act.wait_ge(s["setup_dve"], 8)
                a_.activation(trig[:, 0], angle, ACT.Sin).then_inc(s["setup_act"], 1)
                a_.activation(trig[:, 1], angle2, ACT.Sin).then_inc(s["setup_act"], 1)

                def copy_sums(item, pair):
                    wait(act, "pv", item, 4, 2 * pair + 2)
                    if pair == 0:
                        wait(act, "x_pe", item - 1, 2)
                    a_.activation(oT[:, 2 * pair:2 * pair + 2, :].rearrange("p g t -> p (g t)"), O_ps[:, :], ACT.Copy).then_inc(s["o_ev"], 1)

                def step(t):
                    prv, n, a, b = t - 1, t + 1, t - 2, t - 3
                    for h in range(H):
                        if active(prv):
                            wait(act, "t_pe", prv, H, h + 1)
                            if h % 4 == 0:
                                used = prv.times(4, h // 4 - 1) if h >= 8 else (prv - 1).times(4, h // 4 + 3)
                                wait_value(act, "pv", used)
                            a_.activation(probs[:, h % 8].rearrange("p k t -> p (k t)"), T_ps[h % 2][:, :], ACT.Exp,
                                          scale=DH ** -0.5).then_inc(s["exp_ok"], 1)
                        if h == 0:
                            if active(b):
                                wait(act, "x2_ok", b, 2)
                                wait(act, "rms", b - 1, 2, 1)
                                wait(act, "nx_ok", b - 1, 2)
                                for c in range(NTC):
                                    if c:
                                        wait(act, "ms_ok", b, 2, 1)
                                    a_.activation(junk[:, :], row[:, b.mod(2), c, 0:C], ACT.Square,
                                                  accum_out=ms[:, 0, c:c + 1]).then_inc(s["ms_ok"], 1)
                            if active(n):
                                wait(act, "x1T_pe", n)
                                wait(act, "q_pe", n - 1, 2)
                                a_.activation(x1T[:, :, :].rearrange("p o t -> p (o t)"), M_ps[0][:, :], ACT.Copy).then_inc(s["x1T_ok"], 1)
                        if h == 14 and active(n):
                            wait(act, "qn_pe", n)
                            wait(act, "oq_ok", n - 4, 2)
                            a_.activation(qn[:, n.mod(4)].rearrange("p c d -> p (c d)"), M_ps[2][:, :], ACT.Copy).then_inc(s["qn_ok"], 1)
                        if h == 15 and active(n + 1):
                            wait(act, "ctT_pe", n + 1)
                            wait(act, "v_pe", n, 2)
                            a_.activation(ctT[:, :, :].rearrange("p o t -> p (o t)"), M_ps[0][:, :], ACT.Copy).then_inc(s["ctT_ok"], 1)
                        if h == 2 and active(a):
                            copy_sums(a, 1)
                        if h == 3:
                            if active(n):
                                wait(act, "q_pe", n, 2)
                                wait(act, "qn_pe", n - 1)
                                wait_ring(act, q_out[(n - 1).mod(2)], n - 1, 2, 64)
                                for dst in (q_hi, q32):
                                    for c in range(NCH):
                                        a_.activation(dst[:, c], M_ps[0][:, c * TOK:(c + 1) * TOK], ACT.Relu,
                                                      bias=bq_sb[:, c:c + 1]).then_inc(s["q_ok"], 1)
                        if h == 7 and active(n):
                            wait(act, "k_pe", n, 2)
                            wait(act, "k_cut", n - 1)
                            for dst in (k_hi, k32):
                                for c in range(NCH):
                                    a_.activation(dst[:, c], M_ps[1][:, c * TOK:(c + 1) * TOK], ACT.Relu,
                                                  bias=bk_sb[:, c:c + 1]).then_inc(s["k_ok"], 1)
                        if h == 3 and active(b):
                            wait(act, "xnT_pe", b)
                            wait(act, "dist_pe", b - 1)
                            a_.activation(xnT[:, :, :].rearrange("p o t -> p (o t)"), M_ps[2][:, :], ACT.Copy).then_inc(s["xnT_ok"], 1)
                        if h == 13 and active(n):
                            wait(act, "v_pe", n, 2)
                            wait(act, "pv", n - 4, 4)
                            a_.activation(v_aug[:, n.mod(4), :, 0:H * VW].rearrange("p k (h w) -> p k h w", w=VW)[:, :, :, 0:DH],
                                          M_ps[1][:, :].rearrange("p (k h w) -> p k h w", k=NTC, w=DH), ACT.Relu).then_inc(s["v_ok"], 1)
                        if h == 4 and active(b):
                            wait(act, "xn_ok", b, 2)
                            wait(act, "pick", b - 1, 7, 2)
                            for c in range(NTC):
                                if c:
                                    wait(act, "nx_ok", b, 2, 1)
                                a_.activation(junk[:, :], xn[:, c], ACT.Square, accum_out=nx[:, c:c + 1]).then_inc(s["nx_ok"], 1)
                        if h == 11 and active(prv):
                            copy_sums(prv, 0)

                steps(act, step)

            @block.tensor
            def _(pe):
                t_ = nc.tensor
                pe.wait_ge(s["ident_ok"], 2)
                pe.wait_ge(s["params"], 14 * 16)
                pe.wait_ge(s["setup_pool"], 13)
                for c in range(NCH):
                    last = t_.transpose(M_ps[0][:, c * E:(c + 1) * E], cent[:, c * P:(c + 1) * P], ident[0:E, 0:E])
                last.then_inc(s["setup_pe"], 1)
                pe.wait_ge(s["setup_dve"], SETUP_DVE - 1)
                for c in range(NCH):
                    last = t_.matmul(M_ps[1][:, 0:E], ones_r[:, :].bitcast(F32), cent_sq[:, c, :], start=(c == 0), stop=(c == NCH - 1))
                last.then_inc(s["setup_pe"], 1)
                pe.wait_ge(s["setup_dve"], SETUP_DVE)

                def flip(dst, src):
                    for oc in range(NCH):
                        for tc in range(NTC):
                            last = t_.transpose(dst[:, oc * TOK + tc * P:oc * TOK + (tc + 1) * P], src[:, tc, oc * P:(oc + 1) * P], ident[:, :])
                    return last

                def neg_flip(item, half, b):
                    wait(pe, "max_ok", item, H, HPC * (half + 1))
                    for c in range(NTC):
                        last = t_.transpose(M_ps[b][0:HPC, c * P:(c + 1) * P], neg_max[:, item.mod(2), c, half * HPC:(half + 1) * HPC], ident[:, :])
                    last.then_inc(s["negT"], 1)

                def weighted_sum(item, grp):
                    wait(pe, "exp_ok", item, H, 4 * grp + 4)
                    if grp == 0:
                        wait(pe, "v_ok", item)
                    prev = item.times(2, grp // 2)
                    wait_value(pe, "o_ev", prev)
                    for kc in range(NTC):
                        for j in range(4):
                            h = 4 * grp + j
                            last = t_.matmul(O_ps[32 * j:32 * j + 32, (grp % 2) * TOK:(grp % 2 + 1) * TOK],
                                             v_aug[:, item.mod(4), kc, h * VW:h * VW + 32], probs[:, h % 8, kc, :],
                                             start=(kc == 0), stop=(kc == NTC - 1))
                    last.then_inc(s["pv"], 1)

                def project(dst, w, xT, oc):
                    for ic in range(NCH):
                        last = t_.matmul(dst[:, oc * TOK:(oc + 1) * TOK], w[:, ic, oc * P:(oc + 1) * P], xT[:, ic, :],
                                         start=(ic == 0), stop=(ic == NCH - 1))
                    return last


                def step(t):
                    cur, prv, n, a, b = t, t - 1, t + 1, t - 2, t - 3
                    for h in range(H):
                        if active(cur):
                            if h % HPC == 0:
                                wait(pe, stack_in[h // HPC], cur, 64)
                            prev = cur.times(H, h - 1)
                            wait_value(pe, "max_ok", prev)
                            base = 64 * cur.mod(2)
                            for c in range(NTC):
                                last = t_.matmul(S_ps[h % 2][:, c * TOK:(c + 1) * TOK], q_st[base:base + STACK, h, c * P:(c + 1) * P],
                                                 k_st[base:base + STACK, h, :], start=True, stop=True)
                            last.then_inc(s["s_pe"], 1)
                        if active(prv):
                            if h % HPC == 0:
                                wait(pe, neg_in[h // HPC], prv, 16)
                            prev = prv.times(H, h - 1)
                            wait_value(pe, "exp_ok", prev)
                            base = 64 * prv.mod(2)
                            for c in range(NTC):
                                last = t_.matmul(T_ps[h % 2][:, c * TOK:(c + 1) * TOK], k_st[base:base + AUG, h, c * P:(c + 1) * P],
                                                 q_st[base:base + AUG, h, :], start=True, stop=True)
                            last.then_inc(s["t_pe"], 1)
                        if h == 0 and active(n):
                            wait(pe, "x1_ok", n, 2)
                            wait(pe, "ctT_ok", n)
                            flip(M_ps[0], x1[:, n.mod(4)]).then_inc(s["x1T_pe"], 1)
                        if h == 1:
                            if active(prv):
                                wait(pe, "qn_ok", t)
                                neg_flip(prv, 1, 2)
                            if active(a):
                                weighted_sum(a, 3)
                        if h in (2, 3) and active(n):
                            wait(pe, "x1T_ok", n)
                            project(M_ps[0], wq_sb, x1T, h - 2).then_inc(s["q_pe"], 1)
                        if h == 3 and active(b):
                            wait(pe, "xn_ok", b, 2)
                            wait(pe, "neg_ok", prv, 4)
                            if not t.runtime:
                                wait(pe, "slot_ok", b - 1, 7)
                            flip(M_ps[2], xn).then_inc(s["xnT_pe"], 1)
                        if h in (4, 5) and active(a):
                            c = h - 4
                            wait(pe, "o_ev", a, 2)
                            if c == 0:
                                wait(pe, "v_ok", t)
                                if not t.runtime:
                                    wait(pe, "k_ok", t, 4)
                                    wait(pe, "o_ok", b, 4, 2)
                            else:
                                wait(pe, "q_ok", n, 4)
                                if not t.runtime:
                                    wait(pe, "ctT_ok", n)
                                    wait(pe, "neg_ok", prv, 4, 2)
                            for g4 in range(H // 4):
                                last = t_.transpose(M_ps[1 - c][:, g4 * P:(g4 + 1) * P], oT[:, g4, c * P:(c + 1) * P], ident[:, :])
                            last.then_inc(s["x_pe"], 1)
                        if h == 5 and active(b):
                            wait(pe, "xnT_ok", b)
                            for c in range(NTC):
                                for oc in range(NCH):
                                    last = t_.matmul(M_ps[2][:, c * E:(c + 1) * E], xnT[:, oc, c * P:(c + 1) * P], centT[:, oc, :],
                                                     start=(oc == 0), stop=(oc == NCH - 1))
                            last.then_inc(s["dist_pe"], 1)
                        if h == 8 and active(prv):
                            weighted_sum(prv, 0)
                        if h in (6, 7) and active(n):
                            wait(pe, "ctT_ok", n)
                            wait(pe, "o_ok", a, 4, 2)
                            wait(pe, "v_ok", t)
                            project(M_ps[1], wk_sb, ctT, h - 6).then_inc(s["k_pe"], 1)
                        if h == 10 and active(prv):
                            weighted_sum(prv, 1)
                        if h == 9:
                            if active(b):
                                wait(pe, "pick", b, 7)
                                r0, r1, tot = 64, 64 + E, 64 + 2 * E
                                t_.matmul(M_ps[2][:, r0:r0 + E], before[:, :], onehot_bf[:, 0, :], start=True, stop=True)
                                t_.matmul(M_ps[2][:, r1:r1 + E], before[:, :], onehot_bf[:, 1, :], start=True, stop=False)
                                t_.matmul(M_ps[2][:, r1:r1 + E], ones_bf[:, :], onehot_bf[:, 0, :], start=False, stop=True)
                                t_.matmul(M_ps[2][:, tot:tot + E], ones_bf[:, :], onehot_bf[:, 0, :], start=True, stop=False)
                                t_.matmul(M_ps[2][:, tot:tot + E], ones_bf[:, :], onehot_bf[:, 1, :], start=False, stop=True)\
                                    .then_inc(s["rank_pe"], 1)
                            if active(cur):
                                wait(pe, "o_ok", a, 4)
                                if not t.runtime:
                                    wait(pe, "q_ok", n, 4)
                                    wait(pe, "ctT_ok", n)
                                neg_flip(cur, 0, 0)
                        if h in (11, 12) and active(n):
                            c = h - 11
                            wait(pe, "k_ok", n, 4)
                            if not t.runtime:
                                wait(pe, "o_ok", a, 4, 2)
                            for ic in range(NCH):
                                t_.matmul(M_ps[1][:, c * C:(c + 1) * C], ctT[:, ic, c * P:(c + 1) * P], wv_sb[:, ic, :],
                                          start=(ic == 0), stop=False)
                            for w in range(2):
                                last = t_.matmul(M_ps[1][:, c * C:(c + 1) * C], ones_r[0:1, :], bv_cut[:, w, :],
                                                 start=False, stop=(w == 1))
                            last.then_inc(s["v_pe"], 1)
                        if h == 14 and active(n):
                            wait(pe, "slot_ok", b, 7)
                            wait(pe, "q_ok", n, 4)
                            if not t.runtime:
                                wait(pe, "neg_ok", prv, 4)
                                wait(pe, "qn_ok", t)
                            for c in range(NTC):
                                for oc in range(NCH):
                                    last = t_.transpose(M_ps[2][:, c * C + oc * P:c * C + (oc + 1) * P],
                                                        q32[:, oc, c * P:(c + 1) * P], ident[:, :])
                            last.then_inc(s["qn_pe"], 1)
                        if h == 13 and active(prv):
                            weighted_sum(prv, 2)
                        if h == 15 and active(n + 1):
                            nn = n + 1
                            wait_ring(pe, ctx_in_s[nn.mod(2)], nn, 2, 16)
                            wait(pe, "neg_ok", cur, 4, 2)
                            if not t.runtime:
                                wait(pe, "q_ok", n, 4)
                                wait(pe, "o_ok", a, 4)
                            flip(M_ps[0], ct[:, nn.mod(2)]).then_inc(s["ctT_pe"], 1)

                steps(pe, step)

            @block.vector
            def _(dve):
                v = nc.vector
                done = [0]

                def setup(ins):
                    done[0] += 1
                    ins.then_inc(s["setup_dve"], 1)
                    dve.wait_ge(s["setup_dve"], done[0])

                dve.wait_ge(s["params"], 14 * 16)
                dve.wait_ge(s["setup_pool"], 13)
                setup(v.tensor_scalar(turns, th_t, 1 / (2 * np.pi), None, ALU.mult))
                setup(v.tensor_scalar(turns, turns, ROUND, -ROUND, ALU.add, ALU.add))
                setup(v.scalar_tensor_tensor(angle, turns, -TWO_PI_A, th_t, ALU.mult, ALU.add))
                setup(v.scalar_tensor_tensor(angle, turns, -TWO_PI_B, angle, ALU.mult, ALU.add))
                setup(v.scalar_tensor_tensor(angle, turns, -TWO_PI_C, angle, ALU.mult, ALU.add))
                setup(v.tensor_scalar(angle, angle, 3.1415925, -3.1415925, ALU.min, ALU.max))
                setup(v.scalar_tensor_tensor(angle2, angle, -1.0, angle, ALU.mult, ALU.max))
                setup(v.tensor_scalar(angle2, angle2, -1.0, np.pi / 2, ALU.mult, ALU.add))
                setup(v.tensor_copy(bv_cut[:, 0], bv_row))
                setup(v.tensor_tensor(bv_cut[:, 1], bv_row, bv_cut[:, 0].bitcast(F32), ALU.subtract))
                dve.wait_ge(s["setup_act"], 4)
                setup(v.tensor_tensor(decay_im[:, :], decay_re[:, :], trig[:, 0], ALU.mult))
                setup(v.tensor_tensor(decay_re[:, :], decay_re[:, :], trig[:, 1], ALU.mult))
                dve.wait_ge(s["setup_pe"], 1)
                ctv = centT[:, :, :].rearrange("p o e -> p (o e)")
                setup(v.tensor_scalar(ctv, M_ps[0][:, 0:NCH * E], -2.0, None, ALU.mult))
                setup(v.scalar_tensor_tensor(cent_sq[:, :, :].rearrange("p o e -> p (o e)"), ctv, 0.25, ctv, ALU.mult, ALU.mult))
                dve.wait_ge(s["setup_pe"], 2)
                setup(v.tensor_copy(cent_norm[:, :], M_ps[1][:, 0:E]))
                assert done[0] == SETUP_DVE

                def stats(item, src, st, mv, name):
                    for c in range(NTC):
                        v.bn_stats(st[:, c], src[:, c]).then_inc(s[name], 1)
                    wait(dve, name, item, 4, 2)
                    dve.sem_inc(s["dve_waits"], 1)
                    for c in range(NTC):
                        v.bn_aggr(mv[:, c], st[:, c]).then_inc(s[name], 1)

                def step(t):
                    cur, prv, nn, a, b = t, t - 1, t + 2, t - 2, t - 3
                    for h in range(H):
                        if active(cur):
                            wait(dve, "s_pe", cur, H, h + 1)
                            if h == 0:
                                wait(dve, "negT", cur - 2, 2)
                            v.tensor_reduce(neg_max[:, cur.mod(2), :, h], S_ps[h % 2][:, :].rearrange("p (c t) -> p c t", c=NTC),
                                            AX.X, ALU.max, negate=True).then_inc(s["max_ok"], 1)
                        if h == 0 and active(nn):
                            wait(dve, "x1_ok", nn - 1, 2)
                            wait(dve, "conv", nn, 5)
                            wait_ring(dve, x_in[nn.mod(2)], nn, 2, 16)
                            v.scalar_tensor_tensor(u[:, :, :], state[:, 0], 1.0, xt[:, nn.mod(2)], ALU.add, ALU.mult).then_inc(s["u_ok"], 1)
                        if h == 1 and active(prv):
                            neg_cut(prv, 1, 2)
                        if h == 2 and active(b):
                            wait(dve, "rms", b, 2)
                            wait(dve, "nx_ok", b - 1, 2)
                            wait(dve, "xnT_pe", b - 1)
                            for c in range(NTC):
                                v.scalar_tensor_tensor(xn[:, c], row[:, b.mod(2), c, 0:C], row[:, b.mod(2), c, C:C + 1], scale_bc[:, :],
                                                       ALU.mult, ALU.mult).then_inc(s["xn_ok"], 1)
                        if h == 3 and active(nn):
                            wait(dve, "u_ok", nn)
                            wait(dve, "rstd1", nn - 1, 2)
                            stats(nn, u, st1, mv1, "ln1")
                        if h in (5, 7) and active(a):
                            c = (h - 5) // 2
                            src = M_ps[1 - c][:, :].rearrange("p (h w) -> p h w", w=32)
                            wait(dve, "x_pe", a, 2, c + 1)
                            v.reciprocal(rden[:, c], src[:, :, DH]).then_inc(s["o_ok"], 1)
                            wait(dve, "o_ok", a, 4, 2 * c + 1)
                            v.tensor_tensor(o[:, c].rearrange("p (h w) -> p h w", w=DH), src[:, :, 0:DH],
                                            rden[:, c].unsqueeze(2).to_broadcast([P, H, DH]), ALU.mult).then_inc(s["o_ok"], 1)
                        if h == 6 and active(b):
                            pick(b)
                        if h == 8 and active(a):
                            wait(dve, "qn_ok", a)
                            wait(dve, "o_ok", a, 4)
                            for c in range(NTC):
                                v.tensor_tensor(oq[:, c].rearrange("p (o h w) -> p o h w", o=NCH, h=HPC),
                                                o[:, c].rearrange("p (o h w) -> p o h w", o=NCH, h=HPC),
                                                qn[:, a.mod(4), c].rearrange("p (o w h) -> p o h w", o=NCH, h=HPC),
                                                ALU.add).then_inc(s["oq_ok"], 1)
                        if h == 9 and active(a):
                            wait(dve, "oq_ok", a, 2)
                            stats(a, oq, stx, mvx, "lnx")
                        if h == 10 and active(cur):
                            neg_cut(cur, 0, 0)
                        if h == 11 and active(b):
                            slots(b)
                        if h == 12 and active(a):
                            wait(dve, "rstdx", a, 2)
                            wait(dve, "x1b_ok", a)
                            for c in range(NTC):
                                v.scalar_tensor_tensor(y1[:, c], oq[:, c], mvx[:, c, 0:1], g_bc[:, :],
                                                       ALU.subtract, ALU.mult).then_inc(s["y_ok"], 1)
                            for c in range(NTC):
                                wait(dve, "y_ok", a, 4, c + 1)
                                v.scalar_tensor_tensor(y2[:, c], y1[:, c], rsx[:, 1, c:c + 1], x1[:, a.mod(4), c],
                                                       ALU.mult, ALU.add).then_inc(s["y_ok"], 1)
                        if h == 14 and active(a):
                            wait(dve, "y_ok", a, 4)
                            stats(a, y2, st2, mv2, "ln2")
                        if h == 13 and active(nn):
                            wait(dve, "rstd1", nn, 2)
                            wait(dve, "y_ok", nn - 4, 4)
                            for c in range(NTC):
                                v.tensor_scalar(x1[:, nn.mod(4), c], u[:, c], mv1[:, c, 0:1], rs1[:, 1, c:c + 1],
                                                ALU.subtract, ALU.mult).then_inc(s["x1_ok"], 1)
                        if h == 15 and active(a):
                            wait(dve, "rstd2", a, 2)
                            wait_ring(dve, scat[a.mod(2)], a - 2, 2, 16 * NTC)
                            for c in range(NTC):
                                v.tensor_scalar(row[:, a.mod(2), c, 0:C], y2[:, c], mv2[:, c, 0:1], rs2[:, 1, c:c + 1],
                                                ALU.subtract, ALU.mult).then_inc(s["x2_ok"], 1)
                            wait(dve, "id_ok", a - 1, 2)
                            v.tensor_copy(row[:, a.mod(2), :, C + 1].bitcast(I32), ids[:, :]).then_inc(s["id_ok"], 1)
                            v.tensor_scalar(ids[:, :], ids[:, :], float(TOK), None, ALU.add).then_inc(s["id_ok"], 1)

                def neg_cut(item, half, b):
                    wait(dve, "negT", item, 2, half + 1)
                    wait_value(dve, "neg_out", item.times(32, 16 * half))
                    src = M_ps[b][0:HPC, 0:TOK]
                    v.tensor_copy(nm_pieces[:, 0], src).then_inc(s["neg_ok"], 1)
                    wait(dve, "neg_ok", item, 4, 2 * half + 1)
                    v.tensor_tensor(nm_pieces[:, 1], src, nm_pieces[:, 0].bitcast(F32), ALU.subtract).then_inc(s["neg_ok"], 1)

                def pick(b):
                    wait(dve, "nx_ok", b, 2)
                    wait(dve, "dist_pe", b)
                    for c in range(NTC):
                        v.tensor_scalar(dist[:, 0, c], cent_norm[:, :], nx[:, c:c + 1], None, ALU.add).then_inc(s["pick"], 1)
                    wait(dve, "pick", b, 7, 2)
                    v.tensor_tensor(dist[:, 1], dist[:, 0], M_ps[2][:, 0:NTC * E].rearrange("p (c e) -> p c e", c=NTC), ALU.add).then_inc(s["pick"], 1)
                    wait(dve, "pick", b, 7, 3)
                    v.tensor_reduce(least[:, :], dist[:, 1], AX.X, ALU.min).then_inc(s["pick"], 1)
                    wait(dve, "pick", b, 7, 4)
                    v.tensor_tensor(cand[:, 0], dist[:, 1], least[:, :].unsqueeze(2).to_broadcast([P, NTC, E]), ALU.is_gt).then_inc(s["pick"], 1)
                    wait(dve, "pick", b, 7, 5)
                    v.scalar_tensor_tensor(cand[:, 1], cand[:, 0], float(E), expert_no[:, :, :], ALU.mult, ALU.add).then_inc(s["pick"], 1)
                    wait(dve, "pick", b, 7, 6)
                    v.tensor_reduce(choice[:, :], cand[:, 1], AX.X, ALU.min).then_inc(s["slot_ok"], 1)
                    wait(dve, "slot_ok", b, 7, 1)
                    ch = choice[:, :].unsqueeze(2).to_broadcast([P, NTC, E])
                    v.tensor_tensor(onehot[:, :, :], expert_no[:, :, :], ch, ALU.is_equal).then_inc(s["slot_ok"], 1)
                    v.tensor_tensor(onehot_bf[:, :, :], expert_no[:, :, :], ch, ALU.is_equal).then_inc(s["pick"], 1)

                def slots(b):
                    wait(dve, "rank_pe", b)
                    wait(dve, "slot_ok", b, 7, 2)
                    wait(dve, "slot_ok", b - 1, 7)
                    v.tensor_tensor(place[:, 0], M_ps[2][:, 64:64 + NTC * E].rearrange("p (c e) -> p c e", c=NTC),
                                    filled[:, :].unsqueeze(1).to_broadcast([P, NTC, E]), ALU.add).then_inc(s["slot_ok"], 1)
                    wait(dve, "slot_ok", b, 7, 3)
                    v.tensor_tensor(place[:, 1], place[:, 0], onehot[:, :, :], ALU.mult).then_inc(s["slot_ok"], 1)
                    v.tensor_tensor(filled[:, :], filled[:, :], M_ps[2][:, 64 + NTC * E:64 + (NTC + 1) * E], ALU.add).then_inc(s["slot_ok"], 1)
                    wait(dve, "slot_ok", b, 7, 4)
                    v.tensor_reduce(slot_f[:, :], place[:, 1], AX.X, ALU.add).then_inc(s["slot_ok"], 1)
                    wait(dve, "slot_ok", b, 7, 6)
                    wait_ring(dve, scat[b.mod(2)], b - 2, 2, 16 * NTC)
                    v.tensor_copy(slot[:, b.mod(2)], slot_f[:, :]).then_inc(s["slot_ok"], 1)

                steps(dve, step)

        def sb2(name, shape, dt=F32):
            return stack.enter_context(nc.sbuf_tensor(name, shape, dt))

        dn_sb = sb2("dn_sb", [P, E * HCH * C])
        base = sb2("base", [1, E])
        count = sb2("count", [1, E])
        tiles = sb2("tiles", [1, E])
        ends = sb2("ends", [1, E])
        starts = sb2("starts", [1, E])
        first = sb2("first", [1, E])
        eno = sb2("eno", [1, E])
        tno = sb2("tno", [1, NTILES])
        tno128 = sb2("tno128", [1, NTILES])
        own = sb2("own", [1, 3, NTILES, E])
        picked = sb2("picked", [1, 2, NTILES, E])
        owned = sb2("owned", [1, NTILES])
        row_f = sb2("row_f", [1, 2, NTILES])
        eno_f = sb2("eno_f", [1, NTILES])
        RING = 4
        xr = sb2("xr", [P, RING, ROWW])
        xs = sb2("xs", [P, 2, C])
        xsT = sb2("xsT", [P, 2, NCH, P])
        gate = sb2("gate", [P, 2, HID])
        gated = sb2("gated", [P, 2, HID])
        gT = sb2("gT", [P, 2, HCH, P])
        y = sb2("y", [P, 2, C])
        st3 = sb2("st3", [P, 6])
        mv3 = sb2("mv3", [P, 2])
        rs3 = sb2("rs3", [P, 2])
        res = sb2("res", [P, 2, C])
        token = sb2("token", [P, 2], U32)
        XT_ps, A_ps, G_ps, GT_ps, Y_ps = (bank(n) for n in ("XT", "A", "G", "GT", "Y"))
        names2 = """down_in table_pool table tails tile0 tile1 tile2 tile3 xs_ok xsT_pe xsT_ok g_pe a_pe gate_ok gated_ok gT_pe gT_act
            y_pe y2_ok ln3 rstd3 res_ok token_ok sent0 sent1 pool_waits sp_waits dve_waits"""
        z = {n: sem("z_" + n) for n in names2.split()}
        tile_in = [z[f"tile{r}"] for r in range(RING)]
        sent = [z["sent0"], z["sent1"]]
        out_rows = out.rearrange("n t d -> (n t) d")

        def const_wait(eng):
            if eng.engine in (mybir.EngineType.Pool, mybir.EngineType.SP):
                eng.sem_inc(z["pool_waits" if eng.engine == mybir.EngineType.Pool else "sp_waits"], 1)

        def wait_value(eng, name, v):
            sm = z[name] if isinstance(name, str) else name
            if isinstance(v, int):
                if v > 0:
                    eng.wait_ge(sm, v)
            else:
                eng.wait_ge(sm, v)
                const_wait(eng)

        def wait(eng, name, item, per=1, j=None):
            wait_value(eng, name, item.times(per, per if j is None else j))

        def wait_ring(eng, sm, item, ring, per):
            wait_value(eng, sm, item.uses(ring) * per)

        def steps(eng, body):
            lead = 4
            loops = (NTILES - 2 - lead) // 4
            for n in range(-1, lead):
                body(Item(0, n))
            with eng.Fori(0, loops) as i:
                for k in range(4):
                    body(Item(i, lead + k))
            for n in range(lead + 4 * loops, NTILES + 2):
                body(Item(0, n))

        def active(item):
            return item.within(0, NTILES)

        with nc.Block() as block:
            @block.sync
            def _(sp):
                for e in range(E):
                    dst = dn_sb[:, e * HCH * C:(e + 1) * HCH * C].rearrange("p (o n) -> p o n", o=HCH)
                    sp.dma_start(dst, down_w[e].rearrange("(o p) n -> p o n", p=P)).then_inc(z["down_in"], 16)
                sp.wait_ge(z["table_pool"], 4)
                sp.wait_ge(z["table"], TABLE)
                for e in range(E):
                    r = sp.value_load(tail_row[0:1, e:e + 1], min_val=0, max_val=PAD - P)
                    sp.dma_start(buckets[bass.ds(r, P), :], pad_row[:, :]).then_inc(z["tails"], 16)
                sp.wait_ge(z["tails"], 16 * E)

                def step(t):
                    n = t + 2
                    if active(n):
                        if n.runtime or n.k >= RING:
                            wait(sp, "token_ok", n - RING)
                        r = sp.value_load(tile_row[0:1, bass.ds(n.times(1), 1)], min_val=0, max_val=PAD)
                        sp.dma_start(xr[:, n.mod(RING), :], buckets[bass.ds(r, P), :]).then_inc(tile_in[n.mod(RING)], 16)

                step(Item(0, -2))
                steps(sp, step)
                for p in range(2):
                    sp.wait_ge(sent[p], 16 * ((NTILES + 1 - p) // 2))

            @block.gpsimd
            def _(pool):
                g = nc.gpsimd
                kw = dict(allow_small_or_imprecise_dtypes=True, channel_multiplier=0, base=0)
                g.iota(base[:, :], pattern=[[CAP, E]], **kw).then_inc(z["table_pool"], 1)
                g.iota(eno[:, :], pattern=[[1, E]], **kw).then_inc(z["table_pool"], 1)
                g.iota(tno[:, :], pattern=[[1, NTILES]], **kw).then_inc(z["table_pool"], 1)
                g.iota(tno128[:, :], pattern=[[P, NTILES]], **kw).then_inc(z["table_pool"], 1)
                pool.wait_ge(z["table_pool"], 4)

                def step(t):
                    m, f = t - 1, t - 2
                    if active(f):
                        wait(pool, "res_ok", f)
                        wait(pool, "token_ok", f)
                        g.indirect_dma_start(out=out_rows, out_offset=bass.IndirectOffsetOnAxis(ap=token[:, f.mod(2):f.mod(2) + 1], axis=0),
                                             in_=res[:, f.mod(2), :], in_offset=None, bounds_check=SEQ * TOK - 1,
                                             oob_is_err=False).then_inc(sent[f.mod(2)], 16)
                    if active(m):
                        wait(pool, "ln3", m, 2)
                        g.tensor_scalar(rs3[:, 0:1], mv3[:, 1:2], LN_EPS, None, ALU.add).then_inc(z["rstd3"], 1)
                        wait(pool, "rstd3", m, 2, 1)
                        g.tensor_tensor(rs3[:, 1:2], rs3[:, 0:1], neg_half[:, :], ALU.pow).then_inc(z["rstd3"], 1)

                steps(pool, step)

            @block.scalar
            def _(act):
                a_ = nc.scalar

                def step(t):
                    m, n = t - 1, t + 1
                    if active(t):
                        wait(act, "g_pe", t)
                        wait(act, "gated_ok", t - 2)
                        a_.activation(gate[:, t.mod(2)], G_ps[:, :], ACT.Silu).then_inc(z["gate_ok"], 1)
                    if active(m):
                        wait(act, "gT_pe", m)
                        wait(act, "y_pe", m - 2)
                        a_.activation(gT[:, m.mod(2)].rearrange("p o t -> p (o t)"), GT_ps[:, :], ACT.Copy).then_inc(z["gT_act"], 1)
                    if active(n):
                        wait(act, "xsT_pe", n)
                        wait(act, "a_pe", n - 2)
                        a_.activation(xsT[:, n.mod(2)].rearrange("p o t -> p (o t)"), XT_ps[:, 0:NCH * P], ACT.Copy).then_inc(z["xsT_ok"], 1)

                steps(act, step)

            @block.tensor
            def _(pe):
                t_ = nc.tensor
                pe.wait_ge(z["table"], TABLE)
                pe.wait_ge(z["down_in"], 16 * E)

                def up(t, off, half, ps, name):
                    for ic in range(NCH):
                        last = t_.matmul(ps[:, :], xsT[:, t.mod(2), ic, :],
                                         up_sb[:, bass.ds(off + (ic * 2 * HID + half * HID), HID)],
                                         start=(ic == 0), stop=(ic == NCH - 1))
                    last.then_inc(z[name], 1)

                def step(t):
                    m, n = t - 1, t + 1
                    if active(t):
                        off = pe.value_load(tile_up[0:1, bass.ds(t.times(1), 1)], min_val=0, max_val=(E - 1) * NCH * 2 * HID)
                        wait(pe, "xsT_ok", t)
                        wait(pe, "gate_ok", m)
                        up(t, off, 1, G_ps, "g_pe")
                    if active(m):
                        wait(pe, "gated_ok", m)
                        wait(pe, "gT_act", m - 1)
                        for c in range(HCH):
                            last = t_.transpose(GT_ps[:, c * P:(c + 1) * P], gated[:, m.mod(2), c * P:(c + 1) * P], ident[:, :])
                        last.then_inc(z["gT_pe"], 1)
                    if active(n):
                        wait(pe, "xs_ok", n)
                        wait(pe, "xsT_ok", t)
                        for c in range(NCH):
                            last = t_.transpose(XT_ps[:, c * P:(c + 1) * P], xs[:, n.mod(2), c * P:(c + 1) * P], ident[:, :])
                        last.then_inc(z["xsT_pe"], 1)
                    if active(t):
                        wait(pe, "gated_ok", m)
                        up(t, off, 0, A_ps, "a_pe")
                    if active(m):
                        off = pe.value_load(tile_dn[0:1, bass.ds(m.times(1), 1)], min_val=0, max_val=(E - 1) * HCH * C)
                        wait(pe, "gT_act", m)
                        wait(pe, "y2_ok", m - 1)
                        for c in range(HCH):
                            last = t_.matmul(Y_ps[:, 0:C], gT[:, m.mod(2), c, :], dn_sb[:, bass.ds(off + c * C, C)],
                                             start=(c == 0), stop=(c == HCH - 1))
                        last.then_inc(z["y_pe"], 1)

                steps(pe, step)

            @block.vector
            def _(dve):
                v = nc.vector
                done = [0]

                def setup(ins):
                    done[0] += 1
                    ins.then_inc(z["table"], 1)
                    dve.wait_ge(z["table"], done[0])

                dve.wait_ge(z["table_pool"], 4)
                setup(v.tensor_tensor(count[:, :], filled[0:1, :], base[:, :], ALU.subtract))
                setup(v.tensor_copy(tail_row[:, :], filled[0:1, :]))
                setup(v.tensor_scalar(tiles[:, :], count[:, :], float(P - 1), 1.0 / P, ALU.add, ALU.mult))
                setup(v.tensor_scalar(tiles[:, :], tiles[:, :], 0.5 / P - 0.5, None, ALU.add))
                setup(v.tensor_scalar(tiles[:, :], tiles[:, :], ROUND, -ROUND, ALU.add, ALU.add))
                setup(v.tensor_copy(ends[:, 0:1], tiles[:, 0:1]))
                for e in range(1, E):
                    setup(v.tensor_tensor(ends[:, e:e + 1], ends[:, e - 1:e], tiles[:, e:e + 1], ALU.add))
                setup(v.tensor_tensor(starts[:, :], ends[:, :], tiles[:, :], ALU.subtract))
                setup(v.scalar_tensor_tensor(first[:, :], starts[:, :], -float(P), base[:, :], ALU.mult, ALU.add))
                every = [1, NTILES, E]
                tb = tno[:, :].unsqueeze(2).to_broadcast(every)
                setup(v.tensor_tensor(own[:, 0], tb, starts[:, :].unsqueeze(1).to_broadcast(every), ALU.is_ge))
                setup(v.tensor_tensor(own[:, 1], tb, ends[:, :].unsqueeze(1).to_broadcast(every), ALU.is_lt))
                setup(v.tensor_tensor(own[:, 2], own[:, 0], own[:, 1], ALU.mult))
                setup(v.tensor_tensor(picked[:, 0], own[:, 2], first[:, :].unsqueeze(1).to_broadcast(every), ALU.mult))
                setup(v.tensor_tensor(picked[:, 1], own[:, 2], eno[:, :].unsqueeze(1).to_broadcast(every), ALU.mult))
                setup(v.tensor_reduce(owned[:, :], own[:, 2], AX.X, ALU.add))
                setup(v.tensor_reduce(row_f[:, 0], picked[:, 0], AX.X, ALU.add))
                setup(v.tensor_reduce(eno_f[:, :], picked[:, 1], AX.X, ALU.add))
                setup(v.scalar_tensor_tensor(row_f[:, 1], tno128[:, :], -float(PAD), row_f[:, 0], ALU.add, ALU.add))
                setup(v.tensor_tensor(row_f[:, 0], row_f[:, 1], owned[:, :], ALU.mult))
                setup(v.tensor_scalar(tile_row[:, :], row_f[:, 0], float(PAD), None, ALU.add))
                setup(v.tensor_scalar(tile_up[:, :], eno_f[:, :], float(NCH * 2 * HID), None, ALU.mult))
                setup(v.tensor_scalar(tile_dn[:, :], eno_f[:, :], float(HCH * C), None, ALU.mult))
                assert done[0] == TABLE

                def step(t):
                    m, n, f = t - 1, t + 1, t - 2
                    if active(n):
                        wait_ring(dve, tile_in[n.mod(RING)], n, RING, 16)
                        wait(dve, "xsT_pe", n - 2)
                        v.scalar_tensor_tensor(xs[:, n.mod(2)], xr[:, n.mod(RING), 0:C], xr[:, n.mod(RING), C:C + 1], scale_bc[:, :],
                                               ALU.mult, ALU.mult).then_inc(z["xs_ok"], 1)
                    if active(f):
                        wait(dve, "rstd3", f, 2)
                        wait_ring(dve, sent[f.mod(2)], f - 2, 2, 16)
                        v.tensor_scalar(res[:, f.mod(2)], y[:, f.mod(2)], mv3[:, 0:1], rs3[:, 1:2],
                                        ALU.subtract, ALU.mult).then_inc(z["res_ok"], 1)
                    if active(t):
                        wait(dve, "gate_ok", t)
                        wait(dve, "a_pe", t)
                        wait(dve, "gT_pe", t - 2)
                        v.tensor_tensor(gated[:, t.mod(2)], A_ps[:, :], gate[:, t.mod(2)], ALU.mult).then_inc(z["gated_ok"], 1)
                    if active(m):
                        wait(dve, "y_pe", m)
                        v.scalar_tensor_tensor(y[:, m.mod(2)], xr[:, m.mod(RING), 0:C], 2.0, Y_ps[:, 0:C],
                                               ALU.mult, ALU.add).then_inc(z["y2_ok"], 1)
                        wait(dve, "y2_ok", m)
                        v.bn_stats(st3[:, :], y[:, m.mod(2)]).then_inc(z["ln3"], 1)
                        wait_ring(dve, sent[m.mod(2)], m - 2, 2, 16)
                        v.tensor_copy(token[:, m.mod(2):m.mod(2) + 1], xr[:, m.mod(RING), C + 1:C + 2].bitcast(U32)).then_inc(z["token_ok"], 1)
                        wait(dve, "ln3", m, 2, 1)
                        dve.sem_inc(z["dve_waits"], 1)
                        v.bn_aggr(mv3[:, :], st3[:, :]).then_inc(z["ln3"], 1)

                steps(dve, step)


TABLE = 28


_INS = ["x", "ctx_1024", "L0_attn_lmlg", "L0_attn_theta", "L0_attn_last_conv_init", "L0_xattn_Wq", "L0_xattn_bq",
        "L0_xattn_Wk", "L0_xattn_bk", "L0_xattn_Wv", "L0_xattn_bv", "L0_xattn_ln_g", "L0_xattn_ln_b",
        "L0_ffn_scale", "L0_ffn_centroids", "L0_ffn_up_w", "L0_ffn_down_w"]
_BY_CHANNEL = {"L0_xattn_Wq", "L0_xattn_bq", "L0_xattn_Wk", "L0_xattn_bk"}


def kernel(**inputs):
    import concourse.bacc as _bacc
    from concourse.bass_utils import run_bass_kernel_spmd as _run

    nc = _bacc.Bacc("TRN2", target_bir_lowering=False, num_devices=1)
    arrays, args = {}, []
    for name in _INS:
        a = np.asarray(inputs[name])
        if name in _BY_CHANNEL:
            lead = a.shape[:-1]
            a = a.reshape(*lead, NCH, HPC, DH).swapaxes(-1, -2).reshape(*lead, C)
        a = np.ascontiguousarray(a)
        arrays[f"in_{name}"] = a
        args.append(nc.dram_tensor(f"in_{name}", a.shape, mybir.dt.from_np(a.dtype), kind="ExternalInput").ap())
    args.append(nc.dram_tensor("out_0", (SEQ, TOK, C), F32, kind="ExternalOutput").ap())
    build(nc, *args)
    r = _run(nc, [arrays], core_ids=[0])
    return r.results[0]["out_0"]
```

```python
import numpy as np
import concourse.bass as bass
from concourse import mybir
from contextlib import ExitStack

F32 = mybir.dt.float32
F32R = mybir.dt.float32r
BF16 = mybir.dt.bfloat16
U32 = mybir.dt.uint32
I32 = mybir.dt.int32
ALU = mybir.AluOpType
ACT = mybir.ActivationFunctionType
AX = mybir.AxisListType

P = 128
SEQ, TOK, C = 32, 256, 256
NCH = C // P
NTC = TOK // P
H = 16
DH = C // H
HPC = H // NCH
E, HID = 8, 512
HCH = HID // P
UPW, DNW = NCH * 2 * HID, HCH * C
LN_EPS, RMS_EPS = 1e-5, 1e-6
ROWW = C + 2
CAP = SEQ * TOK + P
PAD = E * CAP
NTILES = SEQ * TOK // P + E - 1
SETUP_DVE = 15
UP_STEPS = (-2, -1, 0, 1, 2, 3, SEQ - 1, SEQ)
UNROLL = 8
NOID = 1 << 20
STACK = 3 * DH
AUG = STACK + 2
TWO_PI_A = 6.28125
TWO_PI_B = float(np.float32(2 * np.pi - TWO_PI_A))
TWO_PI_C = float(np.float32(2 * np.pi - TWO_PI_A - TWO_PI_B))
ROUND = 1.5 * 2 ** 23


class Item:

    def __init__(self, i, k):
        self.i, self.k = i, k
        self.runtime = not isinstance(i, int)

    def __add__(self, d):
        return Item(self.i, self.k + d)

    def __sub__(self, d):
        return Item(self.i, self.k - d)

    def mod(self, m):
        return self.k % m

    def times(self, c, j=0):
        return self.i * (UNROLL * c) + (self.k * c + j) if self.runtime else self.k * c + j

    def uses(self, m):
        return self.i * (UNROLL // m) + (self.k // m + 1) if self.runtime else self.k // m + 1

    def within(self, lo, hi):
        return self.runtime or lo <= self.k < hi


def build(nc, x, ctx_in, lmlg, theta, last_conv, Wq, bq, Wk, bk, Wv, bv, ln_g, ln_b, ffn_scale, centroids, up_w, down_w, out):
    stack = ExitStack()
    with stack:
        def sb(name, shape, dt=F32):
            return stack.enter_context(nc.sbuf_tensor(name, shape, dt))

        def bank(name, scope=stack):
            return scope.enter_context(nc.psum_tensor(name, [P, 512], F32))

        def sem(name):
            return stack.enter_context(nc.semaphore(name))

        q_dram = nc.dram_tensor("q_pieces", (2, NCH, 2, P, TOK), F32)
        k_dram = nc.dram_tensor("k_pieces", (2, NCH, 2, P, TOK), F32)
        m_dram = nc.dram_tensor("neg_max", (2, 2, 2, HPC, TOK), F32)
        buckets = nc.dram_tensor("buckets", (PAD + P, ROWW), F32)

        up_sb = sb("up_sb", [P, E * UPW], F32R)
        ident = sb("ident", [P, P])
        scale_bc = sb("scale_bc", [P, C])
        neg_half = sb("neg_half", [P, 1])
        filled = sb("filled", [P, E])
        pad_row = sb("pad_row", [P, ROWW])
        tile_row = sb("tile_row", [1, NTILES], I32)
        tile_up = sb("tile_up", [1, NTILES], I32)
        tile_dn = sb("tile_dn", [1, NTILES], I32)
        tail_row = sb("tail_row", [1, E], I32)

        phase1 = ExitStack()

        def sb1(name, shape, dt=F32):
            return phase1.enter_context(nc.sbuf_tensor(name, shape, dt))

        with phase1:
            wq_sb = sb1("wq_sb", [P, NCH, C])
            wk_sb = sb1("wk_sb", [P, NCH, C])
            wv_sb = sb1("wv_sb", [P, NCH, C])
            bq_sb = sb1("bq_sb", [P, NCH])
            bk_sb = sb1("bk_sb", [P, NCH])
            bv_cut = sb1("bv_cut", [1, 2, C], F32R)
            g_bc = sb1("g_bc", [P, C])
            b_bc = sb1("b_bc", [P, C])
            decay_re = sb1("decay_re", [P, C])
            decay_im = sb1("decay_im", [P, C])
            centT = sb1("centT", [P, NCH, E])
            cent_sq = sb1("cent_sq", [P, NCH, E])
            cent_norm = sb1("cent_norm", [P, E])
            ones_r = sb1("ones_r", [P, P], F32R)
            ones_bf = sb1("ones_bf", [P, P], BF16)
            before = sb1("before", [P, P], BF16)
            expert_no = sb1("expert_no", [P, NTC, E])
            state = sb1("state", [P, 2, NTC, C])
            by_im = sb1("by_im", [P, 2, NTC, C])
            xt = sb1("xt", [P, 2, NTC, C])
            ct = sb1("ct", [P, 2, NTC, C])
            u = sb1("u", [P, NTC, C])
            st1 = sb1("st1", [P, NTC, 6])
            mv1 = sb1("mv1", [P, NTC, 2])
            rs1 = sb1("rs1", [P, 2, NTC])
            x1 = sb1("x1", [P, 4, NTC, C])
            x1T = sb1("x1T", [P, NCH, TOK])
            ctT = sb1("ctT", [P, NCH, TOK])
            q32 = sb1("q32", [P, NCH, TOK])
            qn = sb1("qn", [P, 4, NTC, C])
            k32 = sb1("k32", [P, NCH, TOK])
            q_hi = sb1("q_hi", [P, NCH, TOK], F32R)
            q_lo = sb1("q_lo", [P, NCH, TOK], F32R)
            k_hi = sb1("k_hi", [P, NCH, TOK], F32R)
            k_lo = sb1("k_lo", [P, NCH, TOK], F32R)
            VW = DH + 1
            v_aug = sb1("v_aug", [P, 4, NTC, H * VW + 32 - VW])
            q_st = sb1("q_st", [P, H, TOK], F32R)
            k_st = sb1("k_st", [P, H, TOK], F32R)
            neg_max = sb1("neg_max_sb", [P, 2, NTC, H])
            nm_pieces = sb1("nm_pieces", [HPC, 2, TOK], F32R)
            probs = sb1("probs", [P, 8, NTC, TOK])
            lm_t, th_t, turns, angle, angle2 = (probs[:, k, 0, :] for k in range(5))
            trig = probs[:, 5]
            cent, bv_row = probs[0:E, 6, 0, :], probs[0:1, 7, 0, :]
            oT = sb1("oT", [P, H // 4, TOK])
            rden = sb1("rden", [P, NTC, H])
            o = sb1("o", [P, NTC, C])
            oq = sb1("oq", [P, NTC, C])
            stx = sb1("stx", [P, NTC, 6])
            mvx = sb1("mvx", [P, NTC, 2])
            rsx = sb1("rsx", [P, 2, NTC])
            y1, y2 = o, oq
            st2 = sb1("st2", [P, NTC, 6])
            mv2 = sb1("mv2", [P, NTC, 2])
            rs2 = sb1("rs2", [P, 2, NTC])
            row = sb1("row", [P, 2, NTC, ROWW])
            junk = sb1("junk", [P, C], BF16)
            ms = sb1("ms", [P, 2, NTC])
            xn = sb1("xn", [P, NTC, C])
            nx = sb1("nx", [P, NTC])
            xnT = sb1("xnT", [P, NCH, TOK])
            dist = sb1("dist", [P, 2, NTC, E])
            least = sb1("least", [P, NTC])
            cand = sb1("cand", [P, 2, NTC, E])
            choice = sb1("choice", [P, NTC])
            onehot = sb1("onehot", [P, NTC, E])
            onehot_bf = sb1("onehot_bf", [P, NTC, E], BF16)
            place = sb1("place", [P, 2, NTC, E])
            slot_f = sb1("slot_f", [P, NTC])
            slot = sb1("slot", [P, 2, NTC], U32)
            ids = sb1("ids", [P, NTC], I32)

            S_ps = [bank("S0", phase1), bank("S1", phase1)]
            T_ps = [bank("T0", phase1), bank("T1", phase1)]
            O_ps = bank("O", phase1)
            M_ps = [bank(n, phase1) for n in ("M0", "M1", "M2")]
            names = """angles_in params setup_pool setup_dve setup_act setup_pe pads ups ident_ok
                x_in0 x_in1 ctx_in0 ctx_in1 conv u_ok ln1 rstd1 x1_ok x1T_pe x1T_ok ctT_pe ctT_ok
                q_pe q_ok k_pe k_ok q_cut k_cut v_pe v_ok q_out0 q_out1 k_out0 k_out1 stack0 stack1 s_pe max_ok
                negT neg_hi neg_ok neg_out neg_in0 neg_in1 t_pe exp_ok pv o_ev x_pe o_ok qn_pe qn_ok oq_ok lnx rstdx
                x1b_ok y_ok ln2 rstd2 x2_ok ms_ok rms xn_ok nx_ok xnT_pe xnT_ok dist_pe pick rank_pe slot_ok
                id_ok scat0 scat1 pool_waits sp_waits dve_waits"""
            s = {n: sem(n) for n in names.split()}
            x_in, ctx_in_s, q_out, k_out, stack_in = ([s[a + "0"], s[a + "1"]] for a in ("x_in", "ctx_in", "q_out", "k_out", "stack"))
            neg_in, scat = [s["neg_in0"], s["neg_in1"]], [s["scat0"], s["scat1"]]

            def wait(eng, name, item, per=1, j=None):
                if not item.runtime and item.k >= SEQ:
                    item, j = Item(0, SEQ - 1), per
                wait_value(eng, name, item.times(per, per if j is None else j))

            def wait_value(eng, name, v):
                sm = s[name] if isinstance(name, str) else name
                if isinstance(v, int):
                    if v > 0:
                        eng.wait_ge(sm, v)
                else:
                    eng.wait_ge(sm, v)
                    after_register_wait(eng)

            def wait_ring(eng, sm, item, ring, per):
                if not item.runtime:
                    while item.k >= SEQ:
                        item = item - ring
                wait_value(eng, sm, item.uses(ring) * per)

            def after_register_wait(eng):
                if eng.engine in (mybir.EngineType.Pool, mybir.EngineType.SP):
                    eng.sem_inc(s["pool_waits" if eng.engine == mybir.EngineType.Pool else "sp_waits"], 1)

            def steps(eng, body):
                lead = 5
                for n in range(-2, lead):
                    body(Item(0, n))
                loops = (SEQ - 3 - lead) // UNROLL
                with eng.Fori(0, loops) as i:
                    for k in range(UNROLL):
                        body(Item(i, lead + k))
                for n in range(lead + UNROLL * loops, SEQ + 3):
                    body(Item(0, n))

            def active(item):
                return item.within(0, SEQ)

            block = phase1.enter_context(nc.Block())

            x_v = x.rearrange("n (c p) d -> p (n c) d", p=P)
            c_v = ctx_in.rearrange("n (c p) d -> p (n c) d", p=P)

            def bcast(v):
                return v.rearrange("(a n) -> a n", a=1).to_broadcast([P, C])

            @block.sync
            def _(sp):
                def load_x(item):
                    if not active(item):
                        return
                    p = item.mod(2)
                    wait(sp, "u_ok", item - 2)
                    sp.dma_start(xt[:, p], x_v[:, bass.ds(item.times(NTC), NTC), :]).then_inc(x_in[p], 16)

                def load_context(item):
                    if not active(item):
                        return
                    p = item.mod(2)
                    wait(sp, "ctT_pe", item - 2)
                    sp.dma_start(ct[:, p], c_v[:, bass.ds(item.times(NTC), NTC), :]).then_inc(ctx_in_s[p], 16)

                def write_neg(item, half):
                    if not active(item):
                        return
                    p = item.mod(2)
                    wait(sp, "neg_ok", item, 2, half + 1)
                    wait(sp, neg_in[half], item - 2, 16)
                    sp.dma_start(m_dram[p, half].rearrange("w h t -> h w t"), nm_pieces[:, :, :].bitcast(F32)).then_inc(s["neg_out"], 16)

                def read_neg(item, half):
                    if not active(item):
                        return
                    p = item.mod(2)
                    wait(sp, "neg_out", item, 32, 16 * half + 16)
                    sp.dma_start(q_st[64 * p + STACK:64 * p + AUG, half * HPC:(half + 1) * HPC, :].bitcast(F32),
                                 m_dram[p, half]).then_inc(neg_in[half], 16)

                def write_piece(item, dram, w, piece, out):
                    if active(item):
                        sp.dma_start(dram[item.mod(2), :, w].rearrange("o p t -> p o t"), piece[:, :, :].bitcast(F32))\
                            .then_inc(out[item.mod(2)], 16)

                def read_stack(item, half, st, dram, out, once, twice):
                    if not active(item):
                        return
                    p = item.mod(2)
                    b = 64 * p
                    wait_ring(sp, out[p], item, 2, 32)
                    wait(sp, "t_pe", item - 2, H, HPC * (half + 1))
                    hs = slice(half * HPC, (half + 1) * HPC)
                    pieces = dram[p, half].rearrange("w (c h) t -> (w c) h t", h=HPC)
                    sp.dma_start(st[b + once:b + once + DH, hs, :].bitcast(F32), pieces[0:DH]).then_inc(stack_in[half], 16)
                    sp.dma_start(st[b + twice:b + twice + 2 * DH, hs, :].bitcast(F32), pieces).then_inc(stack_in[half], 16)

                def read_q(item, half):
                    read_stack(item, half, q_st, q_dram, q_out, 0, DH)

                def read_k(item, half):
                    read_stack(item, half, k_st, k_dram, k_out, 2 * DH, 0)

                for dst, src in ((lm_t, lmlg), (th_t, theta)):
                    sp.dma_start(dst, bcast(src)).then_inc(s["angles_in"], 16)
                for c in range(NTC):
                    sp.dma_start(state[:, 0, c, :], bcast(last_conv)).then_inc(s["params"], 16)
                load_x(Item(0, 0))
                load_context(Item(0, 0))
                for dst, src in ((wq_sb, Wq), (wk_sb, Wk), (wv_sb, Wv)):
                    sp.dma_start(dst[:, :, :], src.rearrange("(o p) c -> p o c", p=P)).then_inc(s["params"], 16)
                for dst, src in ((bq_sb, bq), (bk_sb, bk)):
                    sp.dma_start(dst[:, :], src.rearrange("(o p) -> p o", p=P), allow_slow_non_contiguous=True).then_inc(s["params"], 16)
                for dst, src in ((g_bc[:, :], ln_g), (b_bc[:, :], ln_b), (scale_bc[:, :], ffn_scale)):
                    sp.dma_start(dst, bcast(src)).then_inc(s["params"], 16)
                sp.dma_start(bv_row, bv.rearrange("(a n) -> a n", a=1)).then_inc(s["params"], 16)
                sp.dma_start(cent, centroids).then_inc(s["params"], 16)

                def ups(e):
                    dst = up_sb[:, e * UPW:(e + 1) * UPW].bitcast(F32).rearrange("p (o n) -> p o n", o=NCH)
                    sp.dma_start(dst, up_w[e].rearrange("(o p) n -> p o n", p=P)).then_inc(s["ups"], 16)

                def step(t):
                    nxt = t + 1
                    load_x(t + 3)
                    load_context(t + 3)
                    write_neg(t - 1, 1)
                    read_neg(t - 1, 1)
                    if active(nxt):
                        for half in range(2):
                            wait(sp, stack_in[half], nxt - 2, 64)
                        wait(sp, "q_ok", nxt, 4, 2)
                    write_piece(nxt, q_dram, 0, q_hi, q_out)
                    if active(nxt):
                        wait(sp, "q_cut", nxt)
                    write_piece(nxt, q_dram, 1, q_lo, q_out)
                    read_q(nxt, 0)
                    if active(nxt):
                        wait(sp, "k_ok", nxt, 4, 2)
                    write_piece(nxt, k_dram, 0, k_hi, k_out)
                    if active(nxt):
                        wait(sp, "k_cut", nxt)
                    write_piece(nxt, k_dram, 1, k_lo, k_out)
                    write_neg(t, 0)
                    read_k(nxt, 0)
                    read_neg(t, 0)
                    read_q(nxt, 1)
                    read_k(nxt, 1)
                    if not t.runtime and t.k in UP_STEPS:
                        ups(UP_STEPS.index(t.k))

                steps(sp, step)
                sp.wait_ge(s["pads"], 16)
                sp.wait_ge(s["ups"], 16 * E)
                for p in range(2):
                    sp.wait_ge(scat[p], 16 * NTC * SEQ // 2)

            @block.gpsimd
            def _(pool):
                g = nc.gpsimd
                g.memset(ident[:, :], 0.0).then_inc(s["ident_ok"], 1)
                pool.wait_ge(s["ident_ok"], 1)
                g.affine_select(out=ident[:, :], in_=ident[:, :], compare_op=ALU.not_equal, fill=1.0, base=0,
                                pattern=[[-1, P]], channel_multiplier=1).then_inc(s["ident_ok"], 1)
                g.memset(neg_half[:, :], -0.5).then_inc(s["setup_pool"], 1)
                g.memset(ones_r[:, :].bitcast(F32), 1.0).then_inc(s["setup_pool"], 1)
                g.memset(ones_bf[:, :], 1.0).then_inc(s["setup_pool"], 1)
                g.memset(before[:, :], 1.0).then_inc(s["setup_pool"], 1)
                g.memset(k_st[:, :, :].bitcast(F32), 1.0).then_inc(s["setup_pool"], 1)
                g.memset(v_aug[:, :, :, :], 1.0).then_inc(s["setup_pool"], 1)
                g.memset(state[:, 1], 0.0).then_inc(s["setup_pool"], 1)
                g.memset(pad_row[:, :], 0.0).then_inc(s["setup_pool"], 1)
                g.iota(ids[:, :], pattern=[[P, NTC]], base=0, channel_multiplier=1).then_inc(s["setup_pool"], 1)
                g.iota(expert_no[:, :, :], pattern=[[0, NTC], [1, E]], base=0, channel_multiplier=0,
                       allow_small_or_imprecise_dtypes=True).then_inc(s["setup_pool"], 1)
                g.iota(filled[:, :], pattern=[[CAP, E]], base=0, channel_multiplier=0,
                       allow_small_or_imprecise_dtypes=True).then_inc(s["setup_pool"], 1)
                pool.wait_ge(s["setup_pool"], 11)
                g.affine_select(out=before[:, :], in_=before[:, :], compare_op=ALU.is_gt, fill=0.0, base=0,
                                pattern=[[1, P]], channel_multiplier=-1).then_inc(s["setup_pool"], 1)
                g.memset(pad_row[:, C + 1:C + 2].bitcast(U32), NOID).then_inc(s["setup_pool"], 1)
                pool.wait_ge(s["setup_pool"], 13)
                g.dma_start(buckets[PAD:PAD + P, :], pad_row[:, :]).then_inc(s["pads"], 16)
                pool.wait_ge(s["params"], 12 * 16)
                pool.wait_ge(s["setup_dve"], 10)

                re_b = decay_re[:, :].unsqueeze(1).to_broadcast([P, 2 * NTC, C])
                im_b = decay_im[:, :].unsqueeze(1).to_broadcast([P, 2 * NTC, C])
                z_all = state[:, :, :, :].rearrange("p r c d -> p (r c) d")

                def conv_products(item, j):
                    if not active(item):
                        return
                    if j == 0:
                        wait(pool, "conv", item - 1, 5)
                        g.tensor_tensor(by_im[:, :, :, :].rearrange("p r c d -> p (r c) d"), z_all, im_b, ALU.mult).then_inc(s["conv"], 1)
                    else:
                        wait(pool, "u_ok", item - 1)
                        g.tensor_tensor(z_all, z_all, re_b, ALU.mult).then_inc(s["conv"], 1)

                def conv_sum(item, j):
                    if not active(item):
                        return
                    if j == 0:
                        wait(pool, "conv", item, 5, 2)
                        g.tensor_tensor(state[:, 1], state[:, 1], by_im[:, 0], ALU.add).then_inc(s["conv"], 1)
                    else:
                        g.tensor_tensor(state[:, 0], state[:, 0], by_im[:, 1], ALU.subtract).then_inc(s["conv"], 1)

                def conv_input(item):
                    if not active(item):
                        return
                    wait_ring(pool, x_in[item.mod(2)], item, 2, 16)
                    wait(pool, "conv", item, 5, 4)
                    g.tensor_tensor(state[:, 0], state[:, 0], xt[:, item.mod(2)], ALU.add).then_inc(s["conv"], 1)

                def rstd(item, ready, per, mv, rs, done):
                    if not active(item):
                        return
                    wait(pool, ready, item, per)
                    g.tensor_scalar(rs[:, 0], mv[:, :, 1], LN_EPS, None, ALU.add).then_inc(s[done], 1)
                    wait(pool, done, item, 2, 1)
                    g.tensor_tensor(rs[:, 1], rs[:, 0], neg_half[:, :].to_broadcast([P, NTC]), ALU.pow).then_inc(s[done], 1)

                def rms(item):
                    if not active(item):
                        return
                    p = item.mod(2)
                    wait(pool, "ms_ok", item, 2)
                    g.tensor_scalar(ms[:, 1], ms[:, 0], 1.0 / C, RMS_EPS, ALU.mult, ALU.add).then_inc(s["rms"], 1)
                    wait(pool, "rms", item, 2, 1)
                    g.tensor_tensor(row[:, p, :, C], ms[:, 1], neg_half[:, :].to_broadcast([P, NTC]), ALU.pow).then_inc(s["rms"], 1)

                def cut(item, src, hi, lo, ready, done, out):
                    if not active(item):
                        return
                    wait(pool, ready, item, 4)
                    wait_ring(pool, out[(item - 1).mod(2)], item - 1, 2, 32)
                    g.tensor_tensor(lo[:, :, :], src, hi[:, :, :].bitcast(F32), ALU.subtract).then_inc(s[done], 1)

                def step(t):
                    n, a, b = t + 1, t - 2, t - 3
                    rms(b)
                    first = not t.runtime and t.k < 0
                    if first:
                        rstd(t + 2, "ln1", 4, mv1, rs1, "rstd1")
                    conv_products(t + 3, 0)
                    if active(a):
                        wait(pool, "x1_ok", a, 2)
                        wait(pool, "x1T_pe", a)
                        g.tensor_tensor(x1[:, a.mod(4)], x1[:, a.mod(4)], b_bc[:, :].unsqueeze(1).to_broadcast([P, NTC, C]),
                                        ALU.add).then_inc(s["x1b_ok"], 1)
                    cut(n, q32[:, :, :], q_hi, q_lo, "q_ok", "q_cut", q_out)
                    conv_products(t + 3, 1)
                    if not first:
                        rstd(t + 2, "ln1", 4, mv1, rs1, "rstd1")
                    conv_sum(t + 3, 0)
                    cut(n, k32[:, :, :], k_hi, k_lo, "k_ok", "k_cut", k_out)
                    conv_sum(t + 3, 1)
                    rstd(a, "lnx", 4, mvx, rsx, "rstdx")
                    if active(b):
                        p = b.mod(2)
                        wait(pool, "slot_ok", b, 7)
                        wait(pool, "id_ok", b, 2)
                        for c in range(NTC):
                            g.indirect_dma_start(out=buckets[:, :], out_offset=bass.IndirectOffsetOnAxis(ap=slot[:, p, c:c + 1], axis=0),
                                                 in_=row[:, p, c, :], in_offset=None, bounds_check=PAD - 1,
                                                 oob_is_err=False).then_inc(scat[p], 16)
                    conv_input(t + 3)
                    rstd(a, "ln2", 4, mv2, rs2, "rstd2")

                conv_products(Item(0, 0), 0)
                conv_products(Item(0, 0), 1)
                conv_sum(Item(0, 0), 0)
                conv_sum(Item(0, 0), 1)
                conv_input(Item(0, 0))
                steps(pool, step)

            @block.scalar
            def _(act):
                a_ = nc.scalar
                act.wait_ge(s["angles_in"], 2 * 16)
                a_.activation(lm_t, lm_t, ACT.Exp).then_inc(s["setup_act"], 1)
                act.wait_ge(s["setup_act"], 1)
                a_.activation(decay_re[:, :], lm_t, ACT.Exp, scale=-1.0).then_inc(s["setup_act"], 1)
                act.wait_ge(s["setup_dve"], 8)
                a_.activation(trig[:, 0], angle, ACT.Sin).then_inc(s["setup_act"], 1)
                a_.activation(trig[:, 1], angle2, ACT.Sin).then_inc(s["setup_act"], 1)

                def neg_upper(item, half, b):
                    wait(act, "negT", item, 2, half + 1)
                    wait_value(act, "neg_out", item.times(32, 16 * half))
                    a_.activation(nm_pieces[:, 0], M_ps[b][0:HPC, 0:TOK], ACT.Copy).then_inc(s["neg_hi"], 1)

                def copy_sums(item, pair):
                    wait(act, "pv", item, 4, 2 * pair + 2)
                    if pair == 0:
                        wait(act, "x_pe", item - 1, 2)
                    a_.activation(oT[:, 2 * pair:2 * pair + 2, :].rearrange("p g t -> p (g t)"), O_ps[:, :], ACT.Copy).then_inc(s["o_ev"], 1)

                def step(t):
                    prv, n, a, b = t - 1, t + 1, t - 2, t - 3
                    for h in range(H):
                        if active(prv):
                            wait(act, "t_pe", prv, H, h + 1)
                            if h % 4 == 0:
                                used = prv.times(4, h // 4 - 1) if h >= 8 else (prv - 1).times(4, h // 4 + 3)
                                wait_value(act, "pv", used)
                            a_.activation(probs[:, h % 8].rearrange("p k t -> p (k t)"), T_ps[h % 2][:, :], ACT.Exp,
                                          scale=DH ** -0.5).then_inc(s["exp_ok"], 1)
                        if h == 0:
                            if active(n):
                                wait(act, "x1T_pe", n)
                                wait(act, "q_pe", n - 1, 2)
                                a_.activation(x1T[:, :, :].rearrange("p o t -> p (o t)"), M_ps[0][:, :], ACT.Copy).then_inc(s["x1T_ok"], 1)
                            if active(b):
                                wait(act, "x2_ok", b, 2)
                                wait(act, "rms", b - 1, 2, 1)
                                wait(act, "nx_ok", b - 1, 2)
                                for c in range(NTC):
                                    if c:
                                        wait(act, "ms_ok", b, 2, 1)
                                    a_.activation(junk[:, :], row[:, b.mod(2), c, 0:C], ACT.Square,
                                                  accum_out=ms[:, 0, c:c + 1]).then_inc(s["ms_ok"], 1)
                        if h == 14 and active(n):
                            wait(act, "qn_pe", n)
                            wait(act, "oq_ok", n - 4, 2)
                            a_.activation(qn[:, n.mod(4)].rearrange("p c d -> p (c d)"), M_ps[2][:, :], ACT.Copy).then_inc(s["qn_ok"], 1)
                        if h == 15 and active(n + 1):
                            wait(act, "ctT_pe", n + 1)
                            wait(act, "v_pe", n, 2)
                            a_.activation(ctT[:, :, :].rearrange("p o t -> p (o t)"), M_ps[0][:, :], ACT.Copy).then_inc(s["ctT_ok"], 1)
                        if h == 1 and active(prv):
                            neg_upper(prv, 1, 2)
                        if h == 9 and active(t):
                            neg_upper(t, 0, 0)
                        if h == 2 and active(a):
                            copy_sums(a, 1)
                        if h == 3:
                            if active(n):
                                wait(act, "q_pe", n, 2)
                                wait(act, "qn_pe", n - 1)
                                wait_ring(act, q_out[(n - 1).mod(2)], n - 1, 2, 32)
                                for dst in (q_hi, q32):
                                    for c in range(NCH):
                                        a_.activation(dst[:, c], M_ps[0][:, c * TOK:(c + 1) * TOK], ACT.Relu,
                                                      bias=bq_sb[:, c:c + 1]).then_inc(s["q_ok"], 1)
                        if h == 7 and active(n):
                            wait(act, "k_pe", n, 2)
                            wait(act, "k_cut", n - 1)
                            wait_ring(act, k_out[(n - 1).mod(2)], n - 1, 2, 32)
                            for dst in (k_hi, k32):
                                for c in range(NCH):
                                    a_.activation(dst[:, c], M_ps[1][:, c * TOK:(c + 1) * TOK], ACT.Relu,
                                                  bias=bk_sb[:, c:c + 1]).then_inc(s["k_ok"], 1)
                        if h == 3 and active(b):
                            wait(act, "xnT_pe", b)
                            wait(act, "dist_pe", b - 1)
                            a_.activation(xnT[:, :, :].rearrange("p o t -> p (o t)"), M_ps[2][:, :], ACT.Copy).then_inc(s["xnT_ok"], 1)
                        if h == 13 and active(n):
                            wait(act, "v_pe", n, 2)
                            wait(act, "pv", n - 4, 4)
                            a_.activation(v_aug[:, n.mod(4), :, 0:H * VW].rearrange("p k (h w) -> p k h w", w=VW)[:, :, :, 0:DH],
                                          M_ps[1][:, :].rearrange("p (k h w) -> p k h w", k=NTC, w=DH), ACT.Relu).then_inc(s["v_ok"], 1)
                        if h == 4 and active(b):
                            wait(act, "xn_ok", b, 2)
                            wait(act, "pick", b - 1, 7, 2)
                            for c in range(NTC):
                                if c:
                                    wait(act, "nx_ok", b, 2, 1)
                                a_.activation(junk[:, :], xn[:, c], ACT.Square, accum_out=nx[:, c:c + 1]).then_inc(s["nx_ok"], 1)
                        if h == 11 and active(prv):
                            copy_sums(prv, 0)

                steps(act, step)

            @block.tensor
            def _(pe):
                t_ = nc.tensor
                pe.wait_ge(s["ident_ok"], 2)
                pe.wait_ge(s["params"], 12 * 16)
                pe.wait_ge(s["setup_pool"], 13)
                for c in range(NCH):
                    last = t_.transpose(M_ps[0][:, c * E:(c + 1) * E], cent[:, c * P:(c + 1) * P], ident[0:E, 0:E])
                last.then_inc(s["setup_pe"], 1)
                pe.wait_ge(s["setup_dve"], SETUP_DVE - 1)
                for c in range(NCH):
                    last = t_.matmul(M_ps[1][:, 0:E], ones_r[:, :].bitcast(F32), cent_sq[:, c, :], start=(c == 0), stop=(c == NCH - 1))
                last.then_inc(s["setup_pe"], 1)
                pe.wait_ge(s["setup_dve"], SETUP_DVE)

                def flip(dst, src):
                    for oc in range(NCH):
                        for tc in range(NTC):
                            last = t_.transpose(dst[:, oc * TOK + tc * P:oc * TOK + (tc + 1) * P], src[:, tc, oc * P:(oc + 1) * P], ident[:, :])
                    return last

                def neg_flip(item, half, b):
                    wait(pe, "max_ok", item, H, HPC * (half + 1))
                    for c in range(NTC):
                        last = t_.transpose(M_ps[b][0:HPC, c * P:(c + 1) * P], neg_max[:, item.mod(2), c, half * HPC:(half + 1) * HPC], ident[:, :])
                    last.then_inc(s["negT"], 1)

                def weighted_sum(item, grp):
                    wait(pe, "exp_ok", item, H, 4 * grp + 4)
                    if grp == 0:
                        wait(pe, "v_ok", item)
                    wait_value(pe, "o_ev", item.times(2, grp // 2))
                    for kc in range(NTC):
                        for j in range(4):
                            h = 4 * grp + j
                            last = t_.matmul(O_ps[32 * j:32 * j + 32, (grp % 2) * TOK:(grp % 2 + 1) * TOK],
                                             v_aug[:, item.mod(4), kc, h * VW:h * VW + 32], probs[:, h % 8, kc, :],
                                             start=(kc == 0), stop=(kc == NTC - 1))
                    last.then_inc(s["pv"], 1)

                def project(dst, w, xT, oc):
                    for ic in range(NCH):
                        last = t_.matmul(dst[:, oc * TOK:(oc + 1) * TOK], w[:, ic, oc * P:(oc + 1) * P], xT[:, ic, :],
                                         start=(ic == 0), stop=(ic == NCH - 1))
                    return last


                def step(t):
                    cur, prv, n, a, b = t, t - 1, t + 1, t - 2, t - 3
                    for h in range(H):
                        if active(cur):
                            if h % HPC == 0:
                                wait(pe, stack_in[h // HPC], cur, 64)
                            wait_value(pe, "max_ok", cur.times(H, h - 1))
                            base = 64 * cur.mod(2)
                            for c in range(NTC):
                                last = t_.matmul(S_ps[h % 2][:, c * TOK:(c + 1) * TOK], q_st[base:base + STACK, h, c * P:(c + 1) * P],
                                                 k_st[base:base + STACK, h, :], start=True, stop=True)
                            last.then_inc(s["s_pe"], 1)
                        if active(prv):
                            if h % HPC == 0:
                                wait(pe, neg_in[h // HPC], prv, 16)
                            wait_value(pe, "exp_ok", prv.times(H, h - 1))
                            base = 64 * prv.mod(2)
                            for c in range(NTC):
                                last = t_.matmul(T_ps[h % 2][:, c * TOK:(c + 1) * TOK], k_st[base:base + AUG, h, c * P:(c + 1) * P],
                                                 q_st[base:base + AUG, h, :], start=True, stop=True)
                            last.then_inc(s["t_pe"], 1)
                        if h == 0 and active(n):
                            wait(pe, "x1_ok", n, 2)
                            wait(pe, "ctT_ok", n)
                            flip(M_ps[0], x1[:, n.mod(4)]).then_inc(s["x1T_pe"], 1)
                        if h == 1:
                            if active(prv):
                                wait(pe, "qn_ok", t)
                                neg_flip(prv, 1, 2)
                            if active(a):
                                weighted_sum(a, 3)
                        if h in (2, 3) and active(n):
                            wait(pe, "x1T_ok", n)
                            project(M_ps[0], wq_sb, x1T, h - 2).then_inc(s["q_pe"], 1)
                        if h == 3 and active(b):
                            wait(pe, "xn_ok", b, 2)
                            wait(pe, "neg_ok", prv, 2)
                            if not t.runtime:
                                wait(pe, "slot_ok", b - 1, 7)
                            flip(M_ps[2], xn).then_inc(s["xnT_pe"], 1)
                        if h in (4, 5) and active(a):
                            c = h - 4
                            wait(pe, "o_ev", a, 2)
                            if c == 0:
                                wait(pe, "v_ok", t)
                                if not t.runtime:
                                    wait(pe, "k_ok", t, 4)
                                    wait(pe, "o_ok", b, 4, 2)
                            else:
                                wait(pe, "q_ok", n, 4)
                                if not t.runtime:
                                    wait(pe, "ctT_ok", n)
                                    wait(pe, "neg_ok", prv, 2, 1)
                            for g4 in range(H // 4):
                                last = t_.transpose(M_ps[1 - c][:, g4 * P:(g4 + 1) * P], oT[:, g4, c * P:(c + 1) * P], ident[:, :])
                            last.then_inc(s["x_pe"], 1)
                        if h == 5 and active(b):
                            wait(pe, "xnT_ok", b)
                            for c in range(NTC):
                                for oc in range(NCH):
                                    last = t_.matmul(M_ps[2][:, c * E:(c + 1) * E], xnT[:, oc, c * P:(c + 1) * P], centT[:, oc, :],
                                                     start=(oc == 0), stop=(oc == NCH - 1))
                            last.then_inc(s["dist_pe"], 1)
                        if h == 8 and active(prv):
                            weighted_sum(prv, 0)
                        if h in (6, 7) and active(n):
                            wait(pe, "ctT_ok", n)
                            wait(pe, "o_ok", a, 4, 2)
                            wait(pe, "v_ok", t)
                            project(M_ps[1], wk_sb, ctT, h - 6).then_inc(s["k_pe"], 1)
                        if h == 10 and active(prv):
                            weighted_sum(prv, 1)
                        if h == 10:
                            if active(b):
                                wait(pe, "pick", b, 7)
                                r0, r1, tot = 64, 64 + E, 64 + 2 * E
                                t_.matmul(M_ps[2][:, r0:r0 + E], before[:, :], onehot_bf[:, 0, :], start=True, stop=True)
                                t_.matmul(M_ps[2][:, r1:r1 + E], before[:, :], onehot_bf[:, 1, :], start=True, stop=False)
                                t_.matmul(M_ps[2][:, r1:r1 + E], ones_bf[:, :], onehot_bf[:, 0, :], start=False, stop=True)
                                t_.matmul(M_ps[2][:, tot:tot + E], ones_bf[:, :], onehot_bf[:, 0, :], start=True, stop=False)
                                t_.matmul(M_ps[2][:, tot:tot + E], ones_bf[:, :], onehot_bf[:, 1, :], start=False, stop=True)\
                                    .then_inc(s["rank_pe"], 1)
                        if h == 9:
                            if active(cur):
                                wait(pe, "o_ok", a, 4)
                                if not t.runtime:
                                    wait(pe, "q_ok", n, 4)
                                    wait(pe, "ctT_ok", n)
                                neg_flip(cur, 0, 0)
                        if h in (11, 12) and active(n):
                            c = h - 11
                            wait(pe, "k_ok", n, 4)
                            if not t.runtime:
                                wait(pe, "o_ok", a, 4, 2)
                            for ic in range(NCH):
                                t_.matmul(M_ps[1][:, c * C:(c + 1) * C], ctT[:, ic, c * P:(c + 1) * P], wv_sb[:, ic, :],
                                          start=(ic == 0), stop=False)
                            for w in range(2):
                                last = t_.matmul(M_ps[1][:, c * C:(c + 1) * C], ones_r[0:1, :], bv_cut[:, w, :],
                                                 start=False, stop=(w == 1))
                            last.then_inc(s["v_pe"], 1)
                        if h == 14 and active(n):
                            wait(pe, "slot_ok", b, 7, 4)
                            wait(pe, "q_ok", n, 4)
                            if not t.runtime:
                                wait(pe, "neg_ok", prv, 2)
                                wait(pe, "qn_ok", t)
                            for c in range(NTC):
                                for oc in range(NCH):
                                    last = t_.transpose(M_ps[2][:, c * C + oc * P:c * C + (oc + 1) * P],
                                                        q32[:, oc, c * P:(c + 1) * P], ident[:, :])
                            last.then_inc(s["qn_pe"], 1)
                        if h == 13 and active(prv):
                            weighted_sum(prv, 2)
                        if h == 15 and active(n + 1):
                            nn = n + 1
                            wait_ring(pe, ctx_in_s[nn.mod(2)], nn, 2, 16)
                            wait(pe, "neg_ok", cur, 2, 1)
                            if not t.runtime:
                                wait(pe, "q_ok", n, 4)
                                wait(pe, "o_ok", a, 4)
                            flip(M_ps[0], ct[:, nn.mod(2)]).then_inc(s["ctT_pe"], 1)

                steps(pe, step)

            @block.vector
            def _(dve):
                v = nc.vector
                done = [0]

                def setup(ins):
                    done[0] += 1
                    ins.then_inc(s["setup_dve"], 1)
                    dve.wait_ge(s["setup_dve"], done[0])

                dve.wait_ge(s["angles_in"], 2 * 16)
                setup(v.tensor_scalar(turns, th_t, 1 / (2 * np.pi), None, ALU.mult))
                setup(v.tensor_scalar(turns, turns, ROUND, -ROUND, ALU.add, ALU.add))
                setup(v.scalar_tensor_tensor(angle, turns, -TWO_PI_A, th_t, ALU.mult, ALU.add))
                setup(v.scalar_tensor_tensor(angle, turns, -TWO_PI_B, angle, ALU.mult, ALU.add))
                setup(v.scalar_tensor_tensor(angle, turns, -TWO_PI_C, angle, ALU.mult, ALU.add))
                setup(v.tensor_scalar(angle, angle, 3.1415925, -3.1415925, ALU.min, ALU.max))
                setup(v.scalar_tensor_tensor(angle2, angle, -1.0, angle, ALU.mult, ALU.max))
                setup(v.tensor_scalar(angle2, angle2, -1.0, np.pi / 2, ALU.mult, ALU.add))
                dve.wait_ge(s["setup_act"], 4)
                setup(v.tensor_tensor(decay_im[:, :], decay_re[:, :], trig[:, 0], ALU.mult))
                setup(v.tensor_tensor(decay_re[:, :], decay_re[:, :], trig[:, 1], ALU.mult))
                dve.wait_ge(s["params"], 12 * 16)
                dve.wait_ge(s["setup_pool"], 13)
                setup(v.tensor_copy(bv_cut[:, 0], bv_row))
                setup(v.tensor_tensor(bv_cut[:, 1], bv_row, bv_cut[:, 0].bitcast(F32), ALU.subtract))
                dve.wait_ge(s["setup_pe"], 1)
                ctv = centT[:, :, :].rearrange("p o e -> p (o e)")
                setup(v.tensor_scalar(ctv, M_ps[0][:, 0:NCH * E], -2.0, None, ALU.mult))
                setup(v.scalar_tensor_tensor(cent_sq[:, :, :].rearrange("p o e -> p (o e)"), ctv, 0.25, ctv, ALU.mult, ALU.mult))
                dve.wait_ge(s["setup_pe"], 2)
                setup(v.tensor_copy(cent_norm[:, :], M_ps[1][:, 0:E]))
                assert done[0] == SETUP_DVE

                def stats(item, src, st, name):
                    for c in range(NTC):
                        v.bn_stats(st[:, c], src[:, c]).then_inc(s[name], 1)

                def moments(item, st, mv, name):
                    wait(dve, name, item, 4, 2)
                    dve.sem_inc(s["dve_waits"], 1)
                    for c in range(NTC):
                        v.bn_aggr(mv[:, c], st[:, c]).then_inc(s[name], 1)

                def step(t):
                    cur, prv, nn, a, b = t, t - 1, t + 2, t - 2, t - 3
                    for h in range(H):
                        if active(cur):
                            wait(dve, "s_pe", cur, H, h + 1)
                            if h == 0:
                                wait(dve, "negT", cur - 2, 2)
                            v.tensor_reduce(neg_max[:, cur.mod(2), :, h], S_ps[h % 2][:, :].rearrange("p (c t) -> p c t", c=NTC),
                                            AX.X, ALU.max, negate=True).then_inc(s["max_ok"], 1)
                        if h == 2 and active(prv):
                            neg_cut(prv, 1, 2)
                        if h == 2 and active(b):
                            wait(dve, "rms", b, 2)
                            wait(dve, "nx_ok", b - 1, 2)
                            wait(dve, "xnT_pe", b - 1)
                            for c in range(NTC):
                                v.scalar_tensor_tensor(xn[:, c], row[:, b.mod(2), c, 0:C], row[:, b.mod(2), c, C:C + 1], scale_bc[:, :],
                                                       ALU.mult, ALU.mult).then_inc(s["xn_ok"], 1)
                        if h == 3 and active(nn):
                            wait(dve, "x1_ok", nn - 1, 2)
                            wait(dve, "conv", nn, 5)
                            wait_ring(dve, x_in[nn.mod(2)], nn, 2, 16)
                            v.scalar_tensor_tensor(u[:, :, :], state[:, 0], 1.0, xt[:, nn.mod(2)], ALU.add, ALU.mult).then_inc(s["u_ok"], 1)
                        if h == 4 and active(nn):
                            wait(dve, "u_ok", nn)
                            wait(dve, "rstd1", nn - 1, 2)
                            stats(nn, u, st1, "ln1")
                        if h == 5:
                            if active(a):
                                divide(a, 0, 0)
                            if active(nn):
                                moments(nn, st1, mv1, "ln1")
                            if active(a):
                                divide(a, 0, 1)
                        if h == 6:
                            if active(b):
                                pick(b, 0)
                                pick(b, 1)
                        if h == 7:
                            if active(a):
                                divide(a, 1, 0)
                            if active(b):
                                pick(b, 2)
                            if active(a):
                                divide(a, 1, 1)
                            if active(b):
                                pick(b, 3)
                            if active(a):
                                add_queries(a, 0)
                            if active(b):
                                pick(b, 4)
                        if h == 8:
                            if active(b):
                                pick(b, 5)
                            if active(a):
                                add_queries(a, 1)
                            if active(b):
                                pick(b, 6)
                        if h == 9 and active(a):
                            wait(dve, "oq_ok", a, 2)
                            stats(a, oq, stx, "lnx")
                            moments(a, stx, mvx, "lnx")
                        if h == 10 and active(cur):
                            neg_cut(cur, 0, 0)
                        if h == 11:
                            if active(b):
                                slots(b, 0)
                            if active(a):
                                gain(a, 0)
                            if active(b):
                                slots(b, 1)
                            if active(a):
                                gain(a, 1)
                            if active(b):
                                slots(b, 2)
                        if h == 12:
                            if active(b):
                                slots(b, 3)
                            if active(a):
                                wait(dve, "rstdx", a, 2)
                                wait(dve, "x1b_ok", a)
                                for c in range(NTC):
                                    wait(dve, "y_ok", a, 4, c + 1)
                                    v.scalar_tensor_tensor(y2[:, c], y1[:, c], rsx[:, 1, c:c + 1], x1[:, a.mod(4), c],
                                                           ALU.mult, ALU.add).then_inc(s["y_ok"], 1)
                        if h == 13 and active(nn):
                            wait(dve, "rstd1", nn, 2)
                            wait(dve, "y_ok", nn - 4, 4)
                            for c in range(NTC):
                                v.tensor_scalar(x1[:, nn.mod(4), c], u[:, c], mv1[:, c, 0:1], rs1[:, 1, c:c + 1],
                                                ALU.subtract, ALU.mult).then_inc(s["x1_ok"], 1)
                        if h == 13 and active(a):
                            wait(dve, "y_ok", a, 4)
                            stats(a, y2, st2, "ln2")
                        if h == 14 and active(a):
                            moments(a, st2, mv2, "ln2")
                        if h == 15 and active(a):
                            wait(dve, "rstd2", a, 2)
                            wait_ring(dve, scat[a.mod(2)], a - 2, 2, 16 * NTC)
                            for c in range(NTC):
                                v.tensor_scalar(row[:, a.mod(2), c, 0:C], y2[:, c], mv2[:, c, 0:1], rs2[:, 1, c:c + 1],
                                                ALU.subtract, ALU.mult).then_inc(s["x2_ok"], 1)
                            wait(dve, "id_ok", a - 1, 2)
                            v.tensor_copy(row[:, a.mod(2), :, C + 1].bitcast(I32), ids[:, :]).then_inc(s["id_ok"], 1)
                            v.tensor_scalar(ids[:, :], ids[:, :], float(TOK), None, ALU.add).then_inc(s["id_ok"], 1)

                def divide(a, c, stage):
                    src = M_ps[1 - c][:, :].rearrange("p (h w) -> p h w", w=32)
                    if stage == 0:
                        wait(dve, "x_pe", a, 2, c + 1)
                        v.reciprocal(rden[:, c], src[:, :, DH]).then_inc(s["o_ok"], 1)
                    else:
                        wait(dve, "o_ok", a, 4, 2 * c + 1)
                        v.tensor_tensor(o[:, c].rearrange("p (h w) -> p h w", w=DH), src[:, :, 0:DH],
                                        rden[:, c].unsqueeze(2).to_broadcast([P, H, DH]), ALU.mult).then_inc(s["o_ok"], 1)

                def add_queries(a, c):
                    if c == 0:
                        wait(dve, "qn_ok", a)
                    wait(dve, "o_ok", a, 4, 2 * c + 2)
                    v.tensor_tensor(oq[:, c].rearrange("p (o h w) -> p o h w", o=NCH, h=HPC),
                                    o[:, c].rearrange("p (o h w) -> p o h w", o=NCH, h=HPC),
                                    qn[:, a.mod(4), c].rearrange("p (o w h) -> p o h w", o=NCH, h=HPC),
                                    ALU.add).then_inc(s["oq_ok"], 1)

                def gain(a, c):
                    wait(dve, "lnx", a, 4, 3 + c)
                    v.scalar_tensor_tensor(y1[:, c], oq[:, c], mvx[:, c, 0:1], g_bc[:, :],
                                           ALU.subtract, ALU.mult).then_inc(s["y_ok"], 1)

                def neg_cut(item, half, b):
                    wait(dve, "neg_hi", item, 2, half + 1)
                    v.tensor_tensor(nm_pieces[:, 1], M_ps[b][0:HPC, 0:TOK], nm_pieces[:, 0].bitcast(F32), ALU.subtract)\
                        .then_inc(s["neg_ok"], 1)

                def pick(b, stage):
                    ch = choice[:, :].unsqueeze(2).to_broadcast([P, NTC, E])
                    if stage == 0:
                        wait(dve, "nx_ok", b, 2)
                        for c in range(NTC):
                            v.tensor_scalar(dist[:, 0, c], cent_norm[:, :], nx[:, c:c + 1], None, ALU.add).then_inc(s["pick"], 1)
                    if stage == 1:
                        wait(dve, "dist_pe", b)
                        wait(dve, "pick", b, 7, 2)
                        v.tensor_tensor(dist[:, 1], dist[:, 0], M_ps[2][:, 0:NTC * E].rearrange("p (c e) -> p c e", c=NTC), ALU.add)\
                            .then_inc(s["pick"], 1)
                    if stage == 2:
                        wait(dve, "pick", b, 7, 3)
                        v.tensor_reduce(least[:, :], dist[:, 1], AX.X, ALU.min).then_inc(s["pick"], 1)
                    if stage == 3:
                        wait(dve, "pick", b, 7, 4)
                        v.tensor_tensor(cand[:, 0], dist[:, 1], least[:, :].unsqueeze(2).to_broadcast([P, NTC, E]), ALU.is_gt)\
                            .then_inc(s["pick"], 1)
                    if stage == 4:
                        wait(dve, "pick", b, 7, 5)
                        v.scalar_tensor_tensor(cand[:, 1], cand[:, 0], float(E), expert_no[:, :, :], ALU.mult, ALU.add).then_inc(s["pick"], 1)
                    if stage == 5:
                        wait(dve, "pick", b, 7, 6)
                        v.tensor_reduce(choice[:, :], cand[:, 1], AX.X, ALU.min).then_inc(s["slot_ok"], 1)
                    if stage == 6:
                        wait(dve, "slot_ok", b, 7, 1)
                        v.tensor_tensor(onehot[:, :, :], expert_no[:, :, :], ch, ALU.is_equal).then_inc(s["slot_ok"], 1)
                        v.tensor_tensor(onehot_bf[:, :, :], expert_no[:, :, :], ch, ALU.is_equal).then_inc(s["pick"], 1)

                def slots(b, stage):
                    if stage == 0:
                        wait(dve, "rank_pe", b)
                        wait(dve, "slot_ok", b, 7, 2)
                        wait(dve, "slot_ok", b - 1, 7)
                        v.tensor_tensor(place[:, 0], M_ps[2][:, 64:64 + NTC * E].rearrange("p (c e) -> p c e", c=NTC),
                                        filled[:, :].unsqueeze(1).to_broadcast([P, NTC, E]), ALU.add).then_inc(s["slot_ok"], 1)
                    if stage == 1:
                        wait(dve, "slot_ok", b, 7, 3)
                        v.tensor_tensor(filled[:, :], filled[:, :], M_ps[2][:, 64 + NTC * E:64 + (NTC + 1) * E], ALU.add).then_inc(s["slot_ok"], 1)
                        v.tensor_tensor(place[:, 1], place[:, 0], onehot[:, :, :], ALU.mult).then_inc(s["slot_ok"], 1)
                    if stage == 2:
                        wait(dve, "slot_ok", b, 7, 5)
                        v.tensor_reduce(slot_f[:, :], place[:, 1], AX.X, ALU.add).then_inc(s["slot_ok"], 1)
                    if stage == 3:
                        wait(dve, "slot_ok", b, 7, 6)
                        wait_ring(dve, scat[b.mod(2)], b - 2, 2, 16 * NTC)
                        v.tensor_copy(slot[:, b.mod(2)], slot_f[:, :]).then_inc(s["slot_ok"], 1)

                steps(dve, step)

        def sb2(name, shape, dt=F32):
            return stack.enter_context(nc.sbuf_tensor(name, shape, dt))

        dn_sb = sb2("dn_sb", [P, E * DNW])
        up_hi = sb2("up_hi", [P, E * UPW], F32R)
        base = sb2("base", [1, E])
        count = sb2("count", [1, E])
        tiles = sb2("tiles", [1, E])
        ends = sb2("ends", [1, E])
        skip = sb2("skip", [1, E])
        tno = sb2("tno", [1, NTILES])
        owned = sb2("owned", [1, NTILES])
        row_f = sb2("row_f", [1, 2, NTILES])
        eno_f = sb2("eno_f", [1, NTILES])
        RING = 4
        xr = sb2("xr", [P, RING, ROWW])
        xs = sb2("xs", [P, C])
        xsT = sb2("xsT", [P, 2, 2, NCH * P], F32R)
        gate = sb2("gate", [P, HID])
        gated = sb2("gated", [P, HID])
        gT = sb2("gT", [P, 2, HCH * P])
        y = sb2("y", [P, C])
        st3 = sb2("st3", [P, 6])
        mv3 = sb2("mv3", [P, 2])
        rs3 = sb2("rs3", [P, 2])
        res = sb2("res", [P, 2, C])
        token = sb2("token", [P, 2], U32)
        by_expert = dict(t=NTILES, e=E)
        past = gT[0:1, :, :].rearrange("a w t -> a (w t)")[:, 0:NTILES * E].rearrange("a (t e) -> a t e", **by_expert)
        picked = xr[0:1, :, :].rearrange("a r w -> a (r w)")[:, 0:NTILES * E].rearrange("a (t e) -> a t e", **by_expert)
        XT_ps, A_ps, G_ps, GT_ps, Y_ps = (bank(n) for n in ("XT", "A", "G", "GT", "Y"))
        names2 = """down_in table_pool table tails up_hi lo_dve lo_pool tile0 tile1 tile2 tile3 xs_ok xsT_pe xsT_hi xsT_lo
            g_pe a_pe gate_ok gated_ok gT_pe gT_ok y_pe y2_ok ln3 rstd3 res_ok token_ok sent0 sent1 pool_waits sp_waits dve_waits"""
        z = {n: sem("z_" + n) for n in names2.split()}
        tile_in = [z[f"tile{r}"] for r in range(RING)]
        sent = [z["sent0"], z["sent1"]]
        out_rows = out.rearrange("n t d -> (n t) d")
        POOL_CUTS = 3

        def const_wait(eng):
            if eng.engine in (mybir.EngineType.Pool, mybir.EngineType.SP):
                eng.sem_inc(z["pool_waits" if eng.engine == mybir.EngineType.Pool else "sp_waits"], 1)

        def wait_value(eng, name, v):
            sm = z[name] if isinstance(name, str) else name
            if isinstance(v, int):
                if v > 0:
                    eng.wait_ge(sm, v)
            else:
                eng.wait_ge(sm, v)
                const_wait(eng)

        def wait(eng, name, item, per=1, j=None):
            wait_value(eng, name, item.times(per, per if j is None else j))

        def wait_ring(eng, sm, item, ring, per):
            wait_value(eng, sm, item.uses(ring) * per)

        def steps(eng, body):
            lead = 4
            loops = (NTILES - 2 - lead) // UNROLL
            for n in range(-2, lead):
                body(Item(0, n))
            with eng.Fori(0, loops) as i:
                for k in range(UNROLL):
                    body(Item(i, lead + k))
            for n in range(lead + UNROLL * loops, NTILES + 2):
                body(Item(0, n))

        def active(item):
            return item.within(0, NTILES)

        with nc.Block() as block:
            @block.sync
            def _(sp):
                for e in range(E):
                    dst = dn_sb[:, e * DNW:(e + 1) * DNW].rearrange("p (o n) -> p o n", o=HCH)
                    sp.dma_start(dst, down_w[e].rearrange("(o p) n -> p o n", p=P)).then_inc(z["down_in"], 16)
                sp.wait_ge(z["table"], 2)
                for e in range(E):
                    r = sp.value_load(tail_row[0:1, e:e + 1], min_val=0, max_val=PAD - P)
                    sp.dma_start(buckets[bass.ds(r, P), :], pad_row[:, :]).then_inc(z["tails"], 16)
                sp.wait_ge(z["tails"], 16 * E)
                sp.wait_ge(z["table"], TABLE)

                def step(t):
                    n = t + 2
                    if active(n):
                        if n.runtime or n.k >= RING:
                            wait(sp, "token_ok", n - RING)
                        r = sp.value_load(tile_row[0:1, bass.ds(n.times(1), 1)], min_val=0, max_val=PAD)
                        sp.dma_start(xr[:, n.mod(RING), :], buckets[bass.ds(r, P), :]).then_inc(tile_in[n.mod(RING)], 16)

                steps(sp, step)
                for p in range(2):
                    sp.wait_ge(sent[p], 16 * ((NTILES + 1 - p) // 2))

            @block.gpsimd
            def _(pool):
                g = nc.gpsimd
                kw = dict(allow_small_or_imprecise_dtypes=True, channel_multiplier=0, base=0)
                g.iota(base[:, :], pattern=[[CAP, E]], **kw).then_inc(z["table_pool"], 1)
                g.iota(tno[:, :], pattern=[[1, NTILES]], **kw).then_inc(z["table_pool"], 1)
                for e in range(POOL_CUTS):
                    pool.wait_ge(z["up_hi"], e + 1)
                    at = slice(e * UPW, (e + 1) * UPW)
                    g.tensor_tensor(up_sb[:, at], up_sb[:, at].bitcast(F32), up_hi[:, at].bitcast(F32), ALU.subtract).then_inc(z["lo_pool"], 1)

                def step(t):
                    m, f = t - 1, t - 2
                    if active(f):
                        wait(pool, "res_ok", f)
                        wait(pool, "token_ok", f)
                        g.indirect_dma_start(out=out_rows, out_offset=bass.IndirectOffsetOnAxis(ap=token[:, f.mod(2):f.mod(2) + 1], axis=0),
                                             in_=res[:, f.mod(2), :], in_offset=None, bounds_check=SEQ * TOK - 1,
                                             oob_is_err=False).then_inc(sent[f.mod(2)], 16)
                    if active(m):
                        wait(pool, "ln3", m, 2)
                        g.tensor_scalar(rs3[:, 0:1], mv3[:, 1:2], LN_EPS, None, ALU.add).then_inc(z["rstd3"], 1)
                        wait(pool, "rstd3", m, 2, 1)
                        g.tensor_tensor(rs3[:, 1:2], rs3[:, 0:1], neg_half[:, :], ALU.pow).then_inc(z["rstd3"], 1)

                steps(pool, step)

            @block.scalar
            def _(act):
                a_ = nc.scalar
                for e in range(E):
                    at = slice(e * UPW, (e + 1) * UPW)
                    a_.activation(up_hi[:, at], up_sb[:, at].bitcast(F32), ACT.Copy).then_inc(z["up_hi"], 1)

                def step(t):
                    m, n = t - 1, t + 1
                    if active(m):
                        wait(act, "gT_pe", m)
                        wait(act, "y_pe", m - 2)
                        a_.activation(gT[:, m.mod(2)], GT_ps[:, :], ACT.Copy).then_inc(z["gT_ok"], 1)
                    if active(t):
                        wait(act, "g_pe", t)
                        wait(act, "gated_ok", m)
                        a_.activation(gate[:, :], G_ps[:, :], ACT.Silu).then_inc(z["gate_ok"], 1)
                    if active(n):
                        wait(act, "xsT_pe", n)
                        wait(act, "a_pe", n - 2)
                        a_.activation(xsT[:, n.mod(2), 0], XT_ps[:, 0:NCH * P], ACT.Copy).then_inc(z["xsT_hi"], 1)

                steps(act, step)

            @block.tensor
            def _(pe):
                t_ = nc.tensor
                pe.wait_ge(z["table"], TABLE)
                pe.wait_ge(z["up_hi"], E)
                pe.wait_ge(z["down_in"], 16 * E)
                pe.wait_ge(z["lo_dve"], E - POOL_CUTS)
                pe.wait_ge(z["lo_pool"], POOL_CUTS)

                def up(ps, xT, off):
                    terms = [(w, src, c) for c in range(NCH) for w, src in ((0, up_hi), (0, up_sb), (1, up_hi))]
                    for k, (w, src, c) in enumerate(terms):
                        last = t_.matmul(ps[:, :], xT[:, w, c * P:(c + 1) * P], src[:, bass.ds(off + c * 2 * HID, HID)],
                                         start=(k == 0), stop=(k == len(terms) - 1))
                    return last

                def step(t):
                    m, n = t - 1, t + 1
                    if active(m):
                        wait(pe, "gated_ok", m)
                        wait(pe, "gT_ok", m - 1)
                        for c in range(HCH):
                            last = t_.transpose(GT_ps[:, c * P:(c + 1) * P], gated[:, c * P:(c + 1) * P], ident[:, :])
                        last.then_inc(z["gT_pe"], 1)
                    if active(t):
                        off = pe.value_load(tile_up[0:1, bass.ds(t.times(1), 1)], min_val=0, max_val=(E - 1) * UPW)
                        wait(pe, "xsT_lo", t)
                        wait(pe, "gate_ok", m)
                        up(G_ps, xsT[:, t.mod(2)], off + HID).then_inc(z["g_pe"], 1)
                    if active(n):
                        wait(pe, "xs_ok", n)
                        wait(pe, "xsT_lo", t)
                        for c in range(NCH):
                            last = t_.transpose(XT_ps[:, c * P:(c + 1) * P], xs[:, c * P:(c + 1) * P], ident[:, :])
                        last.then_inc(z["xsT_pe"], 1)
                    if active(t):
                        wait(pe, "gated_ok", m)
                        up(A_ps, xsT[:, t.mod(2)], off).then_inc(z["a_pe"], 1)
                    if active(m):
                        off = pe.value_load(tile_dn[0:1, bass.ds(m.times(1), 1)], min_val=0, max_val=(E - 1) * DNW)
                        wait(pe, "gT_ok", m)
                        wait(pe, "y2_ok", m - 1)
                        for c in range(HCH):
                            last = t_.matmul(Y_ps[:, 0:C], gT[:, m.mod(2), c * P:(c + 1) * P], dn_sb[:, bass.ds(off + c * C, C)],
                                             start=(c == 0), stop=(c == HCH - 1))
                        last.then_inc(z["y_pe"], 1)

                steps(pe, step)

            @block.vector
            def _(dve):
                v = nc.vector
                done = [0]

                def setup(ins):
                    done[0] += 1
                    ins.then_inc(z["table"], 1)
                    dve.wait_ge(z["table"], done[0])

                dve.wait_ge(z["table_pool"], 2)
                setup(v.tensor_tensor(count[:, :], filled[0:1, :], base[:, :], ALU.subtract))
                setup(v.tensor_copy(tail_row[:, :], filled[0:1, :]))
                setup(v.tensor_scalar(tiles[:, :], count[:, :], 1.0 / P, (P - 1) / P - 0.5 + 0.5 / P, ALU.mult, ALU.add))
                setup(v.tensor_scalar(tiles[:, :], tiles[:, :], ROUND, -ROUND, ALU.add, ALU.add))
                setup(v.tensor_copy(ends[:, 0:1], tiles[:, 0:1]))
                for e in range(1, E):
                    setup(v.tensor_tensor(ends[:, e:e + 1], ends[:, e - 1:e], tiles[:, e:e + 1], ALU.add))
                setup(v.tensor_scalar(skip[:, :], tiles[:, :], -float(P), float(CAP), ALU.mult, ALU.add))
                every = [1, NTILES, E]
                setup(v.tensor_tensor(past, tno[:, :].unsqueeze(2).to_broadcast(every), ends[:, :].unsqueeze(1).to_broadcast(every), ALU.is_ge))
                setup(v.tensor_reduce(eno_f[:, :], past, AX.X, ALU.add))
                setup(v.tensor_tensor(picked, past, skip[:, :].unsqueeze(1).to_broadcast(every), ALU.mult))
                setup(v.tensor_reduce(row_f[:, 0], picked, AX.X, ALU.add))
                setup(v.scalar_tensor_tensor(row_f[:, 1], tno[:, :], float(P), row_f[:, 0], ALU.mult, ALU.add))
                setup(v.tensor_tensor(owned[:, :], tno[:, :], ends[:, E - 1:E].to_broadcast([1, NTILES]), ALU.is_lt))
                setup(v.scalar_tensor_tensor(row_f[:, 0], row_f[:, 1], -float(PAD), owned[:, :], ALU.add, ALU.mult))
                setup(v.tensor_scalar(tile_row[:, :], row_f[:, 0], float(PAD), None, ALU.add))
                setup(v.tensor_scalar(tile_up[:, :], eno_f[:, :], float(E - 1), float(UPW), ALU.min, ALU.mult))
                setup(v.tensor_scalar(tile_dn[:, :], eno_f[:, :], float(E - 1), float(DNW), ALU.min, ALU.mult))
                assert done[0] == TABLE
                for e in range(POOL_CUTS, E):
                    dve.wait_ge(z["up_hi"], e + 1)
                    at = slice(e * UPW, (e + 1) * UPW)
                    v.tensor_tensor(up_sb[:, at], up_sb[:, at].bitcast(F32), up_hi[:, at].bitcast(F32), ALU.subtract).then_inc(z["lo_dve"], 1)

                def step(t):
                    m, n, f = t - 1, t + 1, t - 2
                    if active(f):
                        wait(dve, "rstd3", f, 2)
                        wait_ring(dve, sent[f.mod(2)], f - 2, 2, 16)
                        v.tensor_scalar(res[:, f.mod(2)], y[:, :], mv3[:, 0:1], rs3[:, 1:2],
                                        ALU.subtract, ALU.mult).then_inc(z["res_ok"], 1)
                    if active(n):
                        wait(dve, "xsT_hi", n)
                        v.tensor_tensor(xsT[:, n.mod(2), 1], XT_ps[:, 0:NCH * P], xsT[:, n.mod(2), 0].bitcast(F32), ALU.subtract).then_inc(z["xsT_lo"], 1)
                    if active(t):
                        wait(dve, "gate_ok", t)
                        wait(dve, "a_pe", t)
                        wait(dve, "gT_pe", m)
                        v.tensor_tensor(gated[:, :], A_ps[:, :], gate[:, :], ALU.mult).then_inc(z["gated_ok"], 1)
                    nn = t + 2
                    if active(nn):
                        wait_ring(dve, tile_in[nn.mod(RING)], nn, RING, 16)
                        wait(dve, "xsT_pe", n)
                        v.scalar_tensor_tensor(xs[:, :], xr[:, nn.mod(RING), 0:C], xr[:, nn.mod(RING), C:C + 1], scale_bc[:, :],
                                               ALU.mult, ALU.mult).then_inc(z["xs_ok"], 1)
                    if active(m):
                        wait(dve, "y_pe", m)
                        wait(dve, "res_ok", f)
                        v.scalar_tensor_tensor(y[:, :], xr[:, m.mod(RING), 0:C], 2.0, Y_ps[:, 0:C],
                                               ALU.mult, ALU.add).then_inc(z["y2_ok"], 1)
                        wait(dve, "y2_ok", m)
                        v.bn_stats(st3[:, :], y[:, :]).then_inc(z["ln3"], 1)
                        wait_ring(dve, sent[m.mod(2)], m - 2, 2, 16)
                        v.tensor_copy(token[:, m.mod(2):m.mod(2) + 1], xr[:, m.mod(RING), C + 1:C + 2].bitcast(U32)).then_inc(z["token_ok"], 1)
                        wait(dve, "ln3", m, 2, 1)
                        dve.sem_inc(z["dve_waits"], 1)
                        v.bn_aggr(mv3[:, :], st3[:, :]).then_inc(z["ln3"], 1)

                steps(dve, step)


TABLE = 23


_INS = ["x", "ctx_1024", "L0_attn_lmlg", "L0_attn_theta", "L0_attn_last_conv_init", "L0_xattn_Wq", "L0_xattn_bq",
        "L0_xattn_Wk", "L0_xattn_bk", "L0_xattn_Wv", "L0_xattn_bv", "L0_xattn_ln_g", "L0_xattn_ln_b",
        "L0_ffn_scale", "L0_ffn_centroids", "L0_ffn_up_w", "L0_ffn_down_w"]
_BY_CHANNEL = {"L0_xattn_Wq", "L0_xattn_bq", "L0_xattn_Wk", "L0_xattn_bk"}


def kernel(**inputs):
    import concourse.bacc as _bacc
    from concourse.bass_utils import run_bass_kernel_spmd as _run

    nc = _bacc.Bacc("TRN2", target_bir_lowering=False, num_devices=1)
    arrays, args = {}, []
    for name in _INS:
        a = np.asarray(inputs[name])
        if name in _BY_CHANNEL:
            lead = a.shape[:-1]
            a = a.reshape(*lead, NCH, HPC, DH).swapaxes(-1, -2).reshape(*lead, C)
        a = np.ascontiguousarray(a)
        arrays[f"in_{name}"] = a
        args.append(nc.dram_tensor(f"in_{name}", a.shape, mybir.dt.from_np(a.dtype), kind="ExternalInput").ap())
    args.append(nc.dram_tensor("out_0", (SEQ, TOK, C), F32, kind="ExternalOutput").ap())
    build(nc, *args)
    r = _run(nc, [arrays], core_ids=[0])
    return r.results[0]["out_0"]
```
